# Optimizing a Trainium2 kernel written in Bass

```python
import numpy as np
import jax
import jax.numpy as jnp

def _softmax(x, axis=-1):
    return jax.nn.softmax(x, axis=axis)

def _gelu(x):
    return jax.nn.gelu(x, approximate=True)

def _silu(x):
    return jax.nn.silu(x)

def _sigmoid(x):
    return jax.nn.sigmoid(x)

def _layernorm(x, axis=-1, eps=1e-05):
    m = jnp.mean(x, axis=axis, keepdims=True)
    v = jnp.var(x, axis=axis, keepdims=True)
    return (x - m) / jnp.sqrt(v + eps)

def _scatter_add(tgt, idx, src, axis=0):
    return tgt.at[idx].add(src)

def _segment_sum(src, seg, n):
    return jax.ops.segment_sum(src, seg, n)
kernel_name = 'mk_xattn_ffn_d4_seqx_r8_69ee8a'

def setup_inputs(seed: int=0):
    np.random.seed(seed)
    _w = jnp.asarray

    def _rec_inputs():
        import jax
        import jax.numpy as jnp
        _rk = jax.random.key(seed)
        x = 7.22e-05 + 1 * jax.random.normal(jax.random.fold_in(_rk, 1), (8, 128, 512), jnp.float32)
        _lenS = 128 - jax.random.randint(jax.random.fold_in(_rk, 7), (8,), 0, max(1, 128 // 4) + 1, jnp.int32)
        _lenS2 = 128 - jax.random.randint(jax.random.fold_in(_rk, 8), (8,), 0, max(1, 128 // 4) + 1, jnp.int32)
        _ctx_4096P = jax.random.normal(jax.random.fold_in(_rk, 11), (8, 16, 512), jnp.float32)
        _ctx_4096c = jax.random.dirichlet(jax.random.fold_in(_rk, 511), 0.3 * jnp.ones((16,), jnp.float32), (8, 128))
        _ctx_4096t = jnp.einsum('bsk,bkd->bsd', _ctx_4096c, _ctx_4096P)
        _ctx_4096t = _ctx_4096t * jax.lax.rsqrt(jnp.mean(jnp.square(_ctx_4096t)) + 1e-12) * 0.953939
        ctx_4096 = 4.13588e-05 + 0.999923 * (_ctx_4096t + 0.3 * jax.random.normal(jax.random.fold_in(_rk, 611), (8, 128, 512), jnp.float32))
        _validS = jnp.arange(128)[None, :] < _lenS[:, None]
        _validS2 = jnp.arange(128)[None, :] < _lenS2[:, None]
        _causal = jnp.tril(jnp.ones((128, 128), dtype=bool))
        mask_BxSxS2_bk0 = jnp.logical_not(jnp.broadcast_to(_validS2[:, None, :], (8, 128, 128)))
        mask_BxSxS2_ff1 = jnp.where(jnp.ones((8, 128, 128), dtype=bool), 1.0, 0.0).astype(jnp.float32)
        return (x, ctx_4096, mask_BxSxS2_bk0, mask_BxSxS2_ff1)
    x, ctx_4096, mask_BxSxS2_bk0, mask_BxSxS2_ff1 = _rec_inputs()

    def _L0_xattn_setup():
        import jax, jax.numpy as jnp
        import numpy as np
        B, LQ, LK, D, H, DH = (2, 128, 128, 512, 32, 128)
        EPS = 1e-05

        def _rmsnorm(x, weight):
            var = jnp.mean(jnp.square(x), axis=-1, keepdims=True)
            return x * jax.lax.rsqrt(var + EPS) * weight
        key = jax.random.key(seed)
        ks = jax.random.split(key, 8)
        scale = 0.02
        return {'hidden_states': jax.random.normal(ks[0], (B, LQ, D), jnp.float32), 'key_value_states': jax.random.normal(ks[1], (B, LK, D), jnp.float32), 'attention_mask': jax.random.randint(ks[2], (B, LQ, LK), 0, 2) > 0, 'position_bias': jax.random.normal(ks[3], (H, LQ, LK), jnp.float32), 'ln_weight': jnp.ones((D,), jnp.float32), 'w_q': jax.random.normal(ks[4], (H * DH, D), jnp.float32) * scale, 'w_k': jax.random.normal(ks[5], (H * DH, D), jnp.float32) * scale, 'w_v': jax.random.normal(ks[6], (H * DH, D), jnp.float32) * scale, 'w_out': jax.random.normal(ks[7], (D, H * DH), jnp.float32) * scale}
    _L0_xattn_all = _L0_xattn_setup()
    _L0_xattn_in = {k: v for k, v in _L0_xattn_all.items() if k in ('position_bias', 'ln_weight', 'w_q', 'w_k', 'w_v', 'w_out')}
    del _L0_xattn_all

    def _L0_ffn_setup():
        import jax, jax.numpy as jnp
        import numpy as np
        H = 512
        I = 1792
        G = 128

        def dequant(q, s, g=G):
            O, In = q.shape
            return (q.reshape(O, In // g, g).astype(s.dtype) * s[:, :, None]).reshape(O, In)
        key = jax.random.key(seed)
        ks = jax.random.split(key, 7)
        x = jax.random.normal(ks[0], (2, 256, H), dtype=jnp.float32)

        def mk_qlinear(kq, ksc, out_d, in_d):
            q = jax.random.randint(kq, (out_d, in_d), -8, 8, dtype=jnp.int32)
            s = jax.random.uniform(ksc, (out_d, in_d // G), dtype=jnp.float32, minval=0.005, maxval=0.02)
            return (q, s)
        gate_q, gate_s = mk_qlinear(ks[1], ks[2], I, H)
        up_q, up_s = mk_qlinear(ks[3], ks[4], I, H)
        down_q, down_s = mk_qlinear(ks[5], ks[6], H, I)
        return {'x': x, 'gate_q': gate_q, 'gate_s': gate_s, 'up_q': up_q, 'up_s': up_s, 'down_q': down_q, 'down_s': down_s}
    _L0_ffn_all = _L0_ffn_setup()
    _L0_ffn_in = {k: v for k, v in _L0_ffn_all.items() if k in ('gate_q', 'gate_s', 'up_q', 'up_s', 'down_q', 'down_s')}
    del _L0_ffn_all

    def _L1_xattn_setup():
        import jax, jax.numpy as jnp
        import numpy as np
        B, Q, D = (8, 64, 512)
        CTX = 512
        H, KV, HD = (16, 4, 96)
        G = H // KV
        key = jax.random.key(seed)
        ks = jax.random.split(key, 6)
        s = 0.02
        return {'latents': jax.random.normal(ks[0], (B, Q, D), jnp.float32), 'context': jax.random.normal(ks[1], (B, CTX, D), jnp.float32), 'Wq': jax.random.normal(ks[2], (H * HD, D), jnp.float32) * s, 'Wk': jax.random.normal(ks[3], (KV * HD, D), jnp.float32) * s, 'Wv': jax.random.normal(ks[4], (KV * HD, D), jnp.float32) * s, 'Wo': jax.random.normal(ks[5], (D, H * HD), jnp.float32) * s}
    _L1_xattn_all = _L1_xattn_setup()
    _L1_xattn_in = {k: v for k, v in _L1_xattn_all.items() if k in ('Wq', 'Wk', 'Wv', 'Wo')}
    del _L1_xattn_all

    def _L1_ffn_setup():
        import jax, jax.numpy as jnp
        import numpy as np
        key = jax.random.key(seed)
        k = jax.random.split(key, 6)
        x = jax.random.normal(k[0], (4, 256, 512), jnp.float32)
        W = jax.random.normal(k[1], (512, 512), jnp.float32) * 0.02
        bias = jax.random.normal(k[2], (512,), jnp.float32) * 0.02
        A = jax.random.normal(k[3], (16, 16, 512), jnp.float32) * 0.02
        Bf = jax.random.normal(k[4], (16, 512, 16), jnp.float32) * 0.02
        coeffs = jax.random.uniform(k[5], (16,), jnp.float32)
        scales = jnp.full((16,), 0.5, jnp.float32)
        return {'x': x, 'W': W, 'bias': bias, 'A': A, 'Bf': Bf, 'coeffs': coeffs, 'scales': scales}
    _L1_ffn_all = _L1_ffn_setup()
    _L1_ffn_in = {k: v for k, v in _L1_ffn_all.items() if k in ('W', 'bias', 'A', 'Bf', 'coeffs', 'scales')}
    del _L1_ffn_all

    def _L2_xattn_setup():
        import jax, jax.numpy as jnp
        import numpy as np
        EMB_DIM = 64
        HEADS = 8
        key = jax.random.key(seed)
        kq, kk, kv = jax.random.split(key, 3)
        B, C, N = (8, EMB_DIM, 512)
        q = jax.random.normal(kq, (B, C, N), dtype=jnp.float32)
        k = jax.random.normal(kk, (B, C, N), dtype=jnp.float32)
        v = jax.random.normal(kv, (B, C, N), dtype=jnp.float32)
        return {'q': q, 'k': k, 'v': v}
    _L2_xattn_all = _L2_xattn_setup()
    _L2_xattn_in = {k: v for k, v in _L2_xattn_all.items() if k in ()}
    del _L2_xattn_all

    def _L2_ffn_setup():
        import jax, jax.numpy as jnp
        import numpy as np
        OUT, IN, RANK = (512, 512, 128)
        B, T = (4, 512)
        key = jax.random.key(seed)
        kx, ku, ks, kv = jax.random.split(key, 4)
        x = jax.random.normal(kx, (B, T, IN), dtype=jnp.float32)
        U = jax.random.normal(ku, (OUT, RANK), dtype=jnp.float32) / np.sqrt(OUT)
        S = jax.random.uniform(ks, (RANK,), dtype=jnp.float32, minval=0.1, maxval=10.0)
        S = jnp.sort(S)[::-1]
        V = jax.random.normal(kv, (IN, RANK), dtype=jnp.float32) / np.sqrt(IN)
        return {'x': x, 'U': U, 'S': S, 'V': V}
    _L2_ffn_all = _L2_ffn_setup()
    _L2_ffn_in = {k: v for k, v in _L2_ffn_all.items() if k in ('U', 'S', 'V')}
    del _L2_ffn_all

    def _L3_xattn_setup():
        import jax, jax.numpy as jnp
        import numpy as np
        N_Q_HEADS = 32
        N_KV_HEADS = 8
        D_MODEL = 512
        D_K = 128
        D_V = 128
        ROPE_BASE = 10000.0

        def _rope(x):
            d = x.shape[-1]
            s = x.shape[2]
            inv_freq = 1.0 / ROPE_BASE ** (jnp.arange(0, d, 2, dtype=jnp.float32) / d)
            ang = jnp.arange(s, dtype=jnp.float32)[:, None] * inv_freq[None, :]
            cos = jnp.concatenate([jnp.cos(ang), jnp.cos(ang)], axis=-1)[None, None]
            sin = jnp.concatenate([jnp.sin(ang), jnp.sin(ang)], axis=-1)[None, None]
            x1, x2 = (x[..., :d // 2], x[..., d // 2:])
            rot = jnp.concatenate([-x2, x1], axis=-1)
            return x * cos + rot * sin
        key = jax.random.key(seed)
        ks = jax.random.split(key, 8)
        bs, s = (2, 128)
        inp = {'query': jax.random.normal(ks[0], (bs, s, D_MODEL), dtype=jnp.float32), 'key': jax.random.normal(ks[1], (bs, s, D_MODEL), dtype=jnp.float32), 'value': jax.random.normal(ks[2], (bs, s, D_MODEL), dtype=jnp.float32), 'mask': jnp.ones((bs, s, s), dtype=jnp.float32), 'wq': jax.random.normal(ks[3], (D_MODEL, N_Q_HEADS * D_K), dtype=jnp.float32) * 0.02, 'wk': jax.random.normal(ks[4], (D_MODEL, N_KV_HEADS * D_K), dtype=jnp.float32) * 0.02, 'wv': jax.random.normal(ks[5], (D_MODEL, N_KV_HEADS * D_V), dtype=jnp.float32) * 0.02, 'wo': jax.random.normal(ks[6], (N_Q_HEADS * D_V, D_MODEL), dtype=jnp.float32) * 0.02}
        return inp
    _L3_xattn_all = _L3_xattn_setup()
    _L3_xattn_in = {k: v for k, v in _L3_xattn_all.items() if k in ('wq', 'wk', 'wv', 'wo')}
    del _L3_xattn_all

    def _L3_ffn_setup():
        import jax, jax.numpy as jnp
        import numpy as np
        TOP_K = 2
        key = jax.random.key(seed)
        k1, k2, k3 = jax.random.split(key, 3)
        B, S, H, O, E = (1024, 1, 512, 512, 8)
        x = jax.random.normal(k1, (B, S, H), dtype=jnp.float32)
        gate_w = jax.random.normal(k2, (H, E), dtype=jnp.float32) * 0.02
        expert_w = jax.random.normal(k3, (E, H, O), dtype=jnp.float32) * 0.02
        return {'x': x, 'gate_w': gate_w, 'expert_w': expert_w}
    _L3_ffn_all = _L3_ffn_setup()
    _L3_ffn_in = {k: v for k, v in _L3_ffn_all.items() if k in ('gate_w', 'expert_w')}
    del _L3_ffn_all
    return {'x': x, 'ctx_4096': ctx_4096, 'mask_BxSxS2_bk0': mask_BxSxS2_bk0, 'mask_BxSxS2_ff1': mask_BxSxS2_ff1, 'L0_xattn_position_bias': _L0_xattn_in['position_bias'], 'L0_xattn_ln_weight': _L0_xattn_in['ln_weight'], 'L0_xattn_w_q': _L0_xattn_in['w_q'], 'L0_xattn_w_k': _L0_xattn_in['w_k'], 'L0_xattn_w_v': _L0_xattn_in['w_v'], 'L0_xattn_w_out': _L0_xattn_in['w_out'], 'L0_ffn_gate_q': _L0_ffn_in['gate_q'], 'L0_ffn_gate_s': _L0_ffn_in['gate_s'], 'L0_ffn_up_q': _L0_ffn_in['up_q'], 'L0_ffn_up_s': _L0_ffn_in['up_s'], 'L0_ffn_down_q': _L0_ffn_in['down_q'], 'L0_ffn_down_s': _L0_ffn_in['down_s'], 'L1_xattn_Wq': _L1_xattn_in['Wq'], 'L1_xattn_Wk': _L1_xattn_in['Wk'], 'L1_xattn_Wv': _L1_xattn_in['Wv'], 'L1_xattn_Wo': _L1_xattn_in['Wo'], 'L1_ffn_W': _L1_ffn_in['W'], 'L1_ffn_bias': _L1_ffn_in['bias'], 'L1_ffn_A': _L1_ffn_in['A'], 'L1_ffn_Bf': _L1_ffn_in['Bf'], 'L1_ffn_coeffs': _L1_ffn_in['coeffs'], 'L1_ffn_scales': _L1_ffn_in['scales'], 'L2_ffn_U': _L2_ffn_in['U'], 'L2_ffn_S': _L2_ffn_in['S'], 'L2_ffn_V': _L2_ffn_in['V'], 'L3_xattn_wq': _L3_xattn_in['wq'], 'L3_xattn_wk': _L3_xattn_in['wk'], 'L3_xattn_wv': _L3_xattn_in['wv'], 'L3_xattn_wo': _L3_xattn_in['wo'], 'L3_ffn_gate_w': _L3_ffn_in['gate_w'], 'L3_ffn_expert_w': _L3_ffn_in['expert_w']}

def reference(x, ctx_4096, mask_BxSxS2_bk0, mask_BxSxS2_ff1, L0_xattn_position_bias, L0_xattn_ln_weight, L0_xattn_w_q, L0_xattn_w_k, L0_xattn_w_v, L0_xattn_w_out, L0_ffn_gate_q, L0_ffn_gate_s, L0_ffn_up_q, L0_ffn_up_s, L0_ffn_down_q, L0_ffn_down_s, L1_xattn_Wq, L1_xattn_Wk, L1_xattn_Wv, L1_xattn_Wo, L1_ffn_W, L1_ffn_bias, L1_ffn_A, L1_ffn_Bf, L1_ffn_coeffs, L1_ffn_scales, L2_ffn_U, L2_ffn_S, L2_ffn_V, L3_xattn_wq, L3_xattn_wk, L3_xattn_wv, L3_xattn_wo, L3_ffn_gate_w, L3_ffn_expert_w):
    import jax
    import jax.numpy as jnp

    def _L0_xattn_ref(hidden_states, key_value_states, attention_mask, position_bias, ln_weight, w_q, w_k, w_v, w_out):
        import jax, jax.numpy as jnp
        import numpy as np
        B, LQ, LK, D, H, DH = (2, 128, 128, 512, 32, 128)
        EPS = 1e-05

        def _rmsnorm(x, weight):
            var = jnp.mean(jnp.square(x), axis=-1, keepdims=True)
            return x * jax.lax.rsqrt(var + EPS) * weight
        x = _rmsnorm(hidden_states, ln_weight)
        b, lq, _ = x.shape
        lk = key_value_states.shape[1]
        h_q = (x @ w_q.T).reshape(b, lq, H, DH)
        h_k = (key_value_states @ w_k.T).reshape(b, lk, H, DH)
        h_v = (key_value_states @ w_v.T).reshape(b, lk, H, DH)
        score = jnp.einsum('bqhd,bkhd->bhqk', h_q, h_k)
        score = score + position_bias[None]
        m = attention_mask[:, None]
        score = jnp.where(m, score, -jnp.inf)
        score = jax.nn.softmax(score, axis=-1)
        score = jnp.where(m, score, 0.0)
        attn = jnp.einsum('bhqk,bkhd->bqhd', score, h_v).reshape(b, lq, H * DH)
        out = attn @ w_out.T
        return hidden_states + out

    def _L0_ffn_ref(x, gate_q, gate_s, up_q, up_s, down_q, down_s):
        import jax, jax.numpy as jnp
        import numpy as np
        H = 512
        I = 1792
        G = 128

        def dequant(q, s, g=G):
            O, In = q.shape
            return (q.reshape(O, In // g, g).astype(s.dtype) * s[:, :, None]).reshape(O, In)
        Wg = dequant(gate_q, gate_s)
        Wu = dequant(up_q, up_s)
        Wd = dequant(down_q, down_s)
        gate_score = jax.nn.silu(jnp.einsum('bsh,ih->bsi', x, Wg))
        intermediate = gate_score * jnp.einsum('bsh,ih->bsi', x, Wu)
        return jnp.einsum('bsi,hi->bsh', intermediate, Wd)

    def _L1_xattn_ref(latents, context, Wq, Wk, Wv, Wo):
        import jax, jax.numpy as jnp
        import numpy as np
        B, Q, D = (8, 64, 512)
        CTX = 512
        H, KV, HD = (16, 4, 96)
        G = H // KV
        b, q_len, _ = latents.shape
        hidden = jnp.concatenate([context, latents], axis=1)
        s_len = hidden.shape[1]
        q = (latents @ Wq.T).reshape(b, q_len, H, HD)
        k = (hidden @ Wk.T).reshape(b, s_len, KV, HD)
        v = (hidden @ Wv.T).reshape(b, s_len, KV, HD)
        q = q.transpose(0, 2, 1, 3).reshape(b, KV, G, q_len, HD)
        k = k.transpose(0, 2, 1, 3)
        v = v.transpose(0, 2, 1, 3)
        scale = 1.0 / jnp.sqrt(jnp.asarray(HD, q.dtype))
        scores = jnp.einsum('bkgqd,bksd->bkgqs', q, k) * scale
        attn = jax.nn.softmax(scores.astype(jnp.float32), axis=-1).astype(q.dtype)
        out = jnp.einsum('bkgqs,bksd->bkgqd', attn, v)
        out = out.reshape(b, H, q_len, HD).transpose(0, 2, 1, 3).reshape(b, q_len, H * HD)
        return out @ Wo.T

    def _L1_ffn_ref(x, W, bias, A, Bf, coeffs, scales):
        import jax, jax.numpy as jnp
        import numpy as np
        out = jnp.einsum('bsd,od->bso', x, W) + bias
        xa = jnp.einsum('bsd,erd->ebsr', x, A)
        w = coeffs * scales
        upd = jnp.einsum('ebsr,eor,e->bso', xa, Bf, w)
        return out + upd

    def _L2_xattn_ref(q, k, v):
        import jax, jax.numpy as jnp
        import numpy as np
        EMB_DIM = 64
        HEADS = 8
        B, C, N = q.shape
        H = HEADS
        dh = C // H
        qh = q.transpose(0, 2, 1).reshape(B, N, H, dh)
        kh = k.transpose(0, 2, 1).reshape(B, N, H, dh)
        vh = v.transpose(0, 2, 1).reshape(B, N, H, dh)
        qh = jax.nn.softmax(qh, axis=3)
        kh = jax.nn.softmax(kh, axis=1)
        kvs = jnp.einsum('bnhd,bnhe->bhde', kh, vh)
        out = jnp.einsum('bnhd,bhde->bnhe', qh, kvs)
        return out.transpose(0, 2, 3, 1).reshape(B, C, N)

    def _L2_ffn_ref(x, U, S, V):
        import jax, jax.numpy as jnp
        import numpy as np
        OUT, IN, RANK = (512, 512, 128)
        B, T = (4, 512)
        weight = U * S[None, :] @ V.T
        return jnp.einsum('bti,oi->bto', x, weight)

    def _L3_xattn_ref(query, key, value, mask, wq, wk, wv, wo):
        import jax, jax.numpy as jnp
        import numpy as np
        N_Q_HEADS = 32
        N_KV_HEADS = 8
        D_MODEL = 512
        D_K = 128
        D_V = 128
        ROPE_BASE = 10000.0

        def _rope(x):
            d = x.shape[-1]
            s = x.shape[2]
            inv_freq = 1.0 / ROPE_BASE ** (jnp.arange(0, d, 2, dtype=jnp.float32) / d)
            ang = jnp.arange(s, dtype=jnp.float32)[:, None] * inv_freq[None, :]
            cos = jnp.concatenate([jnp.cos(ang), jnp.cos(ang)], axis=-1)[None, None]
            sin = jnp.concatenate([jnp.sin(ang), jnp.sin(ang)], axis=-1)[None, None]
            x1, x2 = (x[..., :d // 2], x[..., d // 2:])
            rot = jnp.concatenate([-x2, x1], axis=-1)
            return x * cos + rot * sin
        bs, s, _ = query.shape
        g = N_Q_HEADS // N_KV_HEADS
        q = (query @ wq).reshape(bs, s, N_Q_HEADS, D_K).transpose(0, 2, 1, 3)
        k = (key @ wk).reshape(bs, s, N_KV_HEADS, D_K).transpose(0, 2, 1, 3)
        v = (value @ wv).reshape(bs, s, N_KV_HEADS, D_V).transpose(0, 2, 1, 3)
        q = _rope(q)
        k = _rope(k)
        scale = jnp.sqrt(jnp.float32(D_K))
        qg = q.reshape(bs, N_KV_HEADS, g, s, D_K)
        scores = jnp.einsum('bhgqd,bhkd->bhgqk', qg, k) / scale
        masked = jnp.where(mask[:, None, None].astype(bool), scores, -1000000000.0)
        w = jax.nn.softmax(masked, axis=-1)
        out = jnp.einsum('bhgqk,bhkd->bhgqd', w, v)
        out = out.reshape(bs, N_Q_HEADS, s, D_V).transpose(0, 2, 1, 3).reshape(bs, s, N_Q_HEADS * D_V)
        return out @ wo

    def _L3_ffn_ref(x, gate_w, expert_w):
        import jax, jax.numpy as jnp
        import numpy as np
        TOP_K = 2
        E = gate_w.shape[-1]
        logits = jnp.einsum('bsh,he->bse', x, gate_w)
        topv, topi = jax.lax.top_k(logits, TOP_K)
        w = jax.nn.softmax(topv, axis=-1)
        onehot = jax.nn.one_hot(topi, E, dtype=x.dtype)
        w_e = jnp.einsum('bske,bsk->bse', onehot, w)
        out = jnp.einsum('bsh,eho,bse->bso', x, expert_w, w_e)
        return out
    x = x + _L0_xattn_ref(_layernorm(x, axis=-1), ctx_4096, mask_BxSxS2_bk0, L0_xattn_position_bias, L0_xattn_ln_weight, L0_xattn_w_q, L0_xattn_w_k, L0_xattn_w_v, L0_xattn_w_out)
    x = x + _L0_ffn_ref(_layernorm(x, axis=-1), L0_ffn_gate_q, L0_ffn_gate_s, L0_ffn_up_q, L0_ffn_up_s, L0_ffn_down_q, L0_ffn_down_s)
    x = x + _L1_xattn_ref(_layernorm(x, axis=-1), ctx_4096, L1_xattn_Wq, L1_xattn_Wk, L1_xattn_Wv, L1_xattn_Wo)
    x = x + _L1_ffn_ref(_layernorm(x, axis=-1), L1_ffn_W, L1_ffn_bias, L1_ffn_A, L1_ffn_Bf, L1_ffn_coeffs, L1_ffn_scales)
    x = x + _L2_xattn_ref(_layernorm(x, axis=-1), ctx_4096, ctx_4096)
    x = x + _L2_ffn_ref(_layernorm(x, axis=-1), L2_ffn_U, L2_ffn_S, L2_ffn_V)
    x = x + _L3_xattn_ref(_layernorm(x, axis=-1), ctx_4096, ctx_4096, mask_BxSxS2_ff1, L3_xattn_wq, L3_xattn_wk, L3_xattn_wv, L3_xattn_wo)
    x = x + _L3_ffn_ref(_layernorm(x, axis=-1), L3_ffn_gate_w, L3_ffn_expert_w)
    return x

_drawn_inputs = setup_inputs


def setup_inputs(seed=0):
    import zlib

    import numpy as np

    out = dict(_drawn_inputs(seed))
    spreads = {'L0_xattn_ln_weight': (1.0, 0.2), 'L1_ffn_scales': (0.5, 0.6)}
    factors = {'L1_xattn_Wq': 8.0,
     'L1_xattn_Wk': 8.0,
     'L1_ffn_bias': 21.673,
     'L1_ffn_A': 3.521,
     'L1_ffn_Bf': 3.548,
     'L1_ffn_coeffs': 8.0,
     'L3_xattn_wq': 8.0,
     'L3_xattn_wk': 8.0}
    for name, (base, spread) in spreads.items():
        noise = np.random.default_rng([zlib.crc32(name.encode()), seed]).standard_normal(out[name].shape)
        drawn = base * np.exp(spread * noise) if base else spread * noise
        out[name] = jnp.asarray(drawn.astype(out[name].dtype))
    for name, factor in factors.items():
        out[name] = (out[name] * factor).astype(out[name].dtype)
    return out
```

```python
from contextlib import ExitStack

import numpy as np

import concourse.bass as bass
from concourse import mybir

F32, F32R = mybir.dt.float32, mybir.dt.float32r
I32, U32, U8 = mybir.dt.int32, mybir.dt.uint32, mybir.dt.uint8
ALU, ACT, AX = mybir.AluOpType, mybir.ActivationFunctionType, mybir.AxisListType

P = 128
B = 8
D = 512
C = D // P
TOK = B * P
HALF = TOK // 2
HB = B // 2
EPS = 1e-5
MASKED = -1e30


class Tiles:

    def __init__(self, nc, ctx, name):
        self.nc, self.ctx, self.name, self.sems = nc, ctx, name, []
        ctx.callback(self.clear)

    def clear(self):
        if self.sems:
            self.nc.clear_and_free_semaphores(self.sems)
            self.nc.all_engine_barrier()

    def sb(self, name, shape, dt=F32):
        return self.ctx.enter_context(self.nc.sbuf_tensor(f"{self.name}_{name}", shape, dt))

    def pair(self, name, shape):
        return self.sb(name + "_hi", shape, F32R), self.sb(name + "_lo", shape, F32R)

    def sem(self, name):
        self.sems.append(self.nc.alloc_semaphore(f"{self.name}_{name}"))
        return self.sems[-1]


def product(nc, out, wt, x, first, last, begun=None):
    (wh, wl), (xh, xl) = wt, x
    ins = nc.tensor.matmul(out, wh, xh, start=first, stop=False)
    if begun is not None:
        ins.then_inc(begun, 1)
    nc.tensor.matmul(out, wl, xh, start=False, stop=False)
    return nc.tensor.matmul(out, wh, xl, start=False, stop=last)


def rounded(nc, G, hi, x):
    zero = G.zero[0:x.shape[0]]
    for size in x.shape[2:]:
        zero = zero.unsqueeze(1)
    return nc.gpsimd.tensor_tensor(hi, x, zero.to_broadcast(list(x.shape)), ALU.add)


def at(pair, *index):
    return pair[0][index], pair[1][index]


ALL = slice(None)


class Norm:

    SLOTS = 4

    def __init__(self, t, G, h, rms_weight=None):
        self.nc, self.G, self.h, self.rms_weight = t.nc, G, h, rms_weight
        self.stats = t.sb("ln_stats", [P, B, 6])
        self.mean_var = t.sb("ln_mean_var", [P, B, 2])
        self.var_eps = t.sb("ln_var_eps", [P, B])
        self.root = t.sb("ln_root", [P, B])
        self.rstd = t.sb("ln_rstd", [P, B])
        self.rrms = t.sb("ln_rrms", [P, B])
        self.stats_done = t.sem("ln_stats_done")
        self.moments = t.sem("ln_moments")
        self.rooted = t.sem("ln_rooted")
        self.h_step = t.sem("ln_h_step")
        self.h_ready = t.sem("ln_h_ready")
        self.turned = t.sem("ln_turned")
        self.hi_done = t.sem("ln_hi_done")
        self.lo_done = t.sem("ln_lo_done")

    def normed(self, v, i, tile):
        nc, h, x = self.nc, self.h, self.G.x
        if self.rms_weight is None:
            nc.vector.tensor_scalar(h[:, i, :], x[:, tile, :], self.mean_var[:, tile, 0:1],
                                    self.rstd[:, bass.ds(tile, 1)], ALU.subtract, ALU.mult
                                    ).then_inc(self.h_ready, 1)
            return
        nc.vector.tensor_scalar(h[:, i, :], x[:, tile, :], self.mean_var[:, tile, 0:1],
                                self.rstd[:, bass.ds(tile, 1)], ALU.subtract, ALU.mult
                                ).then_inc(self.h_step, 1)
        v.wait_ge(self.h_step, tile * 2 + 1)
        nc.vector.tensor_tensor(x[:, tile, :], x[:, tile, :], h[:, i, :], ALU.add
                                ).then_inc(self.h_step, 1)
        v.wait_ge(self.h_step, tile * 2 + 2)
        nc.vector.scalar_tensor_tensor(out=h[:, i, :], in0=h[:, i, :],
                                       scalar=self.rrms[:, bass.ds(tile, 1)],
                                       in1=self.rms_weight[:], op0=ALU.mult, op1=ALU.mult
                                       ).then_inc(self.h_ready, 1)

    def low(self, v, tile):
        G, cols = self.G, bass.ds(tile * P, P)
        v.wait_ge(self.hi_done, tile + 1)
        self.nc.vector.tensor_tensor(
            G.xn[1][:, :, cols], G.ps[:, tile, :].rearrange("p (c t) -> p c t", c=C),
            G.xn[0][:, :, cols].bitcast(F32), ALU.subtract).then_inc(self.lo_done, 1)

    def vector(self, v):
        self.vector_stats(v)
        with v.Fori(0, self.SLOTS) as i:
            self.normed(v, i, i)
        with v.Fori(0, B - self.SLOTS) as i:
            v.wait_ge(self.turned, i + 1)
            self.normed(v, i, i + self.SLOTS)
            self.low(v, i)
        with v.Fori(B - self.SLOTS, B) as i:
            self.low(v, i)

    def vector_stats(self, v):
        nc, G = self.nc, self.G
        with v.Fori(0, B) as i:
            nc.vector.bn_stats(self.stats[:, i, :], G.x[:, i, :]).then_inc(self.stats_done, 1)
        v.wait_ge(self.stats_done, B)
        for i in range(B):
            nc.vector.bn_aggr(self.mean_var[:, i, :], self.stats[:, i, :]).then_inc(self.stats_done, 1)
        v.wait_ge(self.stats_done, 2 * B)
        var = self.mean_var[:, :, 1]
        nc.vector.tensor_scalar(self.var_eps[:], var, EPS, None, ALU.add).then_inc(self.moments, 1)
        v.wait_ge(self.rooted, 1)
        nc.vector.reciprocal(self.rstd[:], self.root[:]).then_inc(self.stats_done, 1)
        v.wait_ge(self.stats_done, 2 * B + 1)
        if self.rms_weight is not None:
            nc.vector.tensor_tensor(self.rrms[:], var, self.rstd[:], ALU.mult
                                    ).then_inc(self.stats_done, 1)
            v.wait_ge(self.stats_done, 2 * B + 2)
            nc.vector.tensor_tensor(self.rrms[:], self.rrms[:], self.rstd[:], ALU.mult
                                    ).then_inc(self.stats_done, 1)
            v.wait_ge(self.stats_done, 2 * B + 3)
            nc.vector.tensor_scalar(self.var_eps[:], self.rrms[:], EPS, None, ALU.add
                                    ).then_inc(self.moments, 1)
            v.wait_ge(self.rooted, 2)
            nc.vector.reciprocal(self.rrms[:], self.root[:]).then_inc(self.stats_done, 1)
            v.wait_ge(self.stats_done, 2 * B + 4)

    def scalar(self, a):
        nc, G = self.nc, self.G
        self.scalar_roots(a)
        with a.Fori(0, B) as i:
            a.wait_ge(self.turned, i + 1)
            nc.scalar.copy(G.xn[0][:, :, bass.ds(i * P, P)],
                           G.ps[:, i, :].rearrange("p (c t) -> p c t", c=C)).then_inc(self.hi_done, 1)

    def scalar_roots(self, a):
        nc = self.nc
        for k in range(1 if self.rms_weight is None else 2):
            a.wait_ge(self.moments, k + 1)
            nc.scalar.activation(self.root[:], self.var_eps[:], ACT.Sqrt).then_inc(self.rooted, 1)

    def tensor(self, pe):
        for i in range(B):
            pe.wait_ge(self.h_ready, i + 1)
            for c in range(C):
                last = self.nc.tensor.transpose(self.G.ps[:, i, c * P:(c + 1) * P],
                                                self.h[:, i % self.SLOTS, c * P:(c + 1) * P],
                                                self.G.ident[:])
            last.then_inc(self.turned, 1)


class Globals:
    pass


def load_phase(nc, G, d):
    with ExitStack() as ctx:
        t = Tiles(nc, ctx, "load")
        raw = t.sb("ctx_raw", [P, C, TOK])
        loaded = t.sem("loaded")
        ctx_in = [t.sem(f"ctx_in{c}") for c in range(C)]
        hi_done, lo_done = t.sem("hi_done"), t.sem("lo_done")
        block = ctx.enter_context(nc.Block())

        @block.sync
        def _(sp):
            sp.dma_start(G.x[:], d["x"].rearrange("b p d -> p b d")).then_inc(loaded, 16)
            for c in range(C):
                sp.dma_start(raw[:, c, :], d["ctxT"][c]).then_inc(ctx_in[c], 16)
            sp.dma_start(G.ident[:], d["ident"]).then_inc(loaded, 16)
            sp.wait_ge(loaded, 32)

        @block.gpsimd
        def _(pool):
            nc.gpsimd.memset(G.zero[:], 0.0)

        @block.scalar
        def _(a):
            for c in range(C):
                a.wait_ge(ctx_in[c], 16)
                nc.scalar.copy(G.ctx[0][:, c, :], raw[:, c, :]).then_inc(hi_done, 1)

        @block.vector
        def _(v):
            for c in range(C):
                v.wait_ge(hi_done, c + 1)
                nc.vector.tensor_tensor(G.ctx[1][:, c, :], raw[:, c, :],
                                        G.ctx[0][:, c, :].bitcast(F32), ALU.subtract)


class Attention:

    def __init__(self, name, groups, dh, shared_kv, on_latents, scale, bias, mask, rope):
        self.name, self.groups, self.dh, self.shared_kv = name, groups, dh, shared_kv
        self.on_latents, self.scale, self.bias, self.mask, self.rope = on_latents, scale, bias, mask, rope


def attention_phase(nc, G, d, A):
    NJ, dh, NG = 4, A.dh, A.groups
    QW = NJ * dh
    sources = [G.ctx] + ([G.xn] if A.on_latents else [])
    NS = len(sources)
    NK = NS * P
    own_kv = not A.shared_kv
    ks, vs = (range(NJ), range(HB)) if own_kv else (range(NS), range(NS))
    if own_kv:
        order = "Q0 K0 Q1 K1 S0 Q2 E0 K2 N0 S1 Q3 E1 K3 N1 S2 V0 E2 S3 N2 V1 E3 N3 " \
                "T0 A0 V2 T1 O0 A1 V3 T2 O1 A2 T3 O2 A3 O3"
    elif NS == 2:
        order = "K0 K1 Q0 Q1 S0 S1 Q2 E0 N0 S2 S3 Q3 E1 N1 S4 S5 V0 E2 N2 S6 S7 V1 E3 N3 " \
                "T0 T1 A0 T2 T3 O0 A1 T4 T5 O1 A2 T6 T7 O2 A3 O3"
    else:
        order = "R0 R1 K0 R2 Q0 S0 Q1 R3 E0 S1 Q2 R4 N0 S2 E1 Q3 V0 N1 E2 S3 N2 E3 N3 " \
                "T0 A0 T1 O0 A1 T2 O1 A2 T3 O2 A3 O3"
    steps = [(s[0], int(s[1:])) for s in order.split()]
    jobs = [s for s in steps if s[0] in "QKV"]
    if A.rope:
        pe_steps = []
        names = iter([("K", 0), ("Q", 0), ("Q", 1), ("Q", 2), ("Q", 3)])
        for s in steps:
            if s[0] == "R":
                pe_steps.append(next(names))
            elif s[0] == "V" or s[0] not in "QK":
                pe_steps.append(s)
    else:
        pe_steps = steps
    NJOBS, NSC, NT = len(jobs), NJ * NS, HB * NS
    assert NJOBS % 2 == 0

    with ExitStack() as ctx:
        t = Tiles(nc, ctx, A.name)
        KW = QW if own_kv else dh
        wq, wk, wv = t.pair("wq", [P, C, QW]), t.pair("wk", [P, C, KW]), t.pair("wv", [P, C, KW])
        wo = t.pair("wo", [dh, NJ, D])
        pieces = [("wq", wq, c) for c in range(C)]
        pieces += [("wk", wk, c) for c in range(C)] if own_kv else [("wk", wk, None)]
        pieces += [("wv", wv, c) for c in range(C)] if own_kv else [("wv", wv, None)]
        pieces += [("wo", wo, j) for j in range(NJ)]
        NP = len(pieces)
        N_QK = NP - (NJ + (C if own_kv else 1))
        N_QKV = NP - NJ
        STAGES = 4 if own_kv else 5
        assert NP % STAGES == 0
        stage = t.sb("stage", [P, STAGES, D])

        q = t.pair("q", [dh, 2, HALF])
        k = t.pair("k", [dh, 2 if own_kv else NS, HALF])
        v = t.pair("v", [P, 2, QW] if own_kv else [P, NS, HB * dh])
        probs = t.sb("probs", [P, NJ, HB * NK])
        probsT = t.pair("probsT", [P, NS, NJ * P])
        heads = t.pair("heads", [dh, NJ * P])
        neg_max = t.sb("neg_max", [P, NJ, HB])
        sums = t.sb("sums", [P, NJ, HB])
        recip = t.sb("recip", [P, NJ, HB])
        if A.bias:
            bias = t.sb("bias", [P, NJ, P])
            ln_w = stage[:, 0, :]
        if A.mask:
            mask_raw = stage[:, 1, 0:B * P // 4].bitcast(U8) if A.mask == "bool" else t.sb("mask_raw", [P, B * P])[:]
            mask_add = t.sb("mask_add", [P, B, P])
            row_kept = t.sb("row_kept", [P, B])
        if A.rope:
            cos, sin = t.sb("cos", [P, P]), t.sb("sin", [P, P])
            straight, crossed = t.sb("straight", [P, 2, HALF]), t.sb("crossed", [P, 2, HALF])

        staged = [t.sem(f"staged{s}") for s in range(STAGES)]
        stage_free = t.sem("stage_free")
        w_hi, w_ready = t.sem("w_hi"), t.sem("w_ready")
        qk_free = t.sem("qk_free")
        tables, mask_in, bias_in, bias_free = t.sem("tables"), t.sem("mask_in"), t.sem("bias_in"), t.sem("bias_free")
        start_used = t.sem("start_used")
        job_done, job_hi, job_out = t.sem("job_done"), t.sem("job_hi"), t.sem("job_out")
        scored, score_free = t.sem("scored"), t.sem("score_free")
        soft, max_ready, exp_done, probs_ready = t.sem("soft"), t.sem("max_ready"), t.sem("exp_done"), t.sem("probs_ready")
        turned, turned_hi, turned_out = t.sem("turned"), t.sem("turned_hi"), t.sem("turned_out")
        headed, heads_hi, heads_out = t.sem("headed"), t.sem("heads_hi"), t.sem("heads_out")
        projected, added = t.sem("projected"), t.sem("added")
        rotating, rotated = t.sem("rotating"), t.sem("rotated")
        norm = Norm(t, G, probs[:, :, 0:D], ln_w if A.bias else None)
        block = ctx.enter_context(nc.Block())

        PROJ, SCORE, TURN, HEAD, OUT = 0, 2, 4, 6, 7

        def job_of(kind, n):
            return jobs.index((kind, n))

        @block.sync
        def _(sp):
            if A.bias:
                sp.dma_start(ln_w, d["ln_w"].partition_broadcast(P)).then_inc(tables, 16)
            if A.mask:
                src = d[A.name + "_mask"].rearrange("b q k -> q b k")
                dst = mask_raw.bitcast(I32) if A.mask == "bool" else mask_raw
                sp.dma_start(dst.rearrange("p (b k) -> p b k", b=B), src).then_inc(mask_in, 16)
            if A.rope:
                sp.dma_start(cos[:], d["cos"]).then_inc(tables, 16)
                sp.dma_start(sin[:], d["sin"]).then_inc(tables, 16)
            if A.bias:
                sp.wait_ge(start_used, 2)
            with sp.Fori(0, NG) as g:
                for n, (name, _, c) in enumerate(pieces):
                    if A.bias and n == N_QK:
                        sp.wait_ge(bias_free, g + 1)
                        sp.dma_start(bias[:], d["bias"][g]).then_inc(bias_in, 16)
                    sp.wait_ge(stage_free, g * NP + n + 1)
                    if c is None:
                        dst = stage[:, n % STAGES, 0:C * dh].rearrange("p (c o) -> p c o", c=C)
                        src = d[A.name + "_" + name][g]
                    else:
                        src = d[A.name + "_" + name][g, c]
                        dst = stage[0:src.shape[0], n % STAGES, 0:src.shape[1]]
                    sp.dma_start(dst, src).then_inc(staged[n % STAGES], 16)

        @block.gpsimd
        def _(pool):
            pool.sem_inc(stage_free, STAGES)
            with pool.Fori(0, NG) as g:
                for n, (name, w, c) in enumerate(pieces):
                    if n == 0:
                        pool.wait_ge(qk_free, g + 1)
                    if n == N_QK:
                        pool.wait_ge(added, g * 2 * HB + 1)
                    turn = g * (NP // STAGES) + n // STAGES
                    pool.wait_ge(staged[n % STAGES], turn * 16 + 16)
                    if c is None:
                        hi, lo = w[0][:], w[1][:]
                        src = stage[:, n % STAGES, 0:C * dh].rearrange("p (c o) -> p c o", c=C)
                    else:
                        hi, lo = w[0][:, c, :], w[1][:, c, :]
                        src = stage[0:hi.shape[0], n % STAGES, 0:hi.shape[1]]
                    rounded(nc, G, hi, src).then_inc(w_hi, 1)
                    pool.wait_ge(w_hi, g * NP + n + 1)
                    nc.gpsimd.tensor_tensor(lo, src, hi.bitcast(F32), ALU.subtract).then_inc(w_ready, 1)
                    pool.wait_ge(w_ready, g * NP + n + 1)
                    pool.sem_inc(stage_free, 1)

        @block.tensor
        def _(pe):
            pe.sem_inc(qk_free, 1)
            norm.tensor(pe)
            pe.wait_ge(norm.lo_done, B)

            def half_group(g, hf):
                u = g * 2 + hf
                toks = slice(hf * HALF, (hf + 1) * HALF)

                def job(kind, n):
                    m = job_of(kind, n)
                    pe.wait_ge(job_out, u * NJOBS + m + 1)
                    bank = G.ps[:, PROJ + m % 2, :]
                    if kind in "QK":
                        if kind == "Q":
                            w, src, cols = wq, G.xn, slice(n * dh, (n + 1) * dh)
                        elif own_kv:
                            w, src, cols = wk, G.ctx, slice(n * dh, (n + 1) * dh)
                        else:
                            w, src, cols = wk, sources[n], slice(0, dh)
                        for c in range(C):
                            last = product(nc, bank[0:dh, :], at(w, ALL, c, cols), at(src, ALL, c, toks),
                                           c == 0, c == C - 1)
                    elif own_kv:
                        tile = slice((hf * HB + n) * P, (hf * HB + n + 1) * P)
                        for c in range(C):
                            last = product(nc, bank, at(G.ctx, ALL, c, tile), at(wv, ALL, c),
                                           c == 0, c == C - 1)
                    else:
                        for b in range(HB):
                            tile = slice((hf * HB + b) * P, (hf * HB + b + 1) * P)
                            for c in range(C):
                                last = product(nc, bank[:, b * dh:(b + 1) * dh],
                                               at(sources[n], ALL, c, tile), at(wv, ALL, c),
                                               c == 0, c == C - 1)
                    last.then_inc(job_done, 1)

                def out_of(kind, n):
                    return u * NJOBS + job_of(kind, n) + 1 + 2

                for kind, n in pe_steps:
                    if kind in "QKV":
                        if (kind, n) == ("V", 0):
                            pe.wait_ge(w_ready, g * NP + N_QKV)
                        job(kind, n)
                    elif kind == "S":
                        j, s = n // NS, n % NS
                        pe.wait_ge(score_free, u * NSC + n + 1)
                        pe.wait_ge(job_out, out_of("K", j) if own_kv else out_of("Q", j))
                        for b in range(HB):
                            col = slice(b * P, (b + 1) * P)
                            last = product(nc, G.ps[:, SCORE + n % 2, col], at(q, ALL, j % 2, col),
                                           at(k, ALL, j % 2 if own_kv else s, col), True, True)
                        last.then_inc(scored, 1)
                    elif kind == "T":
                        b, s = n // NS, n % NS
                        if n == 0:
                            pe.wait_ge(probs_ready, u * NJ + NJ)
                        for j in range(NJ):
                            src = probs[:, j, :].rearrange("p (b k) -> p b k", b=HB)
                            last = nc.tensor.transpose(G.ps[:, TURN + n % 2, j * P:(j + 1) * P],
                                                       src[:, b, s * P:(s + 1) * P], G.ident[:])
                            if hf == 1 and n == 0 and j == 0:
                                last.then_inc(qk_free, 1)
                        last.then_inc(turned, 1)
                    elif kind == "A":
                        pe.wait_ge(turned_out, u * NT + (n + 1) * NS)
                        if own_kv or n == 0:
                            pe.wait_ge(job_out, out_of("V", n if own_kv else NS - 1))
                        for j in range(NJ):
                            for s in range(NS):
                                val = (at(v, ALL, n % 2, slice(j * dh, (j + 1) * dh)) if own_kv
                                       else at(v, ALL, s, slice(n * dh, (n + 1) * dh)))
                                last = product(nc, G.ps[0:dh, HEAD, j * P:(j + 1) * P], val,
                                               at(probsT, ALL, s, slice(j * P, (j + 1) * P)),
                                               s == 0, s == NS - 1)
                        last.then_inc(headed, 1)
                    elif kind == "O":
                        if n == 0:
                            pe.wait_ge(w_ready, g * NP + NP)
                        pe.wait_ge(heads_out, u * HB + n + 1)
                        pe.wait_ge(added, u * HB + n + 1)
                        for j in range(NJ):
                            last = product(nc, G.ps[:, OUT, :], at(heads, ALL, slice(j * P, (j + 1) * P)),
                                           at(wo, ALL, j), j == 0, j == NJ - 1)
                        last.then_inc(projected, 1)

            with pe.Fori(0, NG) as g:
                pe.wait_ge(w_ready, g * NP + N_QK)
                half_group(g, 0)
                half_group(g, 1)

        def job_tiles(kind, n):
            m = job_of(kind, n)
            bank = G.ps[:, PROJ + m % 2, :]
            if kind == "Q":
                return bank[0:dh, :], at(q, ALL, n % 2)
            if kind == "K":
                return bank[0:dh, :], at(k, ALL, n % 2 if own_kv else n)
            if own_kv:
                return bank, at(v, ALL, n % 2)
            return bank[:, 0:HB * dh], at(v, ALL, n)

        @block.scalar
        def _(a):
            norm.scalar(a)

            def half_group(g, hf):
                u = g * 2 + hf
                for kind, n in steps:
                    if kind in "QKV":
                        m = job_of(kind, n)
                        src, (hi, _) = job_tiles(kind, n)
                        if A.rope and kind != "V":
                            a.wait_ge(rotated, u * (NJ + 1) + m + 1)
                            src = straight[:, m % 2, :]
                        else:
                            a.wait_ge(job_done, u * NJOBS + m + 1)
                        nc.scalar.copy(hi, src).then_inc(job_hi, 1)
                    elif kind == "E":
                        a.wait_ge(max_ready, u * NJ + n + 1)
                        for b in range(HB):
                            if A.mask:
                                src = probs[:, n, b * NK:(b + 1) * NK]
                                dst = src
                            else:
                                src = G.ps[:, SCORE:SCORE + NS, b * P:(b + 1) * P]
                                dst = probs[:, n, b * NK:(b + 1) * NK].rearrange("p (s k) -> p s k", s=NS)
                            last = nc.scalar.activation(dst, src, ACT.Exp, bias=neg_max[:, n, b:b + 1],
                                                        scale=A.scale, accum_out=sums[:, n, b:b + 1])
                        last.then_inc(exp_done, 1)
                    elif kind == "T":
                        a.wait_ge(turned, u * NT + n + 1)
                        nc.scalar.copy(probsT[0][:, n % NS, :], G.ps[:, TURN + n % 2, :]).then_inc(turned_hi, 1)
                    elif kind == "A":
                        a.wait_ge(headed, u * HB + n + 1)
                        nc.scalar.copy(heads[0][:], G.ps[0:dh, HEAD, :]).then_inc(heads_hi, 1)

            with a.Fori(0, NG) as g:
                half_group(g, 0)
                half_group(g, 1)

        @block.vector
        def _(dve):
            dve.sem_inc(job_out, 2)
            dve.sem_inc(score_free, 2)
            dve.sem_inc(added, 1)
            if A.bias:
                dve.sem_inc(bias_free, 1)
                dve.wait_ge(tables, 16)
            norm.vector(dve)
            n_soft = 0
            if A.bias:
                dve.wait_ge(norm.h_ready, B)
                dve.sem_inc(start_used, 1)
            if A.mask:
                dve.wait_ge(mask_in, 16)
                nc.vector.tensor_scalar(mask_add[:], mask_raw.rearrange("p (b k) -> p b k", b=B), 0.0, MASKED,
                                        ALU.is_equal, ALU.mult).then_inc(start_used, 1)
                dve.wait_ge(start_used, 2 if A.bias else 1)
                if A.bias:
                    nc.vector.tensor_reduce(row_kept[:], mask_add[:], AX.X, ALU.max).then_inc(start_used, 1)
                    dve.wait_ge(start_used, 3)
                    nc.vector.tensor_scalar(row_kept[:], row_kept[:], 0.0, None, ALU.is_equal
                                            ).then_inc(start_used, 1)
                    dve.wait_ge(start_used, 4)
            if A.rope:
                dve.wait_ge(tables, 32)

            PER_HEAD = (2 if A.bias else 1 if A.mask else 0) + (1 if A.scale != 1.0 else 0) + 1 + (1 if A.bias else 0)

            def half_group(g, hf):
                u = g * 2 + hf
                done = [0]

                def step(ins):
                    done[0] += 1
                    ins.then_inc(soft, 1)
                    dve.wait_ge(soft, u * (NJ * PER_HEAD) + done[0])

                for kind, n in steps:
                    if kind == "R":
                        src = G.ps[:, PROJ + n % 2, :]
                        by_tok = "p (b s) -> p b s"
                        dve.wait_ge(job_done, u * NJOBS + n + 1)
                        nc.vector.tensor_tensor(straight[:, n % 2, :].rearrange(by_tok, b=HB), src.rearrange(by_tok, b=HB),
                                                cos[:].unsqueeze(1).to_broadcast([P, HB, P]), ALU.mult)
                        h = P // 2
                        for lo_, hi_ in ((0, h), (h, 0)):
                            last = nc.vector.tensor_tensor(
                                crossed[lo_:lo_ + h, n % 2, :].rearrange(by_tok, b=HB),
                                src[hi_:hi_ + h, :].rearrange(by_tok, b=HB),
                                sin[hi_:hi_ + h, :].unsqueeze(1).to_broadcast([h, HB, P]), ALU.mult)
                        last.then_inc(rotating, 1)
                        dve.wait_ge(rotating, u * (NJ + 1) + n + 1)
                        nc.vector.tensor_tensor(straight[:, n % 2, :], straight[:, n % 2, :], crossed[:, n % 2, :], ALU.add
                                                ).then_inc(rotated, 1)
                    elif kind in "QKV":
                        m = job_of(kind, n)
                        src, (hi, lo) = job_tiles(kind, n)
                        if A.rope and kind != "V":
                            src = straight[:, m % 2, :]
                        dve.wait_ge(job_hi, u * NJOBS + m + 1)
                        nc.vector.tensor_tensor(lo, src, hi.bitcast(F32), ALU.subtract).then_inc(job_out, 1)
                    elif kind == "S":
                        j, s = n // NS, n % NS
                        if s < NS - 1:
                            continue
                        dve.wait_ge(scored, u * NSC + n + 1)
                        bank = G.ps[:, SCORE + n % 2, :]
                        pj = probs[:, j, :].rearrange("p (b k) -> p b k", b=HB)
                        if A.mask:
                            madd = mask_add[:, hf * HB:(hf + 1) * HB, :]
                            sc = bank.rearrange("p (b k) -> p b k", b=HB)
                            if A.bias:
                                if j == 0 and hf == 0:
                                    dve.wait_ge(bias_in, g * 16 + 16)
                                ins = nc.vector.tensor_tensor(pj, sc, bias[:, j, :].unsqueeze(1).to_broadcast([P, HB, P]),
                                                              ALU.add)
                                step(ins)
                                dve.sem_inc(score_free, 1)
                                if j == NJ - 1 and hf == 1:
                                    dve.sem_inc(bias_free, 1)
                                step(nc.vector.tensor_tensor(pj, pj, madd, ALU.add))
                            else:
                                step(nc.vector.tensor_tensor(pj, sc, madd, ALU.add))
                                dve.sem_inc(score_free, 1)
                            src, axis = pj, AX.X
                        else:
                            src, axis = G.ps[:, SCORE:SCORE + NS, :].rearrange("p s (b k) -> p b s k", b=HB), AX.XY
                        ins = nc.vector.tensor_reduce(neg_max[:, j, :], src, axis, ALU.max, negate=True)
                        if A.scale != 1.0:
                            step(ins)
                            ins = nc.vector.tensor_scalar(neg_max[:, j, :], neg_max[:, j, :], A.scale, None, ALU.mult)
                        ins.then_inc(max_ready, 1)
                    elif kind == "N":
                        dve.wait_ge(exp_done, u * NJ + n + 1)
                        if not A.mask:
                            dve.sem_inc(score_free, NS)
                        step(nc.vector.reciprocal(recip[:, n, :], sums[:, n, :]))
                        if A.bias:
                            step(nc.vector.tensor_tensor(recip[:, n, :], recip[:, n, :],
                                                         row_kept[:, hf * HB:(hf + 1) * HB], ALU.mult))
                        pj = probs[:, n, :].rearrange("p (b k) -> p b k", b=HB)
                        nc.vector.tensor_tensor(pj, pj, recip[:, n, :].unsqueeze(2).to_broadcast([P, HB, NK]),
                                                ALU.mult).then_inc(probs_ready, 1)
                    elif kind == "T":
                        dve.wait_ge(turned_hi, u * NT + n + 1)
                        nc.vector.tensor_tensor(probsT[1][:, n % NS, :], G.ps[:, TURN + n % 2, :],
                                                probsT[0][:, n % NS, :].bitcast(F32), ALU.subtract
                                                ).then_inc(turned_out, 1)
                    elif kind == "A":
                        dve.wait_ge(heads_hi, u * HB + n + 1)
                        nc.vector.tensor_tensor(heads[1][:], G.ps[0:dh, HEAD, :], heads[0][:].bitcast(F32),
                                                ALU.subtract).then_inc(heads_out, 1)
                    elif kind == "O":
                        dve.wait_ge(projected, u * HB + n + 1)
                        x = G.x[:, hf * HB + n, :]
                        nc.vector.tensor_tensor(x, x, G.ps[:, OUT, :], ALU.add).then_inc(added, 1)
                assert done[0] == NJ * PER_HEAD, (done, PER_HEAD)

            with dve.Fori(0, NG) as g:
                half_group(g, 0)
                half_group(g, 1)



def swiglu_phase(nc, G, d):
    I2 = 2
    NG, NP, WIDE = d["glu_w"].shape[0], I2 + 1, 2 * D
    DOWN = I2
    PAIRS = I2 * 2
    OUTS = 4

    with ExitStack() as ctx:
        t = Tiles(nc, ctx, "glu")
        h = t.sb("h", [P, Norm.SLOTS, D])
        stage, scales = t.sb("stage", [P, NP, WIDE]), t.sb("scales", [P, NP, WIDE])
        whole = t.sb("whole", [P, WIDE])
        w = t.pair("w", [P, NP, WIDE])
        gated = t.sb("gated", [P, 2, HALF])
        inner_f = t.sb("inner_f", [P, 2, HALF])
        inner = t.pair("inner", [P, I2, TOK])
        numbers_in = [t.sem(f"numbers_in{s}") for s in range(NP)]
        scales_in = [t.sem(f"scales_in{s}") for s in range(NP)]
        scaled, w_hi, w_ready = t.sem("scaled"), t.sem("w_hi"), t.sem("w_ready")
        gu_free = [t.sem(f"gu_free{i}") for i in range(I2)]
        gate_up, silu_done, pair_out = t.sem("gate_up"), t.sem("silu_done"), t.sem("pair_out")
        inner_hi, inner_out = t.sem("inner_hi"), t.sem("inner_out")
        projected, added = t.sem("projected"), t.sem("added")
        norm = Norm(t, G, h)
        block = ctx.enter_context(nc.Block())

        @block.sync
        def _(sp):
            with sp.Fori(0, NG) as g:
                for n in range(NP):
                    sp.wait_ge(scaled, g * NP + n + 1)
                    sp.dma_start(scales[:, n, :], d["glu_scale"][g, n].partition_broadcast(P)
                                 ).then_inc(scales_in[n], 16)

        @block.gpsimd
        def _(pool):
            def load(g, n):
                pool.dma_start(stage[:, n, :], d["glu_w"][g, n]).then_inc(numbers_in[n], 16)

            def turn(g, more):
                for n in range(NP):
                    m = g * NP + n
                    pool.wait_ge(numbers_in[n], g * 16 + 16)
                    pool.wait_ge(scales_in[n], g * 16 + 16)
                    if n == DOWN:
                        pool.wait_ge(added, g * B + OUTS)
                    else:
                        pool.wait_ge(gu_free[n], g + 1)
                    nc.gpsimd.tensor_tensor(w[0][:, n, :], stage[:, n, :], scales[:, n, :], ALU.mult).then_inc(w_hi, 1)
                    nc.gpsimd.tensor_tensor(whole[:], stage[:, n, :], scales[:, n, :], ALU.mult).then_inc(scaled, 1)
                    pool.wait_ge(scaled, m + NP + 1)
                    if more:
                        load(g + 1, n)
                    pool.wait_ge(w_hi, m + 1)
                    nc.gpsimd.tensor_tensor(w[1][:, n, :], whole[:], w[0][:, n, :].bitcast(F32), ALU.subtract
                                            ).then_inc(w_ready, 1)
                    pool.wait_ge(w_ready, m + 1)

            pool.sem_inc(scaled, NP)
            for n in range(NP):
                load(0, n)
            with pool.Fori(0, NG - 1) as g:
                turn(g, True)
            turn(NG - 1, False)

        @block.tensor
        def _(pe):
            for i in range(I2):
                pe.sem_inc(gu_free[i], 1)
            norm.tensor(pe)
            pe.wait_ge(norm.lo_done, B)
            with pe.Fori(0, NG) as g:
                for i in range(I2):
                    pe.wait_ge(w_ready, g * NP + i + 1)
                    for hf in range(2):
                        n = i * 2 + hf
                        pe.wait_ge(pair_out, g * PAIRS + n + 1)
                        for side in range(2):
                            for c in range(C):
                                last = product(nc, G.ps[:, 2 * (n % 2) + side, :],
                                               at(w, ALL, i, slice(side * D + c * P, side * D + (c + 1) * P)),
                                               at(G.xn, ALL, c, slice(hf * HALF, (hf + 1) * HALF)),
                                               c == 0, c == C - 1,
                                               gu_free[i - 1] if (n % 2, side, c) == (0, 0, 0) and i > 0 else None)
                        last.then_inc(gate_up, 1)
                pe.wait_ge(w_ready, g * NP + NP)
                for tile in range(B):
                    if tile % HB == 0:
                        pe.wait_ge(inner_out, g * PAIRS + PAIRS - 1 + tile // HB + 2)
                    pe.wait_ge(added, g * B + tile + 1)
                    for i in range(I2):
                        last = product(nc, G.ps[:, OUTS + tile % OUTS, :],
                                       at(inner, ALL, i, slice(tile * P, (tile + 1) * P)),
                                       at(w, ALL, DOWN, slice(i * D, (i + 1) * D)), i == 0, i == I2 - 1,
                                       gu_free[I2 - 1] if (tile, i) == (0, 0) else None)
                    last.then_inc(projected, 1)

        def inner_part(n):
            i, hf = n // 2, n % 2
            return at(inner, ALL, i, slice(hf * HALF, (hf + 1) * HALF))

        @block.scalar
        def _(a):
            norm.scalar(a)
            with a.Fori(0, NG) as g:
                for n in range(PAIRS + 1):
                    if n < PAIRS:
                        a.wait_ge(gate_up, g * PAIRS + n + 1)
                        nc.scalar.activation(gated[:, n % 2, :], G.ps[:, 2 * (n % 2), :], ACT.Silu
                                             ).then_inc(silu_done, 1)
                    if n > 0:
                        a.wait_ge(pair_out, g * PAIRS + n + 2)
                        nc.scalar.copy(inner_part(n - 1)[0], inner_f[:, (n - 1) % 2, :]).then_inc(inner_hi, 1)

        @block.vector
        def _(v):
            v.sem_inc(pair_out, 2)
            v.sem_inc(inner_out, 2)
            v.sem_inc(added, OUTS)
            norm.vector(v)
            with v.Fori(0, NG) as g:
                for n in range(PAIRS + 1):
                    if n < PAIRS:
                        v.wait_ge(inner_out, g * PAIRS + n + 1)
                        v.wait_ge(silu_done, g * PAIRS + n + 1)
                        nc.vector.tensor_tensor(inner_f[:, n % 2, :], gated[:, n % 2, :],
                                                G.ps[:, 2 * (n % 2) + 1, :], ALU.mult).then_inc(pair_out, 1)
                    if n > 0:
                        hi, lo = inner_part(n - 1)
                        v.wait_ge(inner_hi, g * PAIRS + n)
                        nc.vector.tensor_tensor(lo, inner_f[:, (n - 1) % 2, :], hi.bitcast(F32), ALU.subtract
                                                ).then_inc(inner_out, 1)
                for tile in range(B):
                    v.wait_ge(projected, g * B + tile + 1)
                    x = G.x[:, tile, :]
                    nc.vector.tensor_tensor(x, x, G.ps[:, OUTS + tile % OUTS, :], ALU.add).then_inc(added, 1)


def low_rank_phase(nc, G, d, name, rank, dense):
    RT = rank // P
    OUTS = 4
    with ExitStack() as ctx:
        t = Tiles(nc, ctx, name)
        h = t.sb("h", [P, Norm.SLOTS, D])
        a, b = t.pair("a", [P, C, rank]), t.pair("b", [P, RT, D])
        parts = [("a", a, C * rank), ("b", b, RT * D)]
        if dense:
            w = t.pair("w", [P, C, D])
            parts.append(("w", w, C * D))
            bias = t.sb("bias", [P, D])
        raw = {k: t.sb(k + "_raw", [P, n]) for k, _, n in parts}
        factors = t.sb("factors", [P, 2, RT])
        weight = t.sb("weight", [P, RT])
        low_f, low = t.sb("low_f", [P, RT, TOK]), t.pair("low", [P, RT, TOK])
        part_in = {k: t.sem(k + "_in") for k, _, _ in parts}
        small_in, w_hi, w_ready = t.sem("small_in"), t.sem("w_hi"), t.sem("w_ready")
        weight_ready, low_done, low_scaled = t.sem("weight_ready"), t.sem("low_done"), t.sem("low_scaled")
        low_hi, low_out, projected, added = t.sem("low_hi"), t.sem("low_out"), t.sem("projected"), t.sem("added")
        norm = Norm(t, G, h)
        block = ctx.enter_context(nc.Block())
        pieces = [(k, pr, n, c) for k, pr, n in parts for c in range(n // 512)]
        halves = [(r, hf) for r in range(RT) for hf in range(2)]
        smalls = 3 if dense else 1

        @block.sync
        def _(sp):
            for k, _, n in parts:
                sp.dma_start(raw[k][:], d[f"{name}_{k}"]).then_inc(part_in[k], 16)
            sp.dma_start(factors[:, 0, :], d[f"{name}_factor0"]).then_inc(small_in, 16)
            if dense:
                sp.dma_start(factors[:, 1, :], d[f"{name}_factor1"]).then_inc(small_in, 16)
                sp.dma_start(bias[:], d[f"{name}_bias"].partition_broadcast(P)).then_inc(small_in, 16)

        @block.gpsimd
        def _(pool):
            for m, (k, pr, n, c) in enumerate(pieces):
                if c == 0:
                    pool.wait_ge(part_in[k], 16)
                cols = slice(c * 512, (c + 1) * 512)
                hi, lo = (x[:].rearrange("p a b -> p (a b)")[:, cols] for x in pr)
                rounded(nc, G, hi, raw[k][:, cols]).then_inc(w_hi, 1)
                pool.wait_ge(w_hi, m + 1)
                nc.gpsimd.tensor_tensor(lo, raw[k][:, cols], hi.bitcast(F32), ALU.subtract).then_inc(w_ready, 1)

        @block.tensor
        def _(pe):
            norm.tensor(pe)
            pe.wait_ge(norm.lo_done, B)
            pe.wait_ge(w_ready, C * rank // 512)
            for n, (r, hf) in enumerate(halves):
                for c in range(C):
                    last = product(nc, G.ps[:, n, :], at(a, ALL, c, slice(r * P, (r + 1) * P)),
                                   at(G.xn, ALL, c, slice(hf * HALF, (hf + 1) * HALF)), c == 0, c == C - 1)
                last.then_inc(low_done, 1)
            pe.wait_ge(w_ready, len(pieces))
            if not dense:
                pe.wait_ge(low_out, len(halves))
            for tile in range(B):
                toks = slice(tile * P, (tile + 1) * P)
                if tile >= OUTS:
                    pe.wait_ge(added, tile - OUTS + 1)
                if dense:
                    for c in range(C):
                        product(nc, G.ps[:, OUTS + tile % OUTS, :], at(G.xn, ALL, c, toks), at(w, ALL, c),
                                c == 0, False)
                    if tile == 0:
                        pe.wait_ge(low_out, len(halves))
                for r in range(RT):
                    last = product(nc, G.ps[:, OUTS + tile % OUTS, :], at(low, ALL, r, toks), at(b, ALL, r),
                                   r == 0 and not dense, r == RT - 1)
                last.then_inc(projected, 1)

        @block.scalar
        def _(act):
            norm.scalar(act)
            act.wait_ge(weight_ready, 1)
            for n, (r, hf) in enumerate(halves):
                toks = slice(hf * HALF, (hf + 1) * HALF)
                act.wait_ge(low_done, n + 1)
                nc.scalar.mul(low_f[:, r, toks], G.ps[:, n, :], weight[:, r:r + 1]).then_inc(low_scaled, 1)
                act.wait_ge(low_scaled, n + 1)
                nc.scalar.copy(low[0][:, r, toks], low_f[:, r, toks]).then_inc(low_hi, 1)

        @block.vector
        def _(v):
            v.wait_ge(small_in, 16 * smalls)
            if dense:
                nc.vector.tensor_tensor(weight[:], factors[:, 0, :], factors[:, 1, :], ALU.mult
                                        ).then_inc(weight_ready, 1)
            else:
                nc.vector.tensor_copy(weight[:], factors[:, 0, :]).then_inc(weight_ready, 1)
            norm.vector(v)
            for n, (r, hf) in enumerate(halves):
                toks = slice(hf * HALF, (hf + 1) * HALF)
                v.wait_ge(low_hi, n + 1)
                nc.vector.tensor_tensor(low[1][:, r, toks], low_f[:, r, toks], low[0][:, r, toks].bitcast(F32),
                                        ALU.subtract).then_inc(low_out, 1)
            for tile in range(B):
                x = G.x[:, tile, :]
                v.wait_ge(projected, tile + 1)
                nc.vector.tensor_tensor(x, x, G.ps[:, OUTS + tile % OUTS, :], ALU.add).then_inc(added, 1)
                if dense:
                    v.wait_ge(added, tile + 1)
                    nc.vector.tensor_tensor(x, x, bias[:], ALU.add)


def linear_attention_phase(nc, G, d):
    H, DH = 8, P // 8
    R2 = 2
    KTURN, QTURN, KV, QBACK, OUT = 0, 2, 4, 5, 6
    with ExitStack() as ctx:
        t = Tiles(nc, ctx, "lin")
        h = t.sb("h", [P, R2, D])
        k_raw, k_soft = t.sb("k_raw", [P, R2, D]), t.sb("k_soft", [P, R2, D])
        k_max, k_sum, k_rec = t.sb("k_max", [P, R2]), t.sb("k_sum", [P, R2]), t.sb("k_rec", [P, R2])
        kT = t.pair("kT", [P, R2, D])
        own_head = t.sb("own_head", [P, P])
        kv_f, kv = t.sb("kv_f", [P, R2, P]), t.pair("kv", [P, R2, P])
        q_max, q_sum = t.sb("q_max", [P, R2, C * H]), t.sb("q_sum", [P, R2, C * H])
        qT = t.sb("qT", [P, R2, D])
        q = t.pair("q", [P, R2, D])
        k_in = [t.sem(f"k_in{i}") for i in range(R2)]
        table_in = t.sem("table_in")
        names = ("k_step k_maxed k_exped k_ready k_turned kT_hi kT_out kv_done kv_masked kv_hi kv_out "
                 "h_ready q_turned q_step q_shifted q_exped q_ready q_back q_hi q_out out_done added").split()
        S = {n: t.sem(n) for n in names}
        norm = Norm(t, G, h)
        block = ctx.enter_context(nc.Block())
        by_head = "p (g e) -> p g e"

        def wide(small):
            return small.unsqueeze(2).to_broadcast([P, C * H, DH])

        @block.sync
        def _(sp):
            sp.dma_start(own_head[:], d["own_head"]).then_inc(table_in, 16)
            with sp.Fori(0, B // R2) as t2:
                for i in range(R2):
                    n = t2 * R2 + i
                    sp.wait_ge(S["k_exped"], n + 1)
                    sp.dma_start(k_raw[:, i, :], d["ctx"][n]).then_inc(k_in[i], 16)

        @block.vector
        def _(v):
            norm.vector_stats(v)
            v.wait_ge(table_in, 16)
            with v.Fori(0, B // R2) as t2:
                for i in range(R2):
                    n = t2 * R2 + i
                    v.wait_ge(k_in[i], t2 * 16 + 16)
                    nc.vector.tensor_reduce(k_max[:, i:i + 1], k_raw[:, i, :], AX.X, ALU.max, negate=True
                                            ).then_inc(S["k_maxed"], 1)
                    nc.vector.tensor_scalar(h[:, i, :], G.x[:, n, :], norm.mean_var[:, n, 0:1],
                                            norm.rstd[:, bass.ds(n, 1)], ALU.subtract, ALU.mult
                                            ).then_inc(S["h_ready"], 1)
                for i in range(R2):
                    n = t2 * R2 + i
                    v.wait_ge(S["q_turned"], n + 1)
                    bank = G.ps[:, QTURN + i, :].rearrange(by_head, e=DH)
                    nc.vector.tensor_reduce(q_max[:, i, :], bank, AX.X, ALU.max).then_inc(S["q_step"], 1)
                    v.wait_ge(S["q_step"], n * 3 + 1)
                    nc.vector.tensor_tensor(qT[:, i, :].rearrange(by_head, e=DH), bank, wide(q_max[:, i, :]),
                                            ALU.subtract).then_inc(S["q_shifted"], 1)
                    v.wait_ge(S["k_exped"], n + R2 + 1)
                    nc.vector.reciprocal(k_rec[:, i:i + 1], k_sum[:, i:i + 1]).then_inc(S["k_step"], 1)
                    v.wait_ge(S["k_step"], n + 1)
                    nc.vector.tensor_scalar(k_soft[:, i, :], k_soft[:, i, :], k_rec[:, i:i + 1], None, ALU.mult
                                            ).then_inc(S["k_ready"], 1)
                    v.wait_ge(S["q_exped"], n + 1)
                    nc.vector.tensor_reduce(q_sum[:, i, :], qT[:, i, :].rearrange(by_head, e=DH), AX.X, ALU.add
                                            ).then_inc(S["q_step"], 1)
                    v.wait_ge(S["q_step"], n * 3 + 2)
                    nc.vector.reciprocal(q_sum[:, i, :], q_sum[:, i, :]).then_inc(S["q_step"], 1)
                    v.wait_ge(S["q_step"], n * 3 + 3)
                    nc.vector.tensor_tensor(qT[:, i, :].rearrange(by_head, e=DH), qT[:, i, :].rearrange(by_head, e=DH),
                                            wide(q_sum[:, i, :]), ALU.mult).then_inc(S["q_ready"], 1)
                for i in range(R2):
                    n = t2 * R2 + i
                    v.wait_ge(S["kT_hi"], n + 1)
                    nc.vector.tensor_tensor(kT[1][:, i, :], G.ps[:, KTURN + i, :], kT[0][:, i, :].bitcast(F32),
                                            ALU.subtract).then_inc(S["kT_out"], 1)
                    v.wait_ge(S["kv_done"], n + 1)
                    nc.vector.tensor_tensor(kv_f[:, i, :], G.ps[:, KV, 0:P], own_head[:], ALU.mult
                                            ).then_inc(S["kv_masked"], 1)
                    v.wait_ge(S["q_hi"], n + 1)
                    nc.vector.tensor_tensor(q[1][:, i, :], G.ps[:, QBACK, :], q[0][:, i, :].bitcast(F32),
                                            ALU.subtract).then_inc(S["q_out"], 1)
                    v.wait_ge(S["kv_hi"], n + 1)
                    nc.vector.tensor_tensor(kv[1][:, i, :], kv_f[:, i, :], kv[0][:, i, :].bitcast(F32),
                                            ALU.subtract).then_inc(S["kv_out"], 1)
                    v.wait_ge(S["out_done"], n + 1)
                    x = G.x[:, n, :]
                    nc.vector.tensor_tensor(x, x, G.ps[:, OUT + i, :], ALU.add).then_inc(S["added"], 1)

        @block.scalar
        def _(a):
            a.sem_inc(S["k_exped"], R2)
            norm.scalar_roots(a)
            with a.Fori(0, B // R2) as t2:
                for i in range(R2):
                    n = t2 * R2 + i
                    a.wait_ge(S["k_maxed"], n + 1)
                    nc.scalar.activation(k_soft[:, i, :], k_raw[:, i, :], ACT.Exp, bias=k_max[:, i:i + 1],
                                         accum_out=k_sum[:, i:i + 1]).then_inc(S["k_exped"], 1)
                    a.wait_ge(S["q_shifted"], n + 1)
                    nc.scalar.activation(qT[:, i, :], qT[:, i, :], ACT.Exp).then_inc(S["q_exped"], 1)
                for i in range(R2):
                    n = t2 * R2 + i
                    a.wait_ge(S["k_turned"], n + 1)
                    nc.scalar.copy(kT[0][:, i, :], G.ps[:, KTURN + i, :]).then_inc(S["kT_hi"], 1)
                    a.wait_ge(S["q_back"], n + 1)
                    nc.scalar.copy(q[0][:, i, :], G.ps[:, QBACK, :]).then_inc(S["q_hi"], 1)
                    a.wait_ge(S["kv_masked"], n + 1)
                    nc.scalar.copy(kv[0][:, i, :], kv_f[:, i, :]).then_inc(S["kv_hi"], 1)

        @block.tensor
        def _(pe):
            def turn(bank, src):
                for c in range(C):
                    last = nc.tensor.transpose(G.ps[:, bank, c * P:(c + 1) * P], src[:, c * P:(c + 1) * P], G.ident[:])
                return last

            with pe.Fori(0, B // R2) as t2:
                for i in range(R2):
                    n = t2 * R2 + i
                    pe.wait_ge(S["h_ready"], n + 1)
                    turn(QTURN + i, h[:, i, :]).then_inc(S["q_turned"], 1)
                for i in range(R2):
                    n = t2 * R2 + i
                    pe.wait_ge(S["k_ready"], n + 1)
                    turn(KTURN + i, k_soft[:, i, :]).then_inc(S["k_turned"], 1)
                for i in range(R2):
                    n = t2 * R2 + i
                    pe.wait_ge(S["q_ready"], n + 1)
                    turn(QBACK, qT[:, i, :]).then_inc(S["q_back"], 1)
                    pe.wait_ge(S["kT_out"], n + 1)
                    for c in range(C):
                        chunk = slice(c * P, (c + 1) * P)
                        last = product(nc, G.ps[:, KV, 0:P], at(kT, ALL, i, chunk),
                                       (G.ctx[0][:, c, bass.ds(n * P, P)], G.ctx[1][:, c, bass.ds(n * P, P)]),
                                       c == 0, c == C - 1)
                    last.then_inc(S["kv_done"], 1)
                    pe.wait_ge(S["kv_out"], n + 1)
                    pe.wait_ge(S["q_out"], n + 1)
                    product(nc, G.ps[:, OUT + i, :], at(kv, ALL, i), at(q, ALL, i), True, True
                            ).then_inc(S["out_done"], 1)


def experts_phase(nc, G, d, out):
    E = d["experts"].shape[0]
    E2 = 2
    NP = E2 * C
    STAGES = 4
    with ExitStack() as ctx:
        t = Tiles(nc, ctx, "moe")
        h = t.sb("h", [P, Norm.SLOTS, D])
        stage = t.sb("stage", [P, STAGES, D])
        w = t.pair("w", [P, E2, C * D])
        gate_raw, gate = t.sb("gate_raw", [P, C, E]), t.pair("gate", [P, C, E])
        numbers = t.sb("numbers", [P, E])
        logits = t.sb("logits", [P, B, E])
        top, top_at = t.sb("top", [P, B, 8]), t.sb("top_at", [P, B, 8], U32)
        top_no = t.sb("top_no", [P, B, 8])
        chosen = t.sb("chosen", [P, 2, B, E])
        share = t.sb("share", [P, 3, B])
        per_expert = t.sb("per_expert", [P, E, B])
        staged = [t.sem(f"staged{s}") for s in range(STAGES)]
        stage_free, w_hi, w_ready, w_free = t.sem("stage_free"), t.sem("w_hi"), t.sem("w_ready"), t.sem("w_free")
        small_in, gate_split = t.sem("small_in"), t.sem("gate_split")
        logits_done, route, exp_in, exp_done = t.sem("logits_done"), t.sem("route"), t.sem("exp_in"), t.sem("exp_done")
        projected, added, stored = t.sem("projected"), t.sem("added"), t.sem("stored")
        norm = Norm(t, G, h)
        block = ctx.enter_context(nc.Block())

        @block.sync
        def _(sp):
            sp.dma_start(gate_raw[:], d["gate_w"]).then_inc(small_in, 16)
            sp.dma_start(numbers[:], d["numbers"].partition_broadcast(P)).then_inc(small_in, 16)
            with sp.Fori(0, E // E2) as g:
                for n in range(NP):
                    sp.wait_ge(stage_free, g * NP + n + 1)
                    sp.dma_start(stage[:, n % STAGES, :], d["experts"][g * E2 + n // C, n % C]
                                 ).then_inc(staged[n % STAGES], 16)
            for tile in range(B):
                sp.wait_ge(added, E * B + tile + 1)
                sp.dma_start(out[tile], G.x[:, tile, :]).then_inc(stored, 16)
            sp.wait_ge(stored, 16 * B)

        @block.gpsimd
        def _(pool):
            pool.sem_inc(stage_free, STAGES)
            pool.wait_ge(small_in, 32)
            nc.gpsimd.tensor_copy(gate[0][:], gate_raw[:]).then_inc(gate_split, 1)
            pool.wait_ge(gate_split, 1)
            nc.gpsimd.tensor_tensor(gate[1][:], gate_raw[:], gate[0][:].bitcast(F32), ALU.subtract
                                    ).then_inc(gate_split, 1)
            with pool.Fori(0, E // E2) as g:
                for n in range(NP):
                    turn = g * (NP // STAGES) + n // STAGES
                    e, c = n // C, n % C
                    cols = slice(c * D, (c + 1) * D)
                    if c == 0:
                        pool.wait_ge(w_free, g * E2 + e + 1)
                    pool.wait_ge(staged[n % STAGES], turn * 16 + 16)
                    src = stage[:, n % STAGES, :]
                    rounded(nc, G, w[0][:, e, cols], src).then_inc(w_hi, 1)
                    pool.wait_ge(w_hi, g * NP + n + 1)
                    nc.gpsimd.tensor_tensor(w[1][:, e, cols], src, w[0][:, e, cols].bitcast(F32), ALU.subtract
                                            ).then_inc(w_ready, 1)
                    pool.wait_ge(w_ready, g * NP + n + 1)
                    pool.sem_inc(stage_free, 1)

        @block.tensor
        def _(pe):
            pe.sem_inc(w_free, 1)
            norm.tensor(pe)
            pe.wait_ge(norm.lo_done, B)
            pe.wait_ge(gate_split, 2)
            for tile in range(B):
                for c in range(C):
                    last = product(nc, G.ps[:, B - 1, tile * E:(tile + 1) * E],
                                   at(G.xn, ALL, c, slice(tile * P, (tile + 1) * P)), at(gate, ALL, c),
                                   c == 0, c == C - 1)
            last.then_inc(logits_done, 1)
            with pe.Fori(0, E // E2) as g:
                for e in range(E2):
                    pe.wait_ge(w_ready, g * NP + (e + 1) * C)
                    for tile in range(B):
                        pe.wait_ge(added, g * (E2 * B) + e * B + tile + 1)
                        for c in range(C):
                            last = product(nc, G.ps[:, tile, :], at(G.xn, ALL, c, slice(tile * P, (tile + 1) * P)),
                                           at(w, ALL, e, slice(c * D, (c + 1) * D)), c == 0, c == C - 1,
                                           w_free if tile == 0 and c == 0 else None)
                        last.then_inc(projected, 1)

        @block.scalar
        def _(a):
            norm.scalar(a)
            a.wait_ge(exp_in, 1)
            nc.scalar.activation(share[:, 1, :], share[:, 0, :], ACT.Exp).then_inc(exp_done, 1)

        @block.vector
        def _(v):
            norm.vector(v)
            done = [0]

            def step(ins):
                done[0] += 1
                ins.then_inc(route, 1)
                v.wait_ge(route, done[0])

            v.wait_ge(logits_done, 1)
            v.wait_ge(small_in, 32)
            step(nc.vector.tensor_copy(logits[:], G.ps[:, B - 1, 0:B * E].rearrange("p (t e) -> p t e", t=B)))
            v.sem_inc(added, B)
            for tile in range(B):
                last = nc.vector.max(top[:, tile, :], logits[:, tile, :])
            step(last)
            for tile in range(B):
                last = nc.vector.max_index(top_at[:, tile, :], top[:, tile, :], logits[:, tile, :])
            step(last)
            step(nc.vector.tensor_copy(top_no[:], top_at[:]))
            nc.vector.tensor_tensor(share[:, 0, :], top[:, :, 1], top[:, :, 0], ALU.subtract).then_inc(exp_in, 1)
            v.wait_ge(exp_done, 1)
            step(nc.vector.tensor_scalar(share[:, 0, :], share[:, 1, :], 1.0, None, ALU.add))
            step(nc.vector.reciprocal(share[:, 2, :], share[:, 0, :]))
            step(nc.vector.tensor_tensor(share[:, 1, :], share[:, 1, :], share[:, 2, :], ALU.mult))
            for rank, s in ((0, 2), (1, 1)):
                step(nc.vector.tensor_tensor(chosen[:, rank], numbers[:].unsqueeze(1).to_broadcast([P, B, E]),
                                             top_no[:, :, rank].unsqueeze(2).to_broadcast([P, B, E]), ALU.is_equal))
                step(nc.vector.tensor_tensor(chosen[:, rank], chosen[:, rank],
                                             share[:, s, :].unsqueeze(2).to_broadcast([P, B, E]), ALU.mult))
            step(nc.vector.tensor_tensor(per_expert[:].rearrange("p e t -> p t e"), chosen[:, 0], chosen[:, 1], ALU.add))
            with v.Fori(0, E) as e:
                for tile in range(B):
                    x = G.x[:, tile, :]
                    v.wait_ge(projected, e * B + tile + 1)
                    nc.vector.scalar_tensor_tensor(out=x, in0=G.ps[:, tile, :],
                                                   scalar=per_expert[:, e, tile:tile + 1], in1=x,
                                                   op0=ALU.mult, op1=ALU.add).then_inc(added, 1)


L0 = Attention("l0", groups=8, dh=128, shared_kv=False, on_latents=False, scale=1.0, bias=True, mask="bool", rope=False)
L1 = Attention("l1", groups=4, dh=96, shared_kv=True, on_latents=True, scale=float(1 / np.sqrt(np.float32(96))),
               bias=False, mask=None, rope=False)
L3 = Attention("l3", groups=8, dh=128, shared_kv=True, on_latents=False, scale=float(1 / np.sqrt(np.float32(128))),
               bias=False, mask="float", rope=True)


PHASES = [
    lambda nc, G, d, out: attention_phase(nc, G, d, L0),
    lambda nc, G, d, out: swiglu_phase(nc, G, d),
    lambda nc, G, d, out: attention_phase(nc, G, d, L1),
    lambda nc, G, d, out: low_rank_phase(nc, G, d, "lora", 256, True),
    lambda nc, G, d, out: linear_attention_phase(nc, G, d),
    lambda nc, G, d, out: low_rank_phase(nc, G, d, "svd", 128, False),
    lambda nc, G, d, out: attention_phase(nc, G, d, L3),
    lambda nc, G, d, out: experts_phase(nc, G, d, out),
]


def build_program(nc, d, out):
    with ExitStack() as ctx:
        t = Tiles(nc, ctx, "all")
        G = Globals()
        G.x = t.sb("x", [P, B, D])
        G.ctx = t.pair("ctx", [P, C, TOK])
        G.xn = t.pair("xn", [P, C, TOK])
        G.ident = t.sb("ident", [P, P])
        G.zero = t.sb("zero", [P, 1])
        G.ps = ctx.enter_context(nc.psum_tensor("ps", [P, 8, 512], F32))
        load_phase(nc, G, d)
        for phase in PHASES:
            phase(nc, G, d, out)


def laid_out(i):
    def rows(w, groups, width, parts):
        return w.reshape(groups, width, parts, -1).transpose(0, 2, 3, 1)

    def fused(w, groups, width):
        return w.reshape(groups, width, C, P).transpose(0, 3, 2, 1)

    def glu_pieces(gate, up, down):
        gu = np.concatenate([gate, up], 2).reshape(7, 2, -1, 2 * D)
        return np.concatenate([gu, np.concatenate([down[0::2], down[1::2]], 2)[:, None]], 1)

    a = {
        "x": i["x"], "ctx": i["ctx_4096"],
        "ctxT": i["ctx_4096"].reshape(TOK, C, P).transpose(1, 2, 0),
        "ident": np.eye(P, dtype=np.float32),
        "l0_mask": i["mask_BxSxS2_bk0"].view(np.int32),
        "bias": i["L0_xattn_position_bias"].reshape(8, 4, P, P).transpose(0, 2, 1, 3),
        "ln_w": i["L0_xattn_ln_weight"],
        "l0_wq": rows(i["L0_xattn_w_q"], 8, 512, C), "l0_wk": rows(i["L0_xattn_w_k"], 8, 512, C),
        "l0_wv": rows(i["L0_xattn_w_v"], 8, 512, C),
        "l0_wo": i["L0_xattn_w_out"].T.reshape(8, 4, P, D),
        "glu_w": glu_pieces(fused(i["L0_ffn_gate_q"], 14, P).reshape(14, P, D),
                            fused(i["L0_ffn_up_q"], 14, P).reshape(14, P, D),
                            i["L0_ffn_down_q"].T.reshape(14, P, D)),
        "glu_scale": glu_pieces(i["L0_ffn_gate_s"].reshape(14, P, C).transpose(0, 2, 1).reshape(14, 1, D),
                                i["L0_ffn_up_s"].reshape(14, P, C).transpose(0, 2, 1).reshape(14, 1, D),
                                i["L0_ffn_down_s"].T.reshape(14, 1, D))[:, :, 0, :],
        "l1_wq": rows(i["L1_xattn_Wq"], 4, 384, C), "l1_wk": fused(i["L1_xattn_Wk"], 4, 96),
        "l1_wv": fused(i["L1_xattn_Wv"], 4, 96), "l1_wo": i["L1_xattn_Wo"].T.reshape(4, 4, 96, D),
        "lora_w": fused(i["L1_ffn_W"], 1, D).reshape(P, C * D), "lora_bias": i["L1_ffn_bias"],
        "lora_a": fused(i["L1_ffn_A"].reshape(256, D), 1, 256).reshape(P, C * 256),
        "lora_b": i["L1_ffn_Bf"].transpose(0, 2, 1).reshape(2, P, D).transpose(1, 0, 2).reshape(P, 2 * D),
        "lora_factor0": np.repeat(i["L1_ffn_coeffs"], 16).reshape(2, P).T,
        "lora_factor1": np.repeat(i["L1_ffn_scales"], 16).reshape(2, P).T,
        "own_head": np.kron(np.eye(8), np.ones((16, 16))).astype(np.float32),
        "svd_a": i["L2_ffn_V"].reshape(C, P, P).transpose(1, 0, 2).reshape(P, C * P),
        "svd_b": i["L2_ffn_U"].T, "svd_factor0": i["L2_ffn_S"].reshape(P, 1),
        "l3_mask": i["mask_BxSxS2_ff1"],
        "l3_wq": i["L3_xattn_wq"].reshape(C, P, 8, 512).transpose(2, 0, 1, 3),
        "l3_wk": i["L3_xattn_wk"].reshape(C, P, 8, P).transpose(2, 1, 0, 3),
        "l3_wv": i["L3_xattn_wv"].reshape(C, P, 8, P).transpose(2, 1, 0, 3),
        "l3_wo": i["L3_xattn_wo"].reshape(8, 4, P, D),
        "gate_w": i["L3_ffn_gate_w"].reshape(C, P, 8).transpose(1, 0, 2),
        "experts": i["L3_ffn_expert_w"].reshape(8, C, P, D),
        "numbers": np.arange(8, dtype=np.float32),
    }
    rate = (np.float32(1.0) / np.float32(10000.0) ** (np.arange(0, P, 2, dtype=np.float32) / np.float32(P)))
    angle = np.arange(P, dtype=np.float32)[:, None] * rate[None, :].astype(np.float32)
    a["cos"] = np.concatenate([np.cos(angle), np.cos(angle)], 1).T
    a["sin"] = np.concatenate([np.sin(angle), -np.sin(angle)], 1).T
    return {k: np.ascontiguousarray(v) for k, v in a.items()}


def kernel(**inputs):
    import concourse.bacc as bacc
    from concourse.bass_utils import run_bass_kernel_spmd

    nc = bacc.Bacc("TRN2", target_bir_lowering=False, num_devices=1)
    arrays = laid_out({k: np.asarray(v) for k, v in inputs.items()})
    d = {k: nc.dram_tensor("in_" + k, v.shape, mybir.dt.from_np(v.dtype), kind="ExternalInput").ap()
         for k, v in arrays.items()}
    out = nc.dram_tensor("out", (B, P, D), F32, kind="ExternalOutput").ap()
    build_program(nc, d, out)
    got = run_bass_kernel_spmd(nc, [{"in_" + k: v for k, v in arrays.items()}], core_ids=[0])
    return got.results[0]["out"]
```

```python
from contextlib import ExitStack

import numpy as np

import concourse.bass as bass
from concourse import mybir

F32, F32R = mybir.dt.float32, mybir.dt.float32r
BF16, I32, U32, U8 = mybir.dt.bfloat16, mybir.dt.int32, mybir.dt.uint32, mybir.dt.uint8
ALU, ACT, AX = mybir.AluOpType, mybir.ActivationFunctionType, mybir.AxisListType

P = 128
B = 8
D = 512
C = D // P
TOK = B * P
HALF = TOK // 2
HB = B // 2
EPS = 1e-5
MASKED = -1e30


class Tiles:

    def __init__(self, nc, ctx, name):
        self.nc, self.ctx, self.name, self.sems = nc, ctx, name, []
        ctx.callback(self.clear)

    def clear(self):
        if self.sems:
            self.nc.clear_and_free_semaphores(self.sems)
            self.nc.all_engine_barrier()

    def sb(self, name, shape, dt=F32):
        return self.ctx.enter_context(self.nc.sbuf_tensor(f"{self.name}_{name}", shape, dt))

    def pair(self, name, shape):
        return self.sb(name + "_hi", shape, F32R), self.sb(name + "_lo", shape, F32R)

    def sem(self, name):
        self.sems.append(self.nc.alloc_semaphore(f"{self.name}_{name}"))
        return self.sems[-1]


def product(nc, out, wt, x, first, last, begun=None):
    (wh, wl), (xh, xl) = wt, x
    ins = nc.tensor.matmul(out, wh, xh, start=first, stop=False)
    if begun is not None:
        ins.then_inc(begun, 1)
    nc.tensor.matmul(out, wl, xh, start=False, stop=False)
    return nc.tensor.matmul(out, wh, xl, start=False, stop=last)


def rounded(nc, G, hi, x):
    zero = G.zero[0:x.shape[0]]
    for size in x.shape[2:]:
        zero = zero.unsqueeze(1)
    return nc.gpsimd.tensor_tensor(hi, x, zero.to_broadcast(list(x.shape)), ALU.add)


def at(pair, *index):
    return pair[0][index], pair[1][index]


ALL = slice(None)


class Norm:

    def __init__(self, t, G, h, rms_weight=None):
        self.SLOTS = h.shape[1]
        self.nc, self.G, self.h, self.rms_weight = t.nc, G, h, rms_weight
        self.stats = t.sb("ln_stats", [P, B, 6])
        self.mean_var = t.sb("ln_mean_var", [P, B, 2])
        self.var_eps = t.sb("ln_var_eps", [P, B])
        self.root = t.sb("ln_root", [P, B])
        self.rstd = t.sb("ln_rstd", [P, B])
        self.rrms = t.sb("ln_rrms", [P, B])
        self.stats_done = t.sem("ln_stats_done")
        self.moments = t.sem("ln_moments")
        self.rooted = t.sem("ln_rooted")
        self.h_step = t.sem("ln_h_step")
        self.h_ready = t.sem("ln_h_ready")
        self.turned = t.sem("ln_turned")
        self.hi_done = t.sem("ln_hi_done")
        self.lo_done = t.sem("ln_lo_done")

    def normed(self, v, i, tile):
        nc, h, x = self.nc, self.h, self.G.x
        if self.rms_weight is None:
            nc.vector.tensor_scalar(h[:, i, :], x[:, tile, :], self.mean_var[:, tile, 0:1],
                                    self.rstd[:, bass.ds(tile, 1)], ALU.subtract, ALU.mult
                                    ).then_inc(self.h_ready, 1)
            return
        nc.vector.tensor_scalar(h[:, i, :], x[:, tile, :], self.mean_var[:, tile, 0:1],
                                self.rstd[:, bass.ds(tile, 1)], ALU.subtract, ALU.mult
                                ).then_inc(self.h_step, 1)
        v.wait_ge(self.h_step, tile * 2 + 1)
        nc.vector.tensor_tensor(x[:, tile, :], x[:, tile, :], h[:, i, :], ALU.add
                                ).then_inc(self.h_step, 1)
        v.wait_ge(self.h_step, tile * 2 + 2)
        nc.vector.scalar_tensor_tensor(out=h[:, i, :], in0=h[:, i, :],
                                       scalar=self.rrms[:, bass.ds(tile, 1)],
                                       in1=self.rms_weight[:], op0=ALU.mult, op1=ALU.mult
                                       ).then_inc(self.h_ready, 1)

    def low(self, v, tile):
        G, cols = self.G, bass.ds(tile * P, P)
        v.wait_ge(self.hi_done, tile + 1)
        self.nc.vector.tensor_tensor(
            G.xn[1][:, :, cols], G.ps[:, tile, :].rearrange("p (c t) -> p c t", c=C),
            G.xn[0][:, :, cols].bitcast(F32), ALU.subtract).then_inc(self.lo_done, 1)

    def vector(self, v):
        self.vector_stats(v)
        with v.Fori(0, self.SLOTS) as i:
            self.normed(v, i, i)
        for turn in range(B // self.SLOTS - 1):
            with v.Fori(0, self.SLOTS) as i:
                tile = i + turn * self.SLOTS
                v.wait_ge(self.turned, tile + 1)
                self.normed(v, i, tile + self.SLOTS)
                self.low(v, tile)
        with v.Fori(B - self.SLOTS, B) as i:
            self.low(v, i)

    def vector_stats(self, v):
        nc, G = self.nc, self.G
        with v.Fori(0, B) as i:
            nc.vector.bn_stats(self.stats[:, i, :], G.x[:, i, :]).then_inc(self.stats_done, 1)
        v.wait_ge(self.stats_done, B)
        for i in range(B):
            nc.vector.bn_aggr(self.mean_var[:, i, :], self.stats[:, i, :]).then_inc(self.stats_done, 1)
        v.wait_ge(self.stats_done, 2 * B)
        var = self.mean_var[:, :, 1]
        nc.vector.tensor_scalar(self.var_eps[:], var, EPS, None, ALU.add).then_inc(self.moments, 1)
        v.wait_ge(self.rooted, 1)
        nc.vector.reciprocal(self.rstd[:], self.root[:]).then_inc(self.stats_done, 1)
        v.wait_ge(self.stats_done, 2 * B + 1)
        if self.rms_weight is not None:
            nc.vector.tensor_tensor(self.rrms[:], var, self.rstd[:], ALU.mult
                                    ).then_inc(self.stats_done, 1)
            v.wait_ge(self.stats_done, 2 * B + 2)
            nc.vector.tensor_tensor(self.rrms[:], self.rrms[:], self.rstd[:], ALU.mult
                                    ).then_inc(self.stats_done, 1)
            v.wait_ge(self.stats_done, 2 * B + 3)
            nc.vector.tensor_scalar(self.var_eps[:], self.rrms[:], EPS, None, ALU.add
                                    ).then_inc(self.moments, 1)
            v.wait_ge(self.rooted, 2)
            nc.vector.reciprocal(self.rrms[:], self.root[:]).then_inc(self.stats_done, 1)
            v.wait_ge(self.stats_done, 2 * B + 4)

    def scalar(self, a):
        nc, G = self.nc, self.G
        self.scalar_roots(a)
        with a.Fori(0, B) as i:
            a.wait_ge(self.turned, i + 1)
            nc.scalar.copy(G.xn[0][:, :, bass.ds(i * P, P)],
                           G.ps[:, i, :].rearrange("p (c t) -> p c t", c=C)).then_inc(self.hi_done, 1)

    def scalar_roots(self, a):
        nc = self.nc
        for k in range(1 if self.rms_weight is None else 2):
            a.wait_ge(self.moments, k + 1)
            nc.scalar.activation(self.root[:], self.var_eps[:], ACT.Sqrt).then_inc(self.rooted, 1)

    def tensor(self, pe):
        for i in range(B):
            pe.wait_ge(self.h_ready, i + 1)
            for c in range(C):
                last = self.nc.tensor.transpose(self.G.ps[:, i, c * P:(c + 1) * P],
                                                self.h[:, i % self.SLOTS, c * P:(c + 1) * P],
                                                self.G.ident[:])
            last.then_inc(self.turned, 1)


class Globals:
    pass


def load_phase(nc, G, d):
    with ExitStack() as ctx:
        t = Tiles(nc, ctx, "load")
        raw = t.sb("ctx_raw", [P, C, TOK])
        loaded = t.sem("loaded")
        ctx_in = [t.sem(f"ctx_in{c}") for c in range(C)]
        hi_done, lo_done = t.sem("hi_done"), t.sem("lo_done")
        block = ctx.enter_context(nc.Block())

        @block.sync
        def _(sp):
            sp.dma_start(G.x[:], d["x"].rearrange("b p d -> p b d")).then_inc(loaded, 16)
            for c in range(C):
                sp.dma_start(raw[:, c, :], d["ctxT"][c]).then_inc(ctx_in[c], 16)
            sp.dma_start(G.ident[:], d["ident"]).then_inc(loaded, 16)
            sp.wait_ge(loaded, 32)

        @block.gpsimd
        def _(pool):
            nc.gpsimd.memset(G.zero[:], 0.0)

        @block.scalar
        def _(a):
            for c in range(C):
                a.wait_ge(ctx_in[c], 16)
                nc.scalar.copy(G.ctx[0][:, c, :], raw[:, c, :]).then_inc(hi_done, 1)

        @block.vector
        def _(v):
            for c in range(C):
                v.wait_ge(hi_done, c + 1)
                nc.vector.tensor_tensor(G.ctx[1][:, c, :], raw[:, c, :],
                                        G.ctx[0][:, c, :].bitcast(F32), ALU.subtract)


class Attention:

    def __init__(self, name, groups, dh, shared_kv, on_latents, scale, bias, mask, rope, order):
        self.name, self.groups, self.dh, self.shared_kv = name, groups, dh, shared_kv
        self.on_latents, self.scale, self.bias, self.mask, self.rope = on_latents, scale, bias, mask, rope
        self.steps = []
        for word in order.split():
            half = 0 if word[0] == "a" else 1
            name = word if word[0] == "W" else word[1:]
            kind = name.rstrip("0123456789")
            self.steps.append((half, kind, int(name[len(kind):])))

    def index(self, half, kind, n, kinds):
        return [s for s in self.steps if s[1] in kinds].index((half, kind, n))


def attention_phase(nc, G, d, A):
    NJ, dh, NG, steps = 4, A.dh, A.groups, A.steps
    QW = NJ * dh
    sources = [G.ctx] + ([G.xn] if A.on_latents else [])
    NS = len(sources)
    NK = NS * P
    own_kv = not A.shared_kv
    HEADS = 2 * NJ
    JOBS = sum(s[1] in ("Q", "K", "V", "U") for s in steps)
    ROTATED = sum(s[1] in ("Q", "K") for s in steps)
    NV = sum(s[1] in ("V", "U") for s in steps)
    assert JOBS % 2 == 0
    Q_RING = 4 if A.rope else 2
    P_RING = 2 if NS == 2 or own_kv else 4
    HEAD_BANKS = 2 if NS == 1 else 1
    HEAD_RING = 1 if own_kv else 2
    PROJ, SCORE, TURN, OUT = 0, 2, 4, 7
    HEAD = TURN + NS
    SCORE_RING = 2 // NS

    with ExitStack() as ctx:
        t = Tiles(nc, ctx, A.name)
        KW = QW if own_kv else dh
        wq, wk, wv = t.pair("wq", [P, C, QW]), t.pair("wk", [P, C, KW]), t.pair("wv", [P, C, KW])
        wo = t.pair("wo", [dh, NJ, D])
        pieces = [("wq", wq, c) for c in range(C)]
        pieces += [("wk", wk, c) for c in range(C)] if own_kv else [("wk", wk, None)]
        N_QK = len(pieces)
        pieces += [("wv", wv, c) for c in range(C)] if own_kv else [("wv", wv, None)]
        N_QKV = len(pieces)
        pieces += [("wo", wo, j) for j in range(NJ)]
        NP = len(pieces)
        STAGES = 4 if own_kv else 5
        assert NP % STAGES == 0
        stage = t.sb("stage", [P, STAGES, D])

        q = t.pair("q", [dh, Q_RING, HALF])
        k = t.pair("k", [dh, 2, HALF] if own_kv else [dh, HB, NK])
        v = t.pair("v", [P, 2, QW] if own_kv else [P, NS, HB * dh])
        if not own_kv:
            values_turned = t.sb("values_turned", [dh, HALF])
        probs = t.sb("probs", [P, P_RING, HB * NK])
        probsT = t.pair("probsT", [P, NS, NJ, HB * P])
        heads = t.pair("heads", [dh, HEAD_RING, NJ * P])
        neg_max = t.sb("neg_max", [P, NJ, HB])
        sums = t.sb("sums", [P, NJ, HB])
        recip = t.sb("recip", [P, NJ, HB])
        if A.bias:
            bias = t.sb("bias", [P, NJ, P])
            ln_w = bias[:].rearrange("p j k -> p (j k)")
        if A.mask:
            mask_raw = stage[:, STAGES - 1, 0:B * P // 4].bitcast(U8) if A.mask == "bool" else \
                t.sb("mask_raw", [P, B * P])[:]
            mask_add = t.sb("mask_add", [P, B, P], BF16)
            row_kept = t.sb("row_kept", [P, B])
        if A.rope:
            cos, sin = t.sb("cos", [P, P]), t.sb("sin", [P, P])
            straight, crossed = t.sb("straight", [P, 2, HALF]), t.sb("crossed", [P, 2, HALF])

        staged = [t.sem(f"staged{s}") for s in range(STAGES)]
        stage_free = t.sem("stage_free")
        first_hi, w_hi, w_ready = t.sem("first_hi"), t.sem("w_hi"), t.sem("w_ready")
        tables, mask_in, bias_in, bias_free = t.sem("tables"), t.sem("mask_in"), t.sem("bias_in"), t.sem("bias_free")
        start_used = t.sem("start_used")
        job_done, job_hi, job_out = t.sem("job_done"), t.sem("job_hi"), t.sem("job_out")
        scored, score_free = t.sem("scored"), t.sem("score_free")
        soft, max_ready, exp_done = t.sem("soft"), t.sem("max_ready"), t.sem("exp_done")
        recip_ready, probs_ready = t.sem("recip_ready"), t.sem("probs_ready")
        turned, turned_hi, turned_out = t.sem("turned"), t.sem("turned_hi"), t.sem("turned_out")
        headed, heads_hi, heads_out = t.sem("headed"), t.sem("heads_hi"), t.sem("heads_out")
        projected, added = t.sem("projected"), t.sem("added")
        if A.rope:
            bank_read, crossing, rotated = t.sem("bank_read"), t.sem("crossing"), t.sem("rotated")
            rotated_hi, rotated_out = t.sem("rotated_hi"), t.sem("rotated_out")
        norm = Norm(t, G, probs[:].rearrange("p a (b c) -> p (a b) c", c=D), ln_w if A.bias else None)
        block = ctx.enter_context(nc.Block())

        def job_no(half, kind, n):
            return A.index(half, kind, n, ("Q", "K", "V", "U"))

        def rotated_no(half, kind, n):
            return A.index(half, kind, n, ("Q", "K"))

        def value_no(half, kind, n):
            return A.index(half, kind, n, ("V", "U"))

        def head_no(half, j):
            return half * NJ + j

        def batch_no(half, b):
            return half * HB + b

        def split_piece(g, n):
            if n < NJ:
                return pieces[N_QKV + n], g * NP + N_QKV + n
            return pieces[n - NJ], g * NP + NP + n - NJ

        def slot_of(n):
            return (N_QKV + n) % STAGES

        def piece_tiles(piece, slot):
            name, w, c = piece
            if c is None:
                return w[0][:], w[1][:], stage[:, slot, 0:C * dh].rearrange("p (c o) -> p c o", c=C)
            hi, lo = w[0][:, c, :], w[1][:, c, :]
            return hi, lo, stage[0:hi.shape[0], slot, 0:hi.shape[1]]

        def arrived(eng, g, n):
            turns = g * (NP // STAGES) + (N_QKV + n) // STAGES
            eng.wait_ge(staged[slot_of(n)], turns * 16 + 16)

        def rotated_tiles(kind, n, m):
            src = straight[:, m % 2, :]
            if kind == "HQ":
                return *at(q, ALL, n), src
            return *at(k, ALL, ALL, slice(0, P)), src.rearrange("p (b t) -> p b t", b=HB)

        def score_bank(i, b):
            if NS == 1:
                return G.ps[:, SCORE + i % 2, b * P:(b + 1) * P]
            return G.ps[:, SCORE + b // 2, b % 2 * NK:(b % 2 + 1) * NK]

        @block.sync
        def _(sp):
            if A.bias:
                sp.dma_start(ln_w, d["ln_w"].partition_broadcast(P)).then_inc(tables, 16)
            if A.mask:
                src = d[A.name + "_mask"].rearrange("b q k -> q b k")
                dst = mask_raw.bitcast(I32) if A.mask == "bool" else mask_raw
                sp.dma_start(dst.rearrange("p (b k) -> p b k", b=B), src).then_inc(mask_in, 16)
            if A.rope:
                sp.dma_start(cos[:], d["cos"]).then_inc(tables, 16)
                sp.dma_start(sin[:], d["sin"]).then_inc(tables, 16)

            def load(piece, g, place, slot):
                name, _, c = piece
                sp.wait_ge(stage_free, place + 1)
                src = d[A.name + "_" + name][g] if c is None else d[A.name + "_" + name][g, c]
                sp.dma_start(piece_tiles(piece, slot)[2], src).then_inc(staged[slot], 16)

            def group(g, more):
                if A.bias:
                    sp.wait_ge(bias_free, g + 1)
                    sp.dma_start(bias[:], d["bias"][g]).then_inc(bias_in, 16)
                for n in range(NP if more else NJ):
                    piece, place = split_piece(g, n)
                    load(piece, g if n < NJ else g + 1, place, slot_of(n))

            for n in range(N_QKV):
                if A.mask == "bool" and n == STAGES - 1:
                    sp.wait_ge(start_used, 1)
                load(pieces[n], 0, n, n % STAGES)
            with sp.Fori(0, NG - 1) as g:
                group(g, True)
            group(NG - 1, False)

        @block.gpsimd
        def _(pool):
            pool.sem_inc(stage_free, STAGES)
            for n in range(N_QKV):
                hi, lo, raw = piece_tiles(pieces[n], n % STAGES)
                pool.wait_ge(staged[n % STAGES], 16 * (n // STAGES) + 16)
                rounded(nc, G, hi, raw).then_inc(first_hi, 1)
                pool.wait_ge(first_hi, n + 1)
                nc.gpsimd.tensor_tensor(lo, raw, hi.bitcast(F32), ALU.subtract).then_inc(w_ready, 1)
                pool.wait_ge(w_ready, n + 1)
                pool.sem_inc(stage_free, 1)

            def group(g, more):
                for half, kind, n in steps:
                    if kind == "W" and (more or n < NJ):
                        piece, place = split_piece(g, n)
                        hi, lo, raw = piece_tiles(piece, slot_of(n))
                        pool.wait_ge(w_hi, place - N_QKV + 1)
                        nc.gpsimd.tensor_tensor(lo, raw, hi.bitcast(F32), ALU.subtract).then_inc(w_ready, 1)
                        pool.wait_ge(w_ready, place + 1)
                        pool.sem_inc(stage_free, 1)
                    elif kind == "N":
                        i = head_no(half, n)
                        pool.wait_ge(recip_ready, g * HEADS + i + 1)
                        pj = probs[:, i % P_RING, :].rearrange("p (b k) -> p b k", b=HB)
                        nc.gpsimd.tensor_tensor(pj, pj, recip[:, n, :].unsqueeze(2).to_broadcast([P, HB, NK]),
                                                ALU.mult).then_inc(probs_ready, 1)
                    elif kind in ("Q", "K") and A.rope:
                        m = rotated_no(half, kind, n)
                        pool.wait_ge(crossing, g * ROTATED + m + 1)
                        nc.gpsimd.tensor_tensor(straight[:, m % 2, :], straight[:, m % 2, :], crossed[:, m % 2, :],
                                                ALU.add).then_inc(rotated, 1)
                    elif kind in ("HQ", "HK"):
                        m = rotated_no(half, kind[1], n)
                        hi, lo, src = rotated_tiles(kind, n, m)
                        pool.wait_ge(rotated_hi, g * ROTATED + m + 1)
                        nc.gpsimd.tensor_tensor(lo, src, hi.bitcast(F32), ALU.subtract
                                                ).then_inc(rotated_out, 1)

            with pool.Fori(0, NG - 1) as g:
                group(g, True)
            group(NG - 1, False)

        @block.tensor
        def _(pe):
            pe.sem_inc(projected, HEAD_RING)
            pe.sem_inc(turned, P_RING)
            norm.tensor(pe)
            pe.wait_ge(norm.lo_done, HB)

            def job(g, half, kind, n):
                m = job_no(half, kind, n)
                pe.wait_ge(bank_read if A.rope else job_out, g * JOBS + m + 1)
                bank = G.ps[:, PROJ + m % 2, :]
                if kind in ("Q", "K"):
                    toks = slice(half * HALF, (half + 1) * HALF)
                    w, src = (wq, G.xn) if kind == "Q" else (wk, G.ctx if own_kv else sources[n])
                    cols = slice(n * dh, (n + 1) * dh) if kind == "Q" or own_kv else slice(0, dh)
                    for c in range(C):
                        last = product(nc, bank[0:dh, :], at(w, ALL, c, cols), at(src, ALL, c, toks),
                                       c == 0, c == C - 1)
                elif own_kv:
                    tile = slice((half * HB + n) * P, (half * HB + n + 1) * P)
                    for c in range(C):
                        last = product(nc, bank, at(G.ctx, ALL, c, tile), at(wv, ALL, c), c == 0, c == C - 1)
                elif kind == "V":
                    toks = slice(half * HALF, (half + 1) * HALF)
                    for c in range(C):
                        last = product(nc, bank[0:dh, :], at(wv, ALL, c), at(sources[n], ALL, c, toks),
                                       c == 0, c == C - 1)
                else:
                    if A.rope:
                        pe.wait_ge(job_out, g * NV + value_no(half, "V", n) + 1)
                    else:
                        pe.wait_ge(job_out, g * JOBS + job_no(half, "V", n) + 1 + 2)
                    for b in range(HB):
                        last = nc.tensor.transpose(bank[:, b * dh:(b + 1) * dh],
                                                   values_turned[:, b * P:(b + 1) * P], G.ident[0:dh, 0:dh])
                last.then_inc(job_done, 1)

            def group(g):
                pe.wait_ge(w_ready, g * NP + N_QK)
                for half, kind, n in steps:
                    if kind in ("Q", "K", "V", "U"):
                        if (half, kind, n) == (0, "V", 0):
                            pe.wait_ge(w_ready, g * NP + N_QKV)
                        job(g, half, kind, n)
                    elif kind == "S":
                        i = head_no(half, n)
                        if A.rope:
                            pe.wait_ge(rotated_out, g * ROTATED + rotated_no(half, "Q", n) + 1 + 2)
                        else:
                            made = job_no(half, "K", n) if own_kv else job_no(half, "Q", n)
                            pe.wait_ge(job_out, g * JOBS + made + 1 + 2)
                        pe.wait_ge(score_free if A.mask else exp_done, g * HEADS + i + 1)
                        for b in range(HB):
                            col = slice(b * P, (b + 1) * P)
                            last = product(nc, score_bank(i, b), at(q, ALL, n % Q_RING, col),
                                           at(k, ALL, n % 2, col) if own_kv else at(k, ALL, b), True, True)
                        last.then_inc(scored, 1)
                    elif kind == "T":
                        i = head_no(half, n)
                        pe.wait_ge(turned_out, g * HEADS + i + 1)
                        pe.wait_ge(probs_ready, g * HEADS + i + 1)
                        if i == 0:
                            pe.wait_ge(norm.lo_done, B)
                        src = probs[:, i % P_RING, :].rearrange("p (b k) -> p b k", b=HB)
                        for s in range(NS):
                            for b in range(HB):
                                last = nc.tensor.transpose(G.ps[:, TURN + s, b * P:(b + 1) * P],
                                                           src[:, b, s * P:(s + 1) * P], G.ident[:])
                        last.then_inc(turned, 1)
                    elif kind == "A":
                        m = batch_no(half, n)
                        pe.wait_ge(heads_out, g * B + m + 1)
                        pe.wait_ge(turned_out, g * HEADS + NJ * (half + 1) + 1)
                        if own_kv or n == 0:
                            if A.rope:
                                pe.wait_ge(job_out, g * NV + value_no(half, "U", NS - 1) + 1)
                            else:
                                last_v = job_no(half, "V", n) if own_kv else job_no(half, "U", NS - 1)
                                pe.wait_ge(job_out, g * JOBS + last_v + 1 + 2)
                        bank = G.ps[0:dh, HEAD + m % HEAD_BANKS, :]
                        cols = slice(n * P, (n + 1) * P)
                        if own_kv:
                            for j in range(NJ):
                                last = product(nc, bank[:, j * P:(j + 1) * P],
                                               at(v, ALL, n % 2, slice(j * dh, (j + 1) * dh)),
                                               at(probsT, ALL, 0, j, cols), True, True)
                        else:
                            for s in range(NS):
                                last = product(nc, bank, at(v, ALL, s, slice(n * dh, (n + 1) * dh)),
                                               at(probsT, ALL, s, ALL, cols), s == 0, s == NS - 1)
                        last.then_inc(headed, 1)
                    elif kind == "O":
                        m = batch_no(half, n)
                        if m == 0:
                            pe.wait_ge(w_ready, g * NP + NP)
                        pe.wait_ge(heads_out, g * B + m + 1 + HEAD_BANKS)
                        pe.wait_ge(added, g * B + m + 1)
                        for j in range(NJ):
                            last = product(nc, G.ps[:, OUT, :],
                                           at(heads, ALL, m % HEAD_RING, slice(j * P, (j + 1) * P)),
                                           at(wo, ALL, j), j == 0, j == NJ - 1)
                        last.then_inc(projected, 1)

            with pe.Fori(0, NG) as g:
                group(g)

        def job_tiles(half, kind, n):
            bank = G.ps[:, PROJ + job_no(half, kind, n) % 2, :]
            if kind == "Q":
                return bank[0:dh, :], at(q, ALL, n % Q_RING)
            if kind == "K" and own_kv:
                return bank[0:dh, :], at(k, ALL, n % 2)
            if kind == "K":
                return bank[0:dh, :].rearrange("p (b t) -> p b t", b=HB), \
                    at(k, ALL, ALL, slice(n * P, (n + 1) * P))
            if own_kv:
                return bank, at(v, ALL, n % 2)
            if kind == "V":
                return bank[0:dh, :], (values_turned[:], None)
            return bank[:, 0:HB * dh], at(v, ALL, n)

        @block.scalar
        def _(a):
            if not A.mask:
                a.sem_inc(exp_done, 1)
            norm.scalar(a)

            def group(g, more):
                for half, kind, n in steps:
                    if kind in ("V", "U") or kind in ("Q", "K") and not A.rope:
                        m = job_no(half, kind, n)
                        src, (hi, _) = job_tiles(half, kind, n)
                        a.wait_ge(job_done, g * JOBS + m + 1)
                        nc.scalar.copy(hi, src).then_inc(job_hi, 1)
                    elif kind in ("HQ", "HK"):
                        m = rotated_no(half, kind[1], n)
                        hi, _, src = rotated_tiles(kind, n, m)
                        a.wait_ge(rotated, g * ROTATED + m + 1)
                        nc.scalar.copy(hi, src).then_inc(rotated_hi, 1)
                    elif kind == "W" and (more or n < NJ):
                        piece, place = split_piece(g, n)
                        hi, _, raw = piece_tiles(piece, slot_of(n))
                        arrived(a, g, n)
                        nc.scalar.copy(hi, raw).then_inc(w_hi, 1)
                    elif kind == "E":
                        i = head_no(half, n)
                        a.wait_ge(max_ready, g * HEADS + i + 1)
                        if not A.mask:
                            a.wait_ge(turned, g * HEADS + i + 1)
                        for b in range(HB):
                            dst = probs[:, i % P_RING, b * NK:(b + 1) * NK]
                            src = dst if A.mask else score_bank(i, b)
                            last = nc.scalar.activation(dst, src, ACT.Exp, bias=neg_max[:, n, b:b + 1],
                                                        scale=A.scale, accum_out=sums[:, n, b:b + 1])
                        last.then_inc(exp_done, 1)
                    elif kind == "T":
                        i = head_no(half, n)
                        a.wait_ge(turned, g * HEADS + i + 1 + P_RING)
                        nc.scalar.copy(probsT[0][:, :, n, :], G.ps[:, TURN:TURN + NS, :]).then_inc(turned_hi, 1)
                    elif kind == "A":
                        m = batch_no(half, n)
                        a.wait_ge(headed, g * B + m + 1)
                        a.wait_ge(projected, g * B + m + 1)
                        nc.scalar.copy(heads[0][:, m % HEAD_RING, :], G.ps[0:dh, HEAD + m % HEAD_BANKS, :]
                                       ).then_inc(heads_hi, 1)

            with a.Fori(0, NG - 1) as g:
                group(g, True)
            group(NG - 1, False)

        PER_HEAD = (2 if A.bias else 1 if A.mask else 0) + (A.scale != 1.0) + bool(A.bias)
        EXP_CREDIT = 0 if A.mask else 1

        @block.vector
        def _(dve):
            dve.sem_inc(bank_read if A.rope else job_out, 2)
            dve.sem_inc(score_free, SCORE_RING)
            dve.sem_inc(turned_out, 1)
            dve.sem_inc(heads_out, HEAD_BANKS)
            dve.sem_inc(added, 1)
            if A.mask:
                dve.wait_ge(mask_in, 16)
                nc.vector.tensor_scalar(mask_add[:], mask_raw.rearrange("p (b k) -> p b k", b=B), 0.0, MASKED,
                                        ALU.is_equal, ALU.mult).then_inc(start_used, 1)
                dve.wait_ge(start_used, 1)
            if A.bias:
                nc.vector.tensor_reduce(row_kept[:], mask_add[:], AX.X, ALU.max).then_inc(start_used, 1)
                dve.wait_ge(start_used, 2)
                nc.vector.tensor_scalar(row_kept[:], row_kept[:], 0.0, None, ALU.is_equal
                                        ).then_inc(start_used, 1)
                dve.wait_ge(start_used, 3)
                dve.wait_ge(tables, 16)
            norm.vector(dve)
            if A.bias:
                dve.wait_ge(norm.h_ready, B)
                dve.sem_inc(bias_free, 1)
            if A.rope:
                dve.wait_ge(tables, 32)

            def rotate(g, half, kind, n):
                m, by_tok, rows = rotated_no(half, kind, n), "p (b s) -> p b s", P // 2
                src = G.ps[:, PROJ + job_no(half, kind, n) % 2, :]
                dve.wait_ge(job_done, g * JOBS + job_no(half, kind, n) + 1)
                dve.wait_ge(rotated_out, g * ROTATED + m + 1)
                nc.vector.tensor_tensor(straight[:, m % 2, :].rearrange(by_tok, b=HB), src.rearrange(by_tok, b=HB),
                                        cos[:].unsqueeze(1).to_broadcast([P, HB, P]), ALU.mult)
                for to, of in ((0, rows), (rows, 0)):
                    last = nc.vector.tensor_tensor(
                        crossed[to:to + rows, m % 2, :].rearrange(by_tok, b=HB),
                        src[of:of + rows, :].rearrange(by_tok, b=HB),
                        sin[of:of + rows, :].unsqueeze(1).to_broadcast([rows, HB, P]), ALU.mult)
                last.then_inc(crossing, 1)
                dve.wait_ge(crossing, g * ROTATED + m + 1)
                dve.sem_inc(bank_read, 1)

            def group(g):
                done = [0]

                def step(ins):
                    done[0] += 1
                    ins.then_inc(soft, 1)
                    dve.wait_ge(soft, g * (HEADS * PER_HEAD) + done[0])

                for half, kind, n in steps:
                    if kind in ("Q", "K") and A.rope:
                        rotate(g, half, kind, n)
                    elif kind in ("Q", "K", "V", "U"):
                        src, (hi, lo) = job_tiles(half, kind, n)
                        m = g * NV + value_no(half, kind, n) if A.rope else g * JOBS + job_no(half, kind, n)
                        dve.wait_ge(job_hi, m + 1)
                        if lo is None:
                            if not A.rope:
                                dve.wait_ge(job_out, m + 2)
                            dve.sem_inc(job_out, 1)
                        else:
                            nc.vector.tensor_tensor(lo, src, hi.bitcast(F32), ALU.subtract).then_inc(job_out, 1)
                        if A.rope:
                            dve.wait_ge(job_out, m + 1)
                            dve.sem_inc(bank_read, 1)
                    elif kind == "S":
                        i = head_no(half, n)
                        dve.wait_ge(scored, g * HEADS + i + 1)
                        if A.mask:
                            dve.wait_ge(turned, g * HEADS + i + 1)
                            sc = G.ps[:, SCORE + i % 2, :].rearrange("p (b k) -> p b k", b=HB)
                            pj = probs[:, i % P_RING, :].rearrange("p (b k) -> p b k", b=HB)
                            madd = mask_add[:, half * HB:(half + 1) * HB, :]
                            if A.bias:
                                if i == 0:
                                    dve.wait_ge(bias_in, g * 16 + 16)
                                step(nc.vector.tensor_tensor(pj, sc, bias[:, n, :].unsqueeze(1).to_broadcast([P, HB, P]),
                                                             ALU.add))
                                dve.sem_inc(score_free, 1)
                                if i == HEADS - 1:
                                    dve.sem_inc(bias_free, 1)
                                step(nc.vector.tensor_tensor(pj, pj, madd, ALU.add))
                            else:
                                step(nc.vector.tensor_tensor(pj, sc, madd, ALU.add))
                                dve.sem_inc(score_free, 1)
                            src, dst = pj, neg_max[:, n, :]
                        else:
                            src = G.ps[:, SCORE:SCORE + NS, :].rearrange("p s (b k) -> p s b k", k=NK)
                            dst = neg_max[:, n, :].rearrange("p (s b) -> p s b", s=NS)
                        ins = nc.vector.tensor_reduce(dst, src, AX.X, ALU.max, negate=True)
                        if A.scale != 1.0:
                            step(ins)
                            ins = nc.vector.tensor_scalar(neg_max[:, n, :], neg_max[:, n, :], A.scale, None, ALU.mult)
                        ins.then_inc(max_ready, 1)
                    elif kind == "N":
                        i = head_no(half, n)
                        dve.wait_ge(exp_done, g * HEADS + i + 1 + EXP_CREDIT)
                        ins = nc.vector.reciprocal(recip[:, n, :], sums[:, n, :])
                        if A.bias:
                            step(ins)
                            ins = nc.vector.tensor_tensor(recip[:, n, :], recip[:, n, :],
                                                          row_kept[:, half * HB:(half + 1) * HB], ALU.mult)
                        ins.then_inc(recip_ready, 1)
                    elif kind == "T":
                        dve.wait_ge(turned_hi, g * HEADS + head_no(half, n) + 1)
                        nc.vector.tensor_tensor(probsT[1][:, :, n, :], G.ps[:, TURN:TURN + NS, :],
                                                probsT[0][:, :, n, :].bitcast(F32), ALU.subtract
                                                ).then_inc(turned_out, 1)
                    elif kind == "A":
                        m = batch_no(half, n)
                        dve.wait_ge(heads_hi, g * B + m + 1)
                        nc.vector.tensor_tensor(heads[1][:, m % HEAD_RING, :], G.ps[0:dh, HEAD + m % HEAD_BANKS, :],
                                                heads[0][:, m % HEAD_RING, :].bitcast(F32), ALU.subtract
                                                ).then_inc(heads_out, 1)
                    elif kind == "O":
                        m = batch_no(half, n)
                        dve.wait_ge(projected, g * B + m + 1 + HEAD_RING)
                        x = G.x[:, m, :]
                        nc.vector.tensor_tensor(x, x, G.ps[:, OUT, :], ALU.add).then_inc(added, 1)
                assert done[0] == HEADS * PER_HEAD

            if A.rope:
                dve.sem_inc(rotated_out, 2)
            with dve.Fori(0, NG) as g:
                group(g)


def swiglu_phase(nc, G, d):
    I2 = 2
    NG, NP, WIDE = d["glu_w"].shape[0], I2 + 1, 2 * D
    DOWN = I2
    PAIRS = I2 * 2
    OUTS = 4

    with ExitStack() as ctx:
        t = Tiles(nc, ctx, "glu")
        h = t.sb("h", [P, 4, D])
        stage, scales = t.sb("stage", [P, NP, WIDE]), t.sb("scales", [P, NP, WIDE])
        whole = t.sb("whole", [P, WIDE])
        w = t.pair("w", [P, NP, WIDE])
        gated = t.sb("gated", [P, 2, HALF])
        inner_f = t.sb("inner_f", [P, 2, HALF])
        inner = t.pair("inner", [P, I2, TOK])
        numbers_in = [t.sem(f"numbers_in{s}") for s in range(NP)]
        scales_in = [t.sem(f"scales_in{s}") for s in range(NP)]
        scaled, w_hi, w_ready = t.sem("scaled"), t.sem("w_hi"), t.sem("w_ready")
        gu_free = [t.sem(f"gu_free{i}") for i in range(I2)]
        gate_up, silu_done, pair_out = t.sem("gate_up"), t.sem("silu_done"), t.sem("pair_out")
        inner_hi, inner_out = t.sem("inner_hi"), t.sem("inner_out")
        projected, added = t.sem("projected"), t.sem("added")
        norm = Norm(t, G, h)
        block = ctx.enter_context(nc.Block())

        @block.sync
        def _(sp):
            with sp.Fori(0, NG) as g:
                for n in range(NP):
                    sp.wait_ge(scaled, g * NP + n + 1)
                    sp.dma_start(scales[:, n, :], d["glu_scale"][g, n].partition_broadcast(P)
                                 ).then_inc(scales_in[n], 16)

        @block.gpsimd
        def _(pool):
            def load(g, n):
                pool.dma_start(stage[:, n, :], d["glu_w"][g, n]).then_inc(numbers_in[n], 16)

            def turn(g, more):
                for n in range(NP):
                    m = g * NP + n
                    pool.wait_ge(numbers_in[n], g * 16 + 16)
                    pool.wait_ge(scales_in[n], g * 16 + 16)
                    if n == DOWN:
                        pool.wait_ge(added, g * B + OUTS)
                    else:
                        pool.wait_ge(gu_free[n], g + 1)
                    nc.gpsimd.tensor_tensor(w[0][:, n, :], stage[:, n, :], scales[:, n, :], ALU.mult).then_inc(w_hi, 1)
                    nc.gpsimd.tensor_tensor(whole[:], stage[:, n, :], scales[:, n, :], ALU.mult).then_inc(scaled, 1)
                    pool.wait_ge(scaled, m + NP + 1)
                    if more:
                        load(g + 1, n)
                    pool.wait_ge(w_hi, m + 1)
                    nc.gpsimd.tensor_tensor(w[1][:, n, :], whole[:], w[0][:, n, :].bitcast(F32), ALU.subtract
                                            ).then_inc(w_ready, 1)
                    pool.wait_ge(w_ready, m + 1)

            pool.sem_inc(scaled, NP)
            for n in range(NP):
                load(0, n)
            with pool.Fori(0, NG - 1) as g:
                turn(g, True)
            turn(NG - 1, False)

        @block.tensor
        def _(pe):
            for i in range(I2):
                pe.sem_inc(gu_free[i], 1)
            norm.tensor(pe)
            pe.wait_ge(norm.lo_done, B)
            with pe.Fori(0, NG) as g:
                for i in range(I2):
                    pe.wait_ge(w_ready, g * NP + i + 1)
                    for hf in range(2):
                        n = i * 2 + hf
                        pe.wait_ge(pair_out, g * PAIRS + n + 1)
                        for side in range(2):
                            for c in range(C):
                                last = product(nc, G.ps[:, 2 * (n % 2) + side, :],
                                               at(w, ALL, i, slice(side * D + c * P, side * D + (c + 1) * P)),
                                               at(G.xn, ALL, c, slice(hf * HALF, (hf + 1) * HALF)),
                                               c == 0, c == C - 1,
                                               gu_free[i - 1] if (n % 2, side, c) == (0, 0, 0) and i > 0 else None)
                        last.then_inc(gate_up, 1)
                pe.wait_ge(w_ready, g * NP + NP)
                for tile in range(B):
                    if tile % HB == 0:
                        pe.wait_ge(inner_out, g * PAIRS + PAIRS - 1 + tile // HB + 2)
                    pe.wait_ge(added, g * B + tile + 1)
                    for i in range(I2):
                        last = product(nc, G.ps[:, OUTS + tile % OUTS, :],
                                       at(inner, ALL, i, slice(tile * P, (tile + 1) * P)),
                                       at(w, ALL, DOWN, slice(i * D, (i + 1) * D)), i == 0, i == I2 - 1,
                                       gu_free[I2 - 1] if (tile, i) == (0, 0) else None)
                    last.then_inc(projected, 1)

        def inner_part(n):
            i, hf = n // 2, n % 2
            return at(inner, ALL, i, slice(hf * HALF, (hf + 1) * HALF))

        @block.scalar
        def _(a):
            norm.scalar(a)
            with a.Fori(0, NG) as g:
                for n in range(PAIRS + 1):
                    if n < PAIRS:
                        a.wait_ge(gate_up, g * PAIRS + n + 1)
                        nc.scalar.activation(gated[:, n % 2, :], G.ps[:, 2 * (n % 2), :], ACT.Silu
                                             ).then_inc(silu_done, 1)
                    if n > 0:
                        a.wait_ge(pair_out, g * PAIRS + n + 2)
                        nc.scalar.copy(inner_part(n - 1)[0], inner_f[:, (n - 1) % 2, :]).then_inc(inner_hi, 1)

        @block.vector
        def _(v):
            v.sem_inc(pair_out, 2)
            v.sem_inc(inner_out, 2)
            v.sem_inc(added, OUTS)
            norm.vector(v)
            with v.Fori(0, NG) as g:
                for n in range(PAIRS + 1):
                    if n < PAIRS:
                        v.wait_ge(inner_out, g * PAIRS + n + 1)
                        v.wait_ge(silu_done, g * PAIRS + n + 1)
                        nc.vector.tensor_tensor(inner_f[:, n % 2, :], gated[:, n % 2, :],
                                                G.ps[:, 2 * (n % 2) + 1, :], ALU.mult).then_inc(pair_out, 1)
                    if n > 0:
                        hi, lo = inner_part(n - 1)
                        v.wait_ge(inner_hi, g * PAIRS + n)
                        nc.vector.tensor_tensor(lo, inner_f[:, (n - 1) % 2, :], hi.bitcast(F32), ALU.subtract
                                                ).then_inc(inner_out, 1)
                for tile in range(B):
                    v.wait_ge(projected, g * B + tile + 1)
                    x = G.x[:, tile, :]
                    nc.vector.tensor_tensor(x, x, G.ps[:, OUTS + tile % OUTS, :], ALU.add).then_inc(added, 1)


def low_rank_phase(nc, G, d, name, rank, dense):
    RT = rank // P
    OUTS = 4
    with ExitStack() as ctx:
        t = Tiles(nc, ctx, name)
        h = t.sb("h", [P, 4, D])
        a, b = t.pair("a", [P, C, rank]), t.pair("b", [P, RT, D])
        parts = [("a", a, C * rank), ("b", b, RT * D)]
        if dense:
            w = t.pair("w", [P, C, D])
            parts.append(("w", w, C * D))
            bias = t.sb("bias", [P, D])
        raw = {k: t.sb(k + "_raw", [P, n]) for k, _, n in parts}
        factors = t.sb("factors", [P, 2, RT])
        weight = t.sb("weight", [P, RT])
        low_f, low = t.sb("low_f", [P, RT, TOK]), t.pair("low", [P, RT, TOK])
        part_in = {k: t.sem(k + "_in") for k, _, _ in parts}
        small_in, w_hi, w_ready = t.sem("small_in"), t.sem("w_hi"), t.sem("w_ready")
        weight_ready, low_done, low_scaled = t.sem("weight_ready"), t.sem("low_done"), t.sem("low_scaled")
        low_hi, low_out, projected, added = t.sem("low_hi"), t.sem("low_out"), t.sem("projected"), t.sem("added")
        norm = Norm(t, G, h)
        block = ctx.enter_context(nc.Block())
        pieces = [(k, pr, n, c) for k, pr, n in parts for c in range(n // 512)]
        halves = [(r, hf) for r in range(RT) for hf in range(2)]
        smalls = 3 if dense else 1

        @block.sync
        def _(sp):
            for k, _, n in parts:
                sp.dma_start(raw[k][:], d[f"{name}_{k}"]).then_inc(part_in[k], 16)
            sp.dma_start(factors[:, 0, :], d[f"{name}_factor0"]).then_inc(small_in, 16)
            if dense:
                sp.dma_start(factors[:, 1, :], d[f"{name}_factor1"]).then_inc(small_in, 16)
                sp.dma_start(bias[:], d[f"{name}_bias"].partition_broadcast(P)).then_inc(small_in, 16)

        @block.gpsimd
        def _(pool):
            for m, (k, pr, n, c) in enumerate(pieces):
                if c == 0:
                    pool.wait_ge(part_in[k], 16)
                cols = slice(c * 512, (c + 1) * 512)
                hi, lo = (x[:].rearrange("p a b -> p (a b)")[:, cols] for x in pr)
                rounded(nc, G, hi, raw[k][:, cols]).then_inc(w_hi, 1)
                pool.wait_ge(w_hi, m + 1)
                nc.gpsimd.tensor_tensor(lo, raw[k][:, cols], hi.bitcast(F32), ALU.subtract).then_inc(w_ready, 1)

        @block.tensor
        def _(pe):
            norm.tensor(pe)
            pe.wait_ge(norm.lo_done, B)
            pe.wait_ge(w_ready, C * rank // 512)
            for n, (r, hf) in enumerate(halves):
                for c in range(C):
                    last = product(nc, G.ps[:, n, :], at(a, ALL, c, slice(r * P, (r + 1) * P)),
                                   at(G.xn, ALL, c, slice(hf * HALF, (hf + 1) * HALF)), c == 0, c == C - 1)
                last.then_inc(low_done, 1)
            pe.wait_ge(w_ready, len(pieces))
            if not dense:
                pe.wait_ge(low_out, len(halves))
            for tile in range(B):
                toks = slice(tile * P, (tile + 1) * P)
                if tile >= OUTS:
                    pe.wait_ge(added, tile - OUTS + 1)
                if dense:
                    for c in range(C):
                        product(nc, G.ps[:, OUTS + tile % OUTS, :], at(G.xn, ALL, c, toks), at(w, ALL, c),
                                c == 0, False)
                    if tile == 0:
                        pe.wait_ge(low_out, len(halves))
                for r in range(RT):
                    last = product(nc, G.ps[:, OUTS + tile % OUTS, :], at(low, ALL, r, toks), at(b, ALL, r),
                                   r == 0 and not dense, r == RT - 1)
                last.then_inc(projected, 1)

        @block.scalar
        def _(act):
            norm.scalar(act)
            act.wait_ge(weight_ready, 1)
            for n, (r, hf) in enumerate(halves):
                toks = slice(hf * HALF, (hf + 1) * HALF)
                act.wait_ge(low_done, n + 1)
                nc.scalar.mul(low_f[:, r, toks], G.ps[:, n, :], weight[:, r:r + 1]).then_inc(low_scaled, 1)
                act.wait_ge(low_scaled, n + 1)
                nc.scalar.copy(low[0][:, r, toks], low_f[:, r, toks]).then_inc(low_hi, 1)

        @block.vector
        def _(v):
            v.wait_ge(small_in, 16 * smalls)
            if dense:
                nc.vector.tensor_tensor(weight[:], factors[:, 0, :], factors[:, 1, :], ALU.mult
                                        ).then_inc(weight_ready, 1)
            else:
                nc.vector.tensor_copy(weight[:], factors[:, 0, :]).then_inc(weight_ready, 1)
            norm.vector(v)
            for n, (r, hf) in enumerate(halves):
                toks = slice(hf * HALF, (hf + 1) * HALF)
                v.wait_ge(low_hi, n + 1)
                nc.vector.tensor_tensor(low[1][:, r, toks], low_f[:, r, toks], low[0][:, r, toks].bitcast(F32),
                                        ALU.subtract).then_inc(low_out, 1)
            for tile in range(B):
                x = G.x[:, tile, :]
                v.wait_ge(projected, tile + 1)
                nc.vector.tensor_tensor(x, x, G.ps[:, OUTS + tile % OUTS, :], ALU.add).then_inc(added, 1)
                if dense:
                    v.wait_ge(added, tile + 1)
                    nc.vector.tensor_tensor(x, x, bias[:], ALU.add)


def linear_attention_phase(nc, G, d):
    H, DH = 8, P // 8
    R2 = 2
    KTURN, QTURN, KV, QBACK, OUT = 0, 2, 4, 5, 6
    with ExitStack() as ctx:
        t = Tiles(nc, ctx, "lin")
        h = t.sb("h", [P, R2, D])
        k_raw, k_soft = t.sb("k_raw", [P, R2, D]), t.sb("k_soft", [P, R2, D])
        k_max, k_sum, k_rec = t.sb("k_max", [P, R2]), t.sb("k_sum", [P, R2]), t.sb("k_rec", [P, R2])
        kT = t.pair("kT", [P, R2, D])
        own_head = t.sb("own_head", [P, P])
        kv_f, kv = t.sb("kv_f", [P, R2, P]), t.pair("kv", [P, R2, P])
        q_max, q_sum = t.sb("q_max", [P, R2, C * H]), t.sb("q_sum", [P, R2, C * H])
        qT = t.sb("qT", [P, R2, D])
        q = t.pair("q", [P, R2, D])
        k_in = [t.sem(f"k_in{i}") for i in range(R2)]
        table_in = t.sem("table_in")
        names = ("k_step k_maxed k_exped k_ready k_turned kT_hi kT_out kv_done kv_masked kv_hi kv_out "
                 "h_ready q_turned q_step q_shifted q_exped q_ready q_back q_hi q_out out_done added").split()
        S = {n: t.sem(n) for n in names}
        norm = Norm(t, G, h)
        block = ctx.enter_context(nc.Block())
        by_head = "p (g e) -> p g e"

        def wide(small):
            return small.unsqueeze(2).to_broadcast([P, C * H, DH])

        @block.sync
        def _(sp):
            sp.dma_start(own_head[:], d["own_head"]).then_inc(table_in, 16)
            with sp.Fori(0, B // R2) as t2:
                for i in range(R2):
                    n = t2 * R2 + i
                    sp.wait_ge(S["k_exped"], n + 1)
                    sp.dma_start(k_raw[:, i, :], d["ctx"][n]).then_inc(k_in[i], 16)

        @block.vector
        def _(v):
            norm.vector_stats(v)
            v.wait_ge(table_in, 16)
            with v.Fori(0, B // R2) as t2:
                for i in range(R2):
                    n = t2 * R2 + i
                    v.wait_ge(k_in[i], t2 * 16 + 16)
                    nc.vector.tensor_reduce(k_max[:, i:i + 1], k_raw[:, i, :], AX.X, ALU.max, negate=True
                                            ).then_inc(S["k_maxed"], 1)
                    nc.vector.tensor_scalar(h[:, i, :], G.x[:, n, :], norm.mean_var[:, n, 0:1],
                                            norm.rstd[:, bass.ds(n, 1)], ALU.subtract, ALU.mult
                                            ).then_inc(S["h_ready"], 1)
                for i in range(R2):
                    n = t2 * R2 + i
                    v.wait_ge(S["q_turned"], n + 1)
                    bank = G.ps[:, QTURN + i, :].rearrange(by_head, e=DH)
                    nc.vector.tensor_reduce(q_max[:, i, :], bank, AX.X, ALU.max).then_inc(S["q_step"], 1)
                    v.wait_ge(S["q_step"], n * 3 + 1)
                    nc.vector.tensor_tensor(qT[:, i, :].rearrange(by_head, e=DH), bank, wide(q_max[:, i, :]),
                                            ALU.subtract).then_inc(S["q_shifted"], 1)
                    v.wait_ge(S["k_exped"], n + R2 + 1)
                    nc.vector.reciprocal(k_rec[:, i:i + 1], k_sum[:, i:i + 1]).then_inc(S["k_step"], 1)
                    v.wait_ge(S["k_step"], n + 1)
                    nc.vector.tensor_scalar(k_soft[:, i, :], k_soft[:, i, :], k_rec[:, i:i + 1], None, ALU.mult
                                            ).then_inc(S["k_ready"], 1)
                    v.wait_ge(S["q_exped"], n + 1)
                    nc.vector.tensor_reduce(q_sum[:, i, :], qT[:, i, :].rearrange(by_head, e=DH), AX.X, ALU.add
                                            ).then_inc(S["q_step"], 1)
                    v.wait_ge(S["q_step"], n * 3 + 2)
                    nc.vector.reciprocal(q_sum[:, i, :], q_sum[:, i, :]).then_inc(S["q_step"], 1)
                    v.wait_ge(S["q_step"], n * 3 + 3)
                    nc.vector.tensor_tensor(qT[:, i, :].rearrange(by_head, e=DH), qT[:, i, :].rearrange(by_head, e=DH),
                                            wide(q_sum[:, i, :]), ALU.mult).then_inc(S["q_ready"], 1)
                for i in range(R2):
                    n = t2 * R2 + i
                    v.wait_ge(S["kT_hi"], n + 1)
                    nc.vector.tensor_tensor(kT[1][:, i, :], G.ps[:, KTURN + i, :], kT[0][:, i, :].bitcast(F32),
                                            ALU.subtract).then_inc(S["kT_out"], 1)
                    v.wait_ge(S["kv_done"], n + 1)
                    nc.vector.tensor_tensor(kv_f[:, i, :], G.ps[:, KV, 0:P], own_head[:], ALU.mult
                                            ).then_inc(S["kv_masked"], 1)
                    v.wait_ge(S["q_hi"], n + 1)
                    nc.vector.tensor_tensor(q[1][:, i, :], G.ps[:, QBACK, :], q[0][:, i, :].bitcast(F32),
                                            ALU.subtract).then_inc(S["q_out"], 1)
                    v.wait_ge(S["kv_hi"], n + 1)
                    nc.vector.tensor_tensor(kv[1][:, i, :], kv_f[:, i, :], kv[0][:, i, :].bitcast(F32),
                                            ALU.subtract).then_inc(S["kv_out"], 1)
                    v.wait_ge(S["out_done"], n + 1)
                    x = G.x[:, n, :]
                    nc.vector.tensor_tensor(x, x, G.ps[:, OUT + i, :], ALU.add).then_inc(S["added"], 1)

        @block.scalar
        def _(a):
            a.sem_inc(S["k_exped"], R2)
            norm.scalar_roots(a)
            with a.Fori(0, B // R2) as t2:
                for i in range(R2):
                    n = t2 * R2 + i
                    a.wait_ge(S["k_maxed"], n + 1)
                    nc.scalar.activation(k_soft[:, i, :], k_raw[:, i, :], ACT.Exp, bias=k_max[:, i:i + 1],
                                         accum_out=k_sum[:, i:i + 1]).then_inc(S["k_exped"], 1)
                    a.wait_ge(S["q_shifted"], n + 1)
                    nc.scalar.activation(qT[:, i, :], qT[:, i, :], ACT.Exp).then_inc(S["q_exped"], 1)
                for i in range(R2):
                    n = t2 * R2 + i
                    a.wait_ge(S["k_turned"], n + 1)
                    nc.scalar.copy(kT[0][:, i, :], G.ps[:, KTURN + i, :]).then_inc(S["kT_hi"], 1)
                    a.wait_ge(S["q_back"], n + 1)
                    nc.scalar.copy(q[0][:, i, :], G.ps[:, QBACK, :]).then_inc(S["q_hi"], 1)
                    a.wait_ge(S["kv_masked"], n + 1)
                    nc.scalar.copy(kv[0][:, i, :], kv_f[:, i, :]).then_inc(S["kv_hi"], 1)

        @block.tensor
        def _(pe):
            def turn(bank, src):
                for c in range(C):
                    last = nc.tensor.transpose(G.ps[:, bank, c * P:(c + 1) * P], src[:, c * P:(c + 1) * P], G.ident[:])
                return last

            with pe.Fori(0, B // R2) as t2:
                for i in range(R2):
                    n = t2 * R2 + i
                    pe.wait_ge(S["h_ready"], n + 1)
                    turn(QTURN + i, h[:, i, :]).then_inc(S["q_turned"], 1)
                for i in range(R2):
                    n = t2 * R2 + i
                    pe.wait_ge(S["k_ready"], n + 1)
                    turn(KTURN + i, k_soft[:, i, :]).then_inc(S["k_turned"], 1)
                for i in range(R2):
                    n = t2 * R2 + i
                    pe.wait_ge(S["q_ready"], n + 1)
                    turn(QBACK, qT[:, i, :]).then_inc(S["q_back"], 1)
                    pe.wait_ge(S["kT_out"], n + 1)
                    for c in range(C):
                        chunk = slice(c * P, (c + 1) * P)
                        last = product(nc, G.ps[:, KV, 0:P], at(kT, ALL, i, chunk),
                                       (G.ctx[0][:, c, bass.ds(n * P, P)], G.ctx[1][:, c, bass.ds(n * P, P)]),
                                       c == 0, c == C - 1)
                    last.then_inc(S["kv_done"], 1)
                    pe.wait_ge(S["kv_out"], n + 1)
                    pe.wait_ge(S["q_out"], n + 1)
                    product(nc, G.ps[:, OUT + i, :], at(kv, ALL, i), at(q, ALL, i), True, True
                            ).then_inc(S["out_done"], 1)


def experts_phase(nc, G, d, out):
    E = d["experts"].shape[0]
    E2 = 2
    NP = E2 * C
    STAGES = 4
    with ExitStack() as ctx:
        t = Tiles(nc, ctx, "moe")
        h = t.sb("h", [P, 4, D])
        stage = t.sb("stage", [P, STAGES, D])
        w = t.pair("w", [P, E2, C * D])
        gate_raw, gate = t.sb("gate_raw", [P, C, E]), t.pair("gate", [P, C, E])
        numbers = t.sb("numbers", [P, E])
        logits = t.sb("logits", [P, B, E])
        top, top_at = t.sb("top", [P, B, 8]), t.sb("top_at", [P, B, 8], U32)
        top_no = t.sb("top_no", [P, B, 8])
        chosen = t.sb("chosen", [P, 2, B, E])
        share = t.sb("share", [P, 3, B])
        per_expert = t.sb("per_expert", [P, E, B])
        staged = [t.sem(f"staged{s}") for s in range(STAGES)]
        stage_free, w_hi, w_ready, w_free = t.sem("stage_free"), t.sem("w_hi"), t.sem("w_ready"), t.sem("w_free")
        small_in, gate_split = t.sem("small_in"), t.sem("gate_split")
        logits_done, route, exp_in, exp_done = t.sem("logits_done"), t.sem("route"), t.sem("exp_in"), t.sem("exp_done")
        projected, added, stored = t.sem("projected"), t.sem("added"), t.sem("stored")
        norm = Norm(t, G, h)
        block = ctx.enter_context(nc.Block())

        @block.sync
        def _(sp):
            sp.dma_start(gate_raw[:], d["gate_w"]).then_inc(small_in, 16)
            sp.dma_start(numbers[:], d["numbers"].partition_broadcast(P)).then_inc(small_in, 16)
            with sp.Fori(0, E // E2) as g:
                for n in range(NP):
                    sp.wait_ge(stage_free, g * NP + n + 1)
                    sp.dma_start(stage[:, n % STAGES, :], d["experts"][g * E2 + n // C, n % C]
                                 ).then_inc(staged[n % STAGES], 16)
            for tile in range(B):
                sp.wait_ge(added, E * B + tile + 1)
                sp.dma_start(out[tile], G.x[:, tile, :]).then_inc(stored, 16)
            sp.wait_ge(stored, 16 * B)

        @block.gpsimd
        def _(pool):
            pool.sem_inc(stage_free, STAGES)
            pool.wait_ge(small_in, 32)
            nc.gpsimd.tensor_copy(gate[0][:], gate_raw[:]).then_inc(gate_split, 1)
            pool.wait_ge(gate_split, 1)
            nc.gpsimd.tensor_tensor(gate[1][:], gate_raw[:], gate[0][:].bitcast(F32), ALU.subtract
                                    ).then_inc(gate_split, 1)
            with pool.Fori(0, E // E2) as g:
                for n in range(NP):
                    turn = g * (NP // STAGES) + n // STAGES
                    e, c = n // C, n % C
                    cols = slice(c * D, (c + 1) * D)
                    if c == 0:
                        pool.wait_ge(w_free, g * E2 + e + 1)
                    pool.wait_ge(staged[n % STAGES], turn * 16 + 16)
                    src = stage[:, n % STAGES, :]
                    rounded(nc, G, w[0][:, e, cols], src).then_inc(w_hi, 1)
                    pool.wait_ge(w_hi, g * NP + n + 1)
                    nc.gpsimd.tensor_tensor(w[1][:, e, cols], src, w[0][:, e, cols].bitcast(F32), ALU.subtract
                                            ).then_inc(w_ready, 1)
                    pool.wait_ge(w_ready, g * NP + n + 1)
                    pool.sem_inc(stage_free, 1)

        @block.tensor
        def _(pe):
            pe.sem_inc(w_free, 1)
            norm.tensor(pe)
            pe.wait_ge(norm.lo_done, B)
            pe.wait_ge(gate_split, 2)
            for tile in range(B):
                for c in range(C):
                    last = product(nc, G.ps[:, B - 1, tile * E:(tile + 1) * E],
                                   at(G.xn, ALL, c, slice(tile * P, (tile + 1) * P)), at(gate, ALL, c),
                                   c == 0, c == C - 1)
            last.then_inc(logits_done, 1)
            with pe.Fori(0, E // E2) as g:
                for e in range(E2):
                    pe.wait_ge(w_ready, g * NP + (e + 1) * C)
                    for tile in range(B):
                        pe.wait_ge(added, g * (E2 * B) + e * B + tile + 1)
                        for c in range(C):
                            last = product(nc, G.ps[:, tile, :], at(G.xn, ALL, c, slice(tile * P, (tile + 1) * P)),
                                           at(w, ALL, e, slice(c * D, (c + 1) * D)), c == 0, c == C - 1,
                                           w_free if tile == 0 and c == 0 else None)
                        last.then_inc(projected, 1)

        @block.scalar
        def _(a):
            norm.scalar(a)
            a.wait_ge(exp_in, 1)
            nc.scalar.activation(share[:, 1, :], share[:, 0, :], ACT.Exp).then_inc(exp_done, 1)

        @block.vector
        def _(v):
            norm.vector(v)
            done = [0]

            def step(ins):
                done[0] += 1
                ins.then_inc(route, 1)
                v.wait_ge(route, done[0])

            v.wait_ge(logits_done, 1)
            v.wait_ge(small_in, 32)
            step(nc.vector.tensor_copy(logits[:], G.ps[:, B - 1, 0:B * E].rearrange("p (t e) -> p t e", t=B)))
            v.sem_inc(added, B)
            for tile in range(B):
                last = nc.vector.max(top[:, tile, :], logits[:, tile, :])
            step(last)
            for tile in range(B):
                last = nc.vector.max_index(top_at[:, tile, :], top[:, tile, :], logits[:, tile, :])
            step(last)
            step(nc.vector.tensor_copy(top_no[:], top_at[:]))
            nc.vector.tensor_tensor(share[:, 0, :], top[:, :, 1], top[:, :, 0], ALU.subtract).then_inc(exp_in, 1)
            v.wait_ge(exp_done, 1)
            step(nc.vector.tensor_scalar(share[:, 0, :], share[:, 1, :], 1.0, None, ALU.add))
            step(nc.vector.reciprocal(share[:, 2, :], share[:, 0, :]))
            step(nc.vector.tensor_tensor(share[:, 1, :], share[:, 1, :], share[:, 2, :], ALU.mult))
            for rank, s in ((0, 2), (1, 1)):
                step(nc.vector.tensor_tensor(chosen[:, rank], numbers[:].unsqueeze(1).to_broadcast([P, B, E]),
                                             top_no[:, :, rank].unsqueeze(2).to_broadcast([P, B, E]), ALU.is_equal))
                step(nc.vector.tensor_tensor(chosen[:, rank], chosen[:, rank],
                                             share[:, s, :].unsqueeze(2).to_broadcast([P, B, E]), ALU.mult))
            step(nc.vector.tensor_tensor(per_expert[:].rearrange("p e t -> p t e"), chosen[:, 0], chosen[:, 1], ALU.add))
            with v.Fori(0, E) as e:
                for tile in range(B):
                    x = G.x[:, tile, :]
                    v.wait_ge(projected, e * B + tile + 1)
                    nc.vector.scalar_tensor_tensor(out=x, in0=G.ps[:, tile, :],
                                                   scalar=per_expert[:, e, tile:tile + 1], in1=x,
                                                   op0=ALU.mult, op1=ALU.add).then_inc(added, 1)


L0 = Attention(
    "l0", groups=8, dh=128, shared_kv=False, on_latents=False, scale=1.0, bias=True, mask="bool", rope=False,
    order="aV0 aQ0 aK0 aQ1 W0 aS0 aK1 aE0 aQ2 aN0 W1 aK2 aS1 aE1 aQ3 W2 aS2 aT0 bQ0 aN1 aK3 aE2 aT1 aN2 aS3 "
          "bK0 bQ1 aE3 aN3 aT2 bS0 W3 aV1 aT3 bK1 aA0 bQ2 bS1 bE0 aO0 bN0 aA1 aV2 aV3 aA2 aO1 bK2 bQ3 W4 bE1 "
          "bS2 W5 W6 W7 bN1 aA3 bT0 aO2 bE2 bK3 bN2 bT1 bS3 W8 bE3 aO3 bN3 bT2 bV0 bT3 bV1 bA0 W9 bA1 W10 bO0 "
          "bV2 bO1 W11 bA2 bV3 W12 W13 bO2 W14 bA3 bO3 W15")
L1 = Attention(
    "l1", groups=4, dh=96, shared_kv=True, on_latents=True, scale=float(1 / np.sqrt(np.float32(96))),
    bias=False, mask=None, rope=False,
    order="aK0 aK1 aQ0 aV0 aS0 aE0 aN0 aQ1 W0 aQ2 aS1 aT0 aE1 aN1 aQ3 aS2 aE2 aU0 aN2 aV1 aT1 aS3 bK0 W1 bK1 "
          "aE3 aT2 aN3 W2 bQ0 bQ1 W3 bS0 aU1 aT3 bE0 bQ2 bN0 aA0 bS1 bE1 aA1 aO0 bS2 aA2 aO1 aA3 bN1 bE2 bT0 "
          "bQ3 bN2 W4 W5 bV0 bS3 bT1 bE3 bU0 bV1 bN3 bT2 aO2 W6 bU1 bT3 aO3 bA0 W7 bA1 bO0 bA2 bO1 W8 W9 bA3 "
          "bO2 bO3")
L3 = Attention(
    "l3", groups=8, dh=128, shared_kv=True, on_latents=False, scale=float(1 / np.sqrt(np.float32(128))),
    bias=False, mask="float", rope=True,
    order="aK0 aHK0 aQ0 aHQ0 aQ1 aHQ1 aQ2 aHQ2 aS0 aE0 aQ3 aS1 aHQ3 aN0 aV0 W0 W1 aE1 aS2 aU0 aN1 aS3 aE2 aN2 "
          "aT0 W2 bK0 bQ0 aE3 aN3 aT1 bHK0 W3 bV0 aT2 bHQ0 bQ1 aT3 bHQ1 bQ2 aA0 aA1 bS0 bS1 bE0 bHQ2 bQ3 bHQ3 "
          "bE1 aO0 bS2 bN0 bE2 aO1 bN1 bN2 aA2 aA3 bT0 bS3 W4 bT1 bE3 bN3 aO2 bT2 bU0 W5 W6 bT3 aO3 bA0 W7 "
          "bA1 bO0 bA2 W8 bO1 W9 bA3 bO2 bO3")


PHASES = [
    lambda nc, G, d, out: attention_phase(nc, G, d, L0),
    lambda nc, G, d, out: swiglu_phase(nc, G, d),
    lambda nc, G, d, out: attention_phase(nc, G, d, L1),
    lambda nc, G, d, out: low_rank_phase(nc, G, d, "lora", 256, True),
    lambda nc, G, d, out: linear_attention_phase(nc, G, d),
    lambda nc, G, d, out: low_rank_phase(nc, G, d, "svd", 128, False),
    lambda nc, G, d, out: attention_phase(nc, G, d, L3),
    lambda nc, G, d, out: experts_phase(nc, G, d, out),
]


def build_program(nc, d, out):
    with ExitStack() as ctx:
        t = Tiles(nc, ctx, "all")
        G = Globals()
        G.x = t.sb("x", [P, B, D])
        G.ctx = t.pair("ctx", [P, C, TOK])
        G.xn = t.pair("xn", [P, C, TOK])
        G.ident = t.sb("ident", [P, P])
        G.zero = t.sb("zero", [P, 1])
        G.ps = ctx.enter_context(nc.psum_tensor("ps", [P, 8, 512], F32))
        load_phase(nc, G, d)
        for phase in PHASES:
            phase(nc, G, d, out)


def laid_out(i):
    def rows(w, groups, width, parts):
        return w.reshape(groups, width, parts, -1).transpose(0, 2, 3, 1)

    def fused(w, groups, width):
        return w.reshape(groups, width, C, P).transpose(0, 3, 2, 1)

    def glu_pieces(gate, up, down):
        gu = np.concatenate([gate, up], 2).reshape(7, 2, -1, 2 * D)
        return np.concatenate([gu, np.concatenate([down[0::2], down[1::2]], 2)[:, None]], 1)

    a = {
        "x": i["x"], "ctx": i["ctx_4096"],
        "ctxT": i["ctx_4096"].reshape(TOK, C, P).transpose(1, 2, 0),
        "ident": np.eye(P, dtype=np.float32),
        "l0_mask": i["mask_BxSxS2_bk0"].view(np.int32),
        "bias": i["L0_xattn_position_bias"].reshape(8, 4, P, P).transpose(0, 2, 1, 3),
        "ln_w": i["L0_xattn_ln_weight"],
        "l0_wq": rows(i["L0_xattn_w_q"], 8, 512, C), "l0_wk": rows(i["L0_xattn_w_k"], 8, 512, C),
        "l0_wv": rows(i["L0_xattn_w_v"], 8, 512, C),
        "l0_wo": i["L0_xattn_w_out"].T.reshape(8, 4, P, D),
        "glu_w": glu_pieces(fused(i["L0_ffn_gate_q"], 14, P).reshape(14, P, D),
                            fused(i["L0_ffn_up_q"], 14, P).reshape(14, P, D),
                            i["L0_ffn_down_q"].T.reshape(14, P, D)),
        "glu_scale": glu_pieces(i["L0_ffn_gate_s"].reshape(14, P, C).transpose(0, 2, 1).reshape(14, 1, D),
                                i["L0_ffn_up_s"].reshape(14, P, C).transpose(0, 2, 1).reshape(14, 1, D),
                                i["L0_ffn_down_s"].T.reshape(14, 1, D))[:, :, 0, :],
        "l1_wq": rows(i["L1_xattn_Wq"], 4, 384, C), "l1_wk": fused(i["L1_xattn_Wk"], 4, 96),
        "l1_wv": fused(i["L1_xattn_Wv"], 4, 96), "l1_wo": i["L1_xattn_Wo"].T.reshape(4, 4, 96, D),
        "lora_w": fused(i["L1_ffn_W"], 1, D).reshape(P, C * D), "lora_bias": i["L1_ffn_bias"],
        "lora_a": fused(i["L1_ffn_A"].reshape(256, D), 1, 256).reshape(P, C * 256),
        "lora_b": i["L1_ffn_Bf"].transpose(0, 2, 1).reshape(2, P, D).transpose(1, 0, 2).reshape(P, 2 * D),
        "lora_factor0": np.repeat(i["L1_ffn_coeffs"], 16).reshape(2, P).T,
        "lora_factor1": np.repeat(i["L1_ffn_scales"], 16).reshape(2, P).T,
        "own_head": np.kron(np.eye(8), np.ones((16, 16))).astype(np.float32),
        "svd_a": i["L2_ffn_V"].reshape(C, P, P).transpose(1, 0, 2).reshape(P, C * P),
        "svd_b": i["L2_ffn_U"].T, "svd_factor0": i["L2_ffn_S"].reshape(P, 1),
        "l3_mask": i["mask_BxSxS2_ff1"],
        "l3_wq": i["L3_xattn_wq"].reshape(C, P, 8, 512).transpose(2, 0, 1, 3),
        "l3_wk": i["L3_xattn_wk"].reshape(C, P, 8, P).transpose(2, 1, 0, 3),
        "l3_wv": i["L3_xattn_wv"].reshape(C, P, 8, P).transpose(2, 1, 0, 3),
        "l3_wo": i["L3_xattn_wo"].reshape(8, 4, P, D),
        "gate_w": i["L3_ffn_gate_w"].reshape(C, P, 8).transpose(1, 0, 2),
        "experts": i["L3_ffn_expert_w"].reshape(8, C, P, D),
        "numbers": np.arange(8, dtype=np.float32),
    }
    rate = (np.float32(1.0) / np.float32(10000.0) ** (np.arange(0, P, 2, dtype=np.float32) / np.float32(P)))
    angle = np.arange(P, dtype=np.float32)[:, None] * rate[None, :].astype(np.float32)
    a["cos"] = np.concatenate([np.cos(angle), np.cos(angle)], 1).T
    a["sin"] = np.concatenate([np.sin(angle), -np.sin(angle)], 1).T
    return {k: np.ascontiguousarray(v) for k, v in a.items()}


def kernel(**inputs):
    import concourse.bacc as bacc
    from concourse.bass_utils import run_bass_kernel_spmd

    nc = bacc.Bacc("TRN2", target_bir_lowering=False, num_devices=1)
    arrays = laid_out({k: np.asarray(v) for k, v in inputs.items()})
    d = {k: nc.dram_tensor("in_" + k, v.shape, mybir.dt.from_np(v.dtype), kind="ExternalInput").ap()
         for k, v in arrays.items()}
    out = nc.dram_tensor("out", (B, P, D), F32, kind="ExternalOutput").ap()
    build_program(nc, d, out)
    got = run_bass_kernel_spmd(nc, [{"in_" + k: v for k, v in arrays.items()}], core_ids=[0])
    return got.results[0]["out"]
```

```python
from contextlib import ExitStack

import numpy as np

import concourse.bass as bass
from concourse import mybir

F32, F32R = mybir.dt.float32, mybir.dt.float32r
BF16, I32, U32, U8 = mybir.dt.bfloat16, mybir.dt.int32, mybir.dt.uint32, mybir.dt.uint8
ALU, ACT, AX = mybir.AluOpType, mybir.ActivationFunctionType, mybir.AxisListType

P = 128
B = 8
D = 512
C = D // P
TOK = B * P
HALF = TOK // 2
HB = B // 2
EPS = 1e-5
MASKED = -1e30


class Tiles:

    def __init__(self, nc, ctx, name):
        self.nc, self.ctx, self.name, self.sems = nc, ctx, name, []
        ctx.callback(self.clear)

    def clear(self):
        if self.sems:
            self.nc.clear_and_free_semaphores(self.sems)
            self.nc.all_engine_barrier()

    def sb(self, name, shape, dt=F32):
        return self.ctx.enter_context(self.nc.sbuf_tensor(f"{self.name}_{name}", shape, dt))

    def pair(self, name, shape):
        return self.sb(name + "_hi", shape, F32R), self.sb(name + "_lo", shape, F32R)

    def sem(self, name):
        self.sems.append(self.nc.alloc_semaphore(f"{self.name}_{name}"))
        return self.sems[-1]


def product(nc, out, wt, x, first, last, begun=None):
    (wh, wl), (xh, xl) = wt, x
    ins = nc.tensor.matmul(out, wh, xh, start=first, stop=False)
    if begun is not None:
        ins.then_inc(begun, 1)
    nc.tensor.matmul(out, wl, xh, start=False, stop=False)
    return nc.tensor.matmul(out, wh, xl, start=False, stop=last)


def rounded(nc, G, hi, x):
    zero = G.zero[0:x.shape[0]]
    for size in x.shape[2:]:
        zero = zero.unsqueeze(1)
    return nc.gpsimd.tensor_tensor(hi, x, zero.to_broadcast(list(x.shape)), ALU.add)


def at(pair, *index):
    return pair[0][index], pair[1][index]


ALL = slice(None)


def tile_stats(nc, G, tile):
    return nc.vector.bn_stats(G.stats[:, tile, :], G.x[:, tile, :])


class Norm:

    def __init__(self, t, G, h, rms_weight=None):
        self.SLOTS = h.shape[1]
        self.nc, self.G, self.h, self.rms_weight = t.nc, G, h, rms_weight
        self.mean_var = t.sb("ln_mean_var", [P, B, 2])
        self.var_eps = t.sb("ln_var_eps", [P, B])
        self.root = t.sb("ln_root", [P, B])
        self.rstd = t.sb("ln_rstd", [P, B])
        self.shift = t.sb("ln_shift", [P, B])
        self.rrms = t.sb("ln_rrms", [P, B])
        self.small = t.sem("ln_small")
        self.moments = t.sem("ln_moments")
        self.rooted = t.sem("ln_rooted")
        self.scaling = t.sem("ln_scaling")
        self.SHARE = 2 if rms_weight is None else 1
        self.h_made = [t.sem(f"ln_h_made{i}") for i in range(self.SHARE)]
        self.x_taken = t.sem("ln_x_taken")
        self.h_ready = self.h_made if rms_weight is None else [t.sem("ln_h_ready")]
        self.turned = t.sem("ln_turned")
        self.hi_done = t.sem("ln_hi_done")
        self.lo_done = t.sem("ln_lo_done")

    def vector(self, v):
        nc, G, h = self.nc, self.G, self.h
        self.vector_moments(v)

        def rms(tile):
            i = tile % self.SLOTS
            v.wait_ge(self.h_made[0], tile + 1)
            nc.vector.tensor_tensor(G.x[:, tile, :], G.x[:, tile, :], h[:, i, :], ALU.add
                                    ).then_inc(self.x_taken, 1)
            v.wait_ge(self.x_taken, tile + 1)
            nc.vector.scalar_tensor_tensor(out=h[:, i, :], in0=h[:, i, :], scalar=self.rrms[:, tile:tile + 1],
                                           in1=self.rms_weight, op0=ALU.mult, op1=ALU.mult
                                           ).then_inc(self.h_ready[0], 1)

        def normed(tile):
            nc.vector.tensor_scalar(h[:, tile % self.SLOTS, :], G.x[:, tile, :], self.mean_var[:, tile, 0:1],
                                    self.rstd[:, tile:tile + 1], ALU.subtract, ALU.mult
                                    ).then_inc(self.h_made[1], 1)

        if self.rms_weight is not None:
            rms(0)
        else:
            for tile in range(1, self.SLOTS, 2):
                normed(tile)
        for tile in range(B):
            if self.rms_weight is not None:
                if tile + 1 < B:
                    rms(tile + 1)
            elif tile % 2 == 1 and tile + self.SLOTS < B:
                v.wait_ge(self.turned, tile + 1)
                normed(tile + self.SLOTS)
            cols = slice(tile * P, (tile + 1) * P)
            v.wait_ge(self.hi_done, tile + 1)
            nc.vector.tensor_tensor(
                G.xn[1][:, :, cols], G.ps[:, tile, :].rearrange("p (c t) -> p c t", c=C),
                G.xn[0][:, :, cols].bitcast(F32), ALU.subtract).then_inc(self.lo_done, 1)

    def vector_moments(self, v):
        nc, G = self.nc, self.G
        for i in range(B):
            nc.vector.bn_aggr(self.mean_var[:, i, :], G.stats[:, i, :]).then_inc(self.small, 1)
        v.wait_ge(self.small, B)
        mean, var = self.mean_var[:, :, 0], self.mean_var[:, :, 1]
        nc.vector.tensor_scalar(self.var_eps[:], var, EPS, None, ALU.add).then_inc(self.moments, 1)
        v.wait_ge(self.rooted, 1)
        nc.vector.reciprocal(self.rstd[:], self.root[:]).then_inc(self.small, 1)
        v.wait_ge(self.small, B + 1)
        nc.vector.scalar_tensor_tensor(out=self.shift[:], in0=mean, scalar=-1.0, in1=self.rstd[:],
                                       op0=ALU.mult, op1=ALU.mult).then_inc(self.scaling, 1)
        if self.rms_weight is not None:
            nc.vector.tensor_tensor(self.rrms[:], var, self.rstd[:], ALU.mult).then_inc(self.small, 1)
            v.wait_ge(self.small, B + 2)
            nc.vector.tensor_tensor(self.rrms[:], self.rrms[:], self.rstd[:], ALU.mult).then_inc(self.small, 1)
            v.wait_ge(self.small, B + 3)
            nc.vector.tensor_scalar(self.var_eps[:], self.rrms[:], EPS, None, ALU.add
                                    ).then_inc(self.moments, 1)
            v.wait_ge(self.rooted, 2)
            nc.vector.reciprocal(self.rrms[:], self.root[:]).then_inc(self.small, 1)
            v.wait_ge(self.small, B + 4)

    def scalar(self, a):
        nc, G = self.nc, self.G
        self.scalar_roots(a)
        a.wait_ge(self.scaling, 1)

        def normed(tile):
            nc.scalar.activation(self.h[:, tile % self.SLOTS, :], G.x[:, tile, :], ACT.Identity,
                                 bias=self.shift[:, tile:tile + 1], scale=self.rstd[:, tile:tile + 1]
                                 ).then_inc(self.h_made[0], 1)

        for tile in range(0, self.SLOTS, self.SHARE):
            normed(tile)
        for tile in range(B):
            a.wait_ge(self.turned, tile + 1)
            if tile % self.SHARE == 0 and tile + self.SLOTS < B:
                normed(tile + self.SLOTS)
            cols = slice(tile * P, (tile + 1) * P)
            nc.scalar.copy(G.xn[0][:, :, cols], G.ps[:, tile, :].rearrange("p (c t) -> p c t", c=C)
                           ).then_inc(self.hi_done, 1)

    def scalar_roots(self, a):
        nc = self.nc
        for k in range(1 if self.rms_weight is None else 2):
            a.wait_ge(self.moments, k + 1)
            nc.scalar.activation(self.root[:], self.var_eps[:], ACT.Sqrt).then_inc(self.rooted, 1)

    def tensor(self, pe):
        for i in range(B):
            ready = self.h_ready
            pe.wait_ge(ready[i % len(ready)], i // len(ready) + 1)
            for c in range(C):
                last = self.nc.tensor.transpose(self.G.ps[:, i, c * P:(c + 1) * P],
                                                self.h[:, i % self.SLOTS, c * P:(c + 1) * P],
                                                self.G.ident[:])
            last.then_inc(self.turned, 1)


class Globals:
    pass


def load_phase(nc, G, d):
    with ExitStack() as ctx:
        t = Tiles(nc, ctx, "load")
        raw = t.sb("ctx_raw", [P, C, TOK])
        x_in, ident_in = t.sem("x_in"), t.sem("ident_in")
        ctx_in = [t.sem(f"ctx_in{c}") for c in range(C)]
        hi_done = t.sem("hi_done")
        block = ctx.enter_context(nc.Block())

        @block.sync
        def _(sp):
            sp.dma_start(G.x[:], d["x"].rearrange("b p d -> p b d")).then_inc(x_in, 16)
            for c in range(C):
                sp.dma_start(raw[:, c, :], d["ctxT"][c]).then_inc(ctx_in[c], 16)
            sp.dma_start(G.ident[:], d["ident"]).then_inc(ident_in, 16)
            sp.wait_ge(ident_in, 16)

        @block.gpsimd
        def _(pool):
            nc.gpsimd.memset(G.zero[:], 0.0)

        @block.scalar
        def _(a):
            for c in range(C):
                a.wait_ge(ctx_in[c], 16)
                nc.scalar.copy(G.ctx[0][:, c, :], raw[:, c, :]).then_inc(hi_done, 1)

        @block.vector
        def _(v):
            v.wait_ge(x_in, 16)
            for tile in range(B):
                tile_stats(nc, G, tile)
            for c in range(C):
                v.wait_ge(hi_done, c + 1)
                nc.vector.tensor_tensor(G.ctx[1][:, c, :], raw[:, c, :],
                                        G.ctx[0][:, c, :].bitcast(F32), ALU.subtract)


class Attention:

    def __init__(self, name, groups, dh, shared_kv, on_latents, scale, bias, mask, rope, order):
        self.name, self.groups, self.dh, self.shared_kv = name, groups, dh, shared_kv
        self.on_latents, self.scale, self.bias, self.mask, self.rope = on_latents, scale, bias, mask, rope
        self.steps = []
        for word in order.split():
            half = 0 if word[0] == "a" else 1
            name = word if word[0] == "W" else word[1:]
            kind = name.rstrip("0123456789")
            self.steps.append((half, kind, int(name[len(kind):])))

    def index(self, half, kind, n, kinds):
        return [s for s in self.steps if s[1] in kinds].index((half, kind, n))


def attention_phase(nc, G, d, A):
    NJ, dh, NG, steps = 4, A.dh, A.groups, A.steps
    QW = NJ * dh
    sources = [G.ctx] + ([G.xn] if A.on_latents else [])
    NS = len(sources)
    NK = NS * P
    own_kv = not A.shared_kv
    HEADS = 2 * NJ
    JOBS = sum(s[1] in ("Q", "K", "V", "U") for s in steps)
    ROTATED = sum(s[1] in ("Q", "K") for s in steps)
    NV = sum(s[1] in ("V", "U") for s in steps)
    assert JOBS % 2 == 0
    Q_RING = 4 if A.rope else 2
    P_RING = 2 if NS == 2 or own_kv else 4
    HEAD_BANKS = 2 if NS == 1 else 1
    HEAD_RING = 2
    PROJ, SCORE, TURN, OUT = 0, 2, 4, 7
    HEAD = TURN + NS
    SCORE_RING = 2 // NS

    with ExitStack() as ctx:
        t = Tiles(nc, ctx, A.name)
        KW = QW if own_kv else dh
        wq, wk, wv = t.pair("wq", [P, C, QW]), t.pair("wk", [P, C, KW]), t.pair("wv", [P, C, KW])
        wo = t.pair("wo", [dh, NJ, D])
        pieces = [("wq", wq, c) for c in range(C)]
        pieces += [("wk", wk, c) for c in range(C)] if own_kv else [("wk", wk, None)]
        N_QK = len(pieces)
        pieces += [("wv", wv, c) for c in range(C)] if own_kv else [("wv", wv, None)]
        N_QKV = len(pieces)
        pieces += [("wo", wo, j) for j in range(NJ)]
        NP = len(pieces)
        STAGES = 2 if own_kv else 5
        POOL_SPLITS = 2 * C if own_kv else C
        assert NP % STAGES == 0
        stage = t.sb("stage", [P, STAGES, D])

        q = t.pair("q", [dh, Q_RING, HALF])
        k = t.pair("k", [dh, 2, HALF] if own_kv else [dh, HB, NK])
        v = t.pair("v", [P, 2, QW] if own_kv else [P, NS, HB * dh])
        if not own_kv:
            values_turned = t.sb("values_turned", [dh, HALF])
        probs = t.sb("probs", [P, P_RING, HB * NK])
        probsT = t.pair("probsT", [P, NS, NJ, HB * P])
        heads = t.pair("heads", [dh, HEAD_RING, NJ * P])
        neg_max = t.sb("neg_max", [P, NJ, HB])
        sums = t.sb("sums", [P, NJ, HB])
        recip = t.sb("recip", [P, NJ, HB])
        if A.bias:
            bias = t.sb("bias", [P, NJ, P])
            ln_w = bias[:].rearrange("p j k -> p (j k)")
        if A.mask:
            mask_raw = stage[:, STAGES - 1, 0:B * P // 4].bitcast(U8) if A.mask == "bool" else \
                t.sb("mask_raw", [P, B * P])[:]
            mask_add = t.sb("mask_add", [P, B, P], BF16)
            row_kept = t.sb("row_kept", [P, B])
        if A.rope:
            cos, sin = t.sb("cos", [P, P]), t.sb("sin", [P, P])
            straight, crossed = t.sb("straight", [P, 2, HALF]), t.sb("crossed", [P, 2, HALF])

        staged = [t.sem(f"staged{s}") for s in range(STAGES)]
        stage_free = t.sem("stage_free")
        first_hi, late_hi, w_hi, w_ready = t.sem("first_hi"), t.sem("late_hi"), t.sem("w_hi"), t.sem("w_ready")
        tables, mask_in, bias_in, bias_free = t.sem("tables"), t.sem("mask_in"), t.sem("bias_in"), t.sem("bias_free")
        start_used = t.sem("start_used")
        job_done, job_hi, job_out = t.sem("job_done"), t.sem("job_hi"), t.sem("job_out")
        scored, score_free = t.sem("scored"), t.sem("score_free")
        soft, max_ready, exp_done = t.sem("soft"), t.sem("max_ready"), t.sem("exp_done")
        recip_ready, probs_ready = t.sem("recip_ready"), t.sem("probs_ready")
        turned, turned_hi, turned_out = t.sem("turned"), t.sem("turned_hi"), t.sem("turned_out")
        headed, heads_hi, heads_out = t.sem("headed"), t.sem("heads_hi"), t.sem("heads_out")
        projected, added = t.sem("projected"), t.sem("added")
        if A.rope:
            bank_read, crossing, rotated = t.sem("bank_read"), t.sem("crossing"), t.sem("rotated")
            rotated_hi, rotated_out = t.sem("rotated_hi"), t.sem("rotated_out")
        norm = Norm(t, G, probs[:].rearrange("p a (b c) -> p (a b) c", c=D), ln_w if A.bias else None)
        block = ctx.enter_context(nc.Block())

        def job_no(half, kind, n):
            return A.index(half, kind, n, ("Q", "K", "V", "U"))

        def rotated_no(half, kind, n):
            return A.index(half, kind, n, ("Q", "K"))

        def value_no(half, kind, n):
            return A.index(half, kind, n, ("V", "U"))

        def head_no(half, j):
            return half * NJ + j

        def batch_no(half, b):
            return half * HB + b

        def split_piece(g, n):
            if n < NJ:
                return pieces[N_QKV + n], g * NP + N_QKV + n
            return pieces[n - NJ], g * NP + NP + n - NJ

        def slot_of(n):
            return (N_QKV + n) % STAGES

        def piece_tiles(piece, slot):
            name, w, c = piece
            if c is None:
                return w[0][:], w[1][:], stage[:, slot, 0:C * dh].rearrange("p (c o) -> p c o", c=C)
            hi, lo = w[0][:, c, :], w[1][:, c, :]
            return hi, lo, stage[0:hi.shape[0], slot, 0:hi.shape[1]]

        def arrived(eng, g, n):
            turns = g * (NP // STAGES) + (N_QKV + n) // STAGES
            eng.wait_ge(staged[slot_of(n)], turns * 16 + 16)

        def rotated_tiles(kind, n, m):
            src = straight[:, m % 2, :]
            if kind == "HQ":
                return *at(q, ALL, n), src
            return *at(k, ALL, ALL, slice(0, P)), src.rearrange("p (b t) -> p b t", b=HB)

        def score_bank(i, b):
            if NS == 1:
                return G.ps[:, SCORE + i % 2, b * P:(b + 1) * P]
            return G.ps[:, SCORE + b // 2, b % 2 * NK:(b % 2 + 1) * NK]

        @block.sync
        def _(sp):
            def tables_and_mask():
                if A.bias:
                    sp.dma_start(ln_w, d["ln_w"].partition_broadcast(P)).then_inc(tables, 16)
                if A.rope:
                    sp.dma_start(cos[:], d["cos"]).then_inc(tables, 16)
                    sp.dma_start(sin[:], d["sin"]).then_inc(tables, 16)
                if A.mask:
                    src = d[A.name + "_mask"].rearrange("b q k -> q b k")
                    dst = mask_raw.bitcast(I32) if A.mask == "bool" else mask_raw
                    sp.dma_start(dst.rearrange("p (b k) -> p b k", b=B), src).then_inc(mask_in, 16)

            def load(piece, g, place, slot):
                name, _, c = piece
                sp.wait_ge(stage_free, place + 1)
                src = d[A.name + "_" + name][g] if c is None else d[A.name + "_" + name][g, c]
                sp.dma_start(piece_tiles(piece, slot)[2], src).then_inc(staged[slot], 16)

            def group(g, more):
                if A.bias:
                    sp.wait_ge(bias_free, g + 1)
                    sp.dma_start(bias[:], d["bias"][g]).then_inc(bias_in, 16)
                for n in range(NP if more else NJ):
                    piece, place = split_piece(g, n)
                    load(piece, g if n < NJ else g + 1, place, slot_of(n))

            if A.bias:
                tables_and_mask()
            for n in range(N_QKV):
                if n == STAGES and not A.bias:
                    tables_and_mask()
                if A.bias and n == STAGES - 1:
                    sp.wait_ge(start_used, 1)
                load(pieces[n], 0, n, n % STAGES)
            with sp.Fori(0, NG - 1) as g:
                group(g, True)
            group(NG - 1, False)

        @block.gpsimd
        def _(pool):
            pool.sem_inc(stage_free, STAGES)
            for n in range(N_QKV):
                hi, lo, raw = piece_tiles(pieces[n], n % STAGES)
                pool.wait_ge(staged[n % STAGES], 16 * (n // STAGES) + 16)
                if n < POOL_SPLITS:
                    rounded(nc, G, hi, raw).then_inc(first_hi, 1)
                    pool.wait_ge(first_hi, n + 1)
                else:
                    pool.wait_ge(late_hi, n - POOL_SPLITS + 1)
                nc.gpsimd.tensor_tensor(lo, raw, hi.bitcast(F32), ALU.subtract).then_inc(w_ready, 1)
                pool.wait_ge(w_ready, n + 1)
                pool.sem_inc(stage_free, 1)

            def group(g, more):
                for half, kind, n in steps:
                    if kind == "W" and (more or n < NJ):
                        piece, place = split_piece(g, n)
                        hi, lo, raw = piece_tiles(piece, slot_of(n))
                        pool.wait_ge(w_hi, place - N_QKV + 1)
                        nc.gpsimd.tensor_tensor(lo, raw, hi.bitcast(F32), ALU.subtract).then_inc(w_ready, 1)
                        pool.wait_ge(w_ready, place + 1)
                        pool.sem_inc(stage_free, 1)
                    elif kind == "N":
                        i = head_no(half, n)
                        pool.wait_ge(recip_ready, g * HEADS + i + 1)
                        pj = probs[:, i % P_RING, :].rearrange("p (b k) -> p b k", b=HB)
                        nc.gpsimd.tensor_tensor(pj, pj, recip[:, n, :].unsqueeze(2).to_broadcast([P, HB, NK]),
                                                ALU.mult).then_inc(probs_ready, 1)
                    elif kind in ("Q", "K") and A.rope:
                        m = rotated_no(half, kind, n)
                        pool.wait_ge(crossing, g * ROTATED + m + 1)
                        nc.gpsimd.tensor_tensor(straight[:, m % 2, :], straight[:, m % 2, :], crossed[:, m % 2, :],
                                                ALU.add).then_inc(rotated, 1)
                    elif kind in ("HQ", "HK"):
                        m = rotated_no(half, kind[1], n)
                        hi, lo, src = rotated_tiles(kind, n, m)
                        pool.wait_ge(rotated_hi, g * ROTATED + m + 1)
                        nc.gpsimd.tensor_tensor(lo, src, hi.bitcast(F32), ALU.subtract
                                                ).then_inc(rotated_out, 1)

            with pool.Fori(0, NG - 1) as g:
                group(g, True)
            group(NG - 1, False)

        @block.tensor
        def _(pe):
            pe.sem_inc(projected, HEAD_RING)
            pe.sem_inc(turned, P_RING)
            norm.tensor(pe)
            pe.wait_ge(norm.lo_done, HB)

            def job(g, half, kind, n):
                m = job_no(half, kind, n)
                pe.wait_ge(bank_read if A.rope else job_out, g * JOBS + m + 1)
                bank = G.ps[:, PROJ + m % 2, :]
                if kind in ("Q", "K"):
                    toks = slice(half * HALF, (half + 1) * HALF)
                    w, src = (wq, G.xn) if kind == "Q" else (wk, G.ctx if own_kv else sources[n])
                    cols = slice(n * dh, (n + 1) * dh) if kind == "Q" or own_kv else slice(0, dh)
                    for c in range(C):
                        last = product(nc, bank[0:dh, :], at(w, ALL, c, cols), at(src, ALL, c, toks),
                                       c == 0, c == C - 1)
                elif own_kv:
                    tile = slice((half * HB + n) * P, (half * HB + n + 1) * P)
                    for c in range(C):
                        last = product(nc, bank, at(G.ctx, ALL, c, tile), at(wv, ALL, c), c == 0, c == C - 1)
                elif kind == "V":
                    toks = slice(half * HALF, (half + 1) * HALF)
                    for c in range(C):
                        last = product(nc, bank[0:dh, :], at(wv, ALL, c), at(sources[n], ALL, c, toks),
                                       c == 0, c == C - 1)
                else:
                    if A.rope:
                        pe.wait_ge(job_out, g * NV + value_no(half, "V", n) + 1)
                    else:
                        pe.wait_ge(job_out, g * JOBS + job_no(half, "V", n) + 1 + 2)
                    for b in range(HB):
                        last = nc.tensor.transpose(bank[:, b * dh:(b + 1) * dh],
                                                   values_turned[:, b * P:(b + 1) * P], G.ident[0:dh, 0:dh])
                last.then_inc(job_done, 1)

            def group(g):
                pe.wait_ge(w_ready, g * NP + N_QK)
                for half, kind, n in steps:
                    if kind in ("Q", "K", "V", "U"):
                        if (half, kind, n) == (0, "V", 0):
                            pe.wait_ge(w_ready, g * NP + N_QKV)
                        job(g, half, kind, n)
                    elif kind == "S":
                        i = head_no(half, n)
                        if A.rope:
                            pe.wait_ge(rotated_out, g * ROTATED + rotated_no(half, "Q", n) + 1 + 2)
                        else:
                            made = job_no(half, "K", n) if own_kv else job_no(half, "Q", n)
                            pe.wait_ge(job_out, g * JOBS + made + 1 + 2)
                        pe.wait_ge(score_free if A.mask else exp_done, g * HEADS + i + 1)
                        for b in range(HB):
                            col = slice(b * P, (b + 1) * P)
                            last = product(nc, score_bank(i, b), at(q, ALL, n % Q_RING, col),
                                           at(k, ALL, n % 2, col) if own_kv else at(k, ALL, b), True, True)
                        last.then_inc(scored, 1)
                    elif kind == "T":
                        i = head_no(half, n)
                        pe.wait_ge(turned_out, g * HEADS + i + 1)
                        pe.wait_ge(probs_ready, g * HEADS + i + 1)
                        if i == 0:
                            pe.wait_ge(norm.lo_done, B)
                        src = probs[:, i % P_RING, :].rearrange("p (b k) -> p b k", b=HB)
                        for s in range(NS):
                            for b in range(HB):
                                last = nc.tensor.transpose(G.ps[:, TURN + s, b * P:(b + 1) * P],
                                                           src[:, b, s * P:(s + 1) * P], G.ident[:])
                        last.then_inc(turned, 1)
                    elif kind == "A":
                        m = batch_no(half, n)
                        pe.wait_ge(heads_out, g * B + m + 1)
                        pe.wait_ge(turned_out, g * HEADS + NJ * (half + 1) + 1)
                        if own_kv or n == 0:
                            if A.rope:
                                pe.wait_ge(job_out, g * NV + value_no(half, "U", NS - 1) + 1)
                            else:
                                last_v = job_no(half, "V", n) if own_kv else job_no(half, "U", NS - 1)
                                pe.wait_ge(job_out, g * JOBS + last_v + 1 + 2)
                        bank = G.ps[0:dh, HEAD + m % HEAD_BANKS, :]
                        cols = slice(n * P, (n + 1) * P)
                        if own_kv:
                            for j in range(NJ):
                                last = product(nc, bank[:, j * P:(j + 1) * P],
                                               at(v, ALL, n % 2, slice(j * dh, (j + 1) * dh)),
                                               at(probsT, ALL, 0, j, cols), True, True)
                        else:
                            for s in range(NS):
                                last = product(nc, bank, at(v, ALL, s, slice(n * dh, (n + 1) * dh)),
                                               at(probsT, ALL, s, ALL, cols), s == 0, s == NS - 1)
                        last.then_inc(headed, 1)
                    elif kind == "O":
                        m = batch_no(half, n)
                        if m == 0:
                            pe.wait_ge(w_ready, g * NP + NP)
                        pe.wait_ge(heads_out, g * B + m + 1 + HEAD_BANKS)
                        pe.wait_ge(added, g * B + m + 1)
                        for j in range(NJ):
                            last = product(nc, G.ps[:, OUT, :],
                                           at(heads, ALL, m % HEAD_RING, slice(j * P, (j + 1) * P)),
                                           at(wo, ALL, j), j == 0, j == NJ - 1)
                        last.then_inc(projected, 1)

            with pe.Fori(0, NG) as g:
                group(g)

        def job_tiles(half, kind, n):
            bank = G.ps[:, PROJ + job_no(half, kind, n) % 2, :]
            if kind == "Q":
                return bank[0:dh, :], at(q, ALL, n % Q_RING)
            if kind == "K" and own_kv:
                return bank[0:dh, :], at(k, ALL, n % 2)
            if kind == "K":
                return bank[0:dh, :].rearrange("p (b t) -> p b t", b=HB), \
                    at(k, ALL, ALL, slice(n * P, (n + 1) * P))
            if own_kv:
                return bank, at(v, ALL, n % 2)
            if kind == "V":
                return bank[0:dh, :], (values_turned[:], None)
            return bank[:, 0:HB * dh], at(v, ALL, n)

        @block.scalar
        def _(a):
            if not A.mask:
                a.sem_inc(exp_done, 1)
            norm.scalar(a)
            for n in range(POOL_SPLITS, N_QKV):
                hi, _, raw = piece_tiles(pieces[n], n % STAGES)
                a.wait_ge(staged[n % STAGES], 16 * (n // STAGES) + 16)
                nc.scalar.copy(hi, raw).then_inc(late_hi, 1)

            def group(g, more):
                for half, kind, n in steps:
                    if kind in ("V", "U") or kind in ("Q", "K") and not A.rope:
                        m = job_no(half, kind, n)
                        src, (hi, _) = job_tiles(half, kind, n)
                        a.wait_ge(job_done, g * JOBS + m + 1)
                        nc.scalar.copy(hi, src).then_inc(job_hi, 1)
                    elif kind in ("HQ", "HK"):
                        m = rotated_no(half, kind[1], n)
                        hi, _, src = rotated_tiles(kind, n, m)
                        a.wait_ge(rotated, g * ROTATED + m + 1)
                        nc.scalar.copy(hi, src).then_inc(rotated_hi, 1)
                    elif kind == "W" and (more or n < NJ):
                        piece, place = split_piece(g, n)
                        hi, _, raw = piece_tiles(piece, slot_of(n))
                        arrived(a, g, n)
                        nc.scalar.copy(hi, raw).then_inc(w_hi, 1)
                    elif kind == "E":
                        i = head_no(half, n)
                        a.wait_ge(max_ready, g * HEADS + i + 1)
                        if not A.mask:
                            a.wait_ge(turned, g * HEADS + i + 1)
                        for b in range(HB):
                            dst = probs[:, i % P_RING, b * NK:(b + 1) * NK]
                            src = dst if A.mask else score_bank(i, b)
                            last = nc.scalar.activation(dst, src, ACT.Exp, bias=neg_max[:, n, b:b + 1],
                                                        scale=A.scale, accum_out=sums[:, n, b:b + 1])
                        last.then_inc(exp_done, 1)
                    elif kind == "T":
                        i = head_no(half, n)
                        a.wait_ge(turned, g * HEADS + i + 1 + P_RING)
                        nc.scalar.copy(probsT[0][:, :, n, :], G.ps[:, TURN:TURN + NS, :]).then_inc(turned_hi, 1)
                    elif kind == "A":
                        m = batch_no(half, n)
                        a.wait_ge(headed, g * B + m + 1)
                        a.wait_ge(projected, g * B + m + 1)
                        nc.scalar.copy(heads[0][:, m % HEAD_RING, :], G.ps[0:dh, HEAD + m % HEAD_BANKS, :]
                                       ).then_inc(heads_hi, 1)

            with a.Fori(0, NG - 1) as g:
                group(g, True)
            group(NG - 1, False)

        PER_HEAD = (2 if A.bias else 1 if A.mask else 0) + (A.scale != 1.0) + bool(A.bias)
        EXP_CREDIT = 0 if A.mask else 1

        @block.vector
        def _(dve):
            dve.sem_inc(bank_read if A.rope else job_out, 2)
            dve.sem_inc(score_free, SCORE_RING)
            dve.sem_inc(turned_out, 1)
            dve.sem_inc(heads_out, HEAD_BANKS)
            dve.sem_inc(added, 1)
            def make_mask():
                dve.wait_ge(mask_in, 16)
                nc.vector.tensor_scalar(mask_add[:], mask_raw.rearrange("p (b k) -> p b k", b=B), 0.0, MASKED,
                                        ALU.is_equal, ALU.mult).then_inc(start_used, 1)
                dve.wait_ge(start_used, 1)

            if A.bias:
                make_mask()
                nc.vector.tensor_reduce(row_kept[:], mask_add[:], AX.X, ALU.max).then_inc(start_used, 1)
                dve.wait_ge(start_used, 2)
                nc.vector.tensor_scalar(row_kept[:], row_kept[:], 0.0, None, ALU.is_equal
                                        ).then_inc(start_used, 1)
                dve.wait_ge(start_used, 3)
                dve.wait_ge(tables, 16)
            norm.vector(dve)
            if A.bias:
                dve.wait_ge(norm.h_ready[0], B)
                dve.sem_inc(bias_free, 1)
            elif A.mask:
                make_mask()
            if A.rope:
                dve.wait_ge(tables, 32)

            def rotate(g, half, kind, n):
                m, by_tok, rows = rotated_no(half, kind, n), "p (b s) -> p b s", P // 2
                src = G.ps[:, PROJ + job_no(half, kind, n) % 2, :]
                dve.wait_ge(job_done, g * JOBS + job_no(half, kind, n) + 1)
                dve.wait_ge(rotated_out, g * ROTATED + m + 1)
                nc.vector.tensor_tensor(straight[:, m % 2, :].rearrange(by_tok, b=HB), src.rearrange(by_tok, b=HB),
                                        cos[:].unsqueeze(1).to_broadcast([P, HB, P]), ALU.mult)
                for to, of in ((0, rows), (rows, 0)):
                    last = nc.vector.tensor_tensor(
                        crossed[to:to + rows, m % 2, :].rearrange(by_tok, b=HB),
                        src[of:of + rows, :].rearrange(by_tok, b=HB),
                        sin[of:of + rows, :].unsqueeze(1).to_broadcast([rows, HB, P]), ALU.mult)
                last.then_inc(crossing, 1)
                dve.wait_ge(crossing, g * ROTATED + m + 1)
                dve.sem_inc(bank_read, 1)

            def group(g, final):
                done = [0]

                def step(ins):
                    done[0] += 1
                    ins.then_inc(soft, 1)
                    dve.wait_ge(soft, g * (HEADS * PER_HEAD) + done[0])

                for half, kind, n in steps:
                    if kind in ("Q", "K") and A.rope:
                        rotate(g, half, kind, n)
                    elif kind in ("Q", "K", "V", "U"):
                        src, (hi, lo) = job_tiles(half, kind, n)
                        m = g * NV + value_no(half, kind, n) if A.rope else g * JOBS + job_no(half, kind, n)
                        dve.wait_ge(job_hi, m + 1)
                        if lo is None:
                            if not A.rope:
                                dve.wait_ge(job_out, m + 2)
                            dve.sem_inc(job_out, 1)
                        else:
                            nc.vector.tensor_tensor(lo, src, hi.bitcast(F32), ALU.subtract).then_inc(job_out, 1)
                        if A.rope:
                            dve.wait_ge(job_out, m + 1)
                            dve.sem_inc(bank_read, 1)
                    elif kind == "S":
                        i = head_no(half, n)
                        dve.wait_ge(scored, g * HEADS + i + 1)
                        if A.mask:
                            dve.wait_ge(turned, g * HEADS + i + 1)
                            sc = G.ps[:, SCORE + i % 2, :].rearrange("p (b k) -> p b k", b=HB)
                            pj = probs[:, i % P_RING, :].rearrange("p (b k) -> p b k", b=HB)
                            madd = mask_add[:, half * HB:(half + 1) * HB, :]
                            if A.bias:
                                if i == 0:
                                    dve.wait_ge(bias_in, g * 16 + 16)
                                step(nc.vector.tensor_tensor(pj, sc, bias[:, n, :].unsqueeze(1).to_broadcast([P, HB, P]),
                                                             ALU.add))
                                dve.sem_inc(score_free, 1)
                                if i == HEADS - 1:
                                    dve.sem_inc(bias_free, 1)
                                step(nc.vector.tensor_tensor(pj, pj, madd, ALU.add))
                            else:
                                step(nc.vector.tensor_tensor(pj, sc, madd, ALU.add))
                                dve.sem_inc(score_free, 1)
                            src, dst = pj, neg_max[:, n, :]
                        else:
                            src = G.ps[:, SCORE:SCORE + NS, :].rearrange("p s (b k) -> p s b k", k=NK)
                            dst = neg_max[:, n, :].rearrange("p (s b) -> p s b", s=NS)
                        ins = nc.vector.tensor_reduce(dst, src, AX.X, ALU.max, negate=True)
                        if A.scale != 1.0:
                            step(ins)
                            ins = nc.vector.tensor_scalar(neg_max[:, n, :], neg_max[:, n, :], A.scale, None, ALU.mult)
                        ins.then_inc(max_ready, 1)
                    elif kind == "N":
                        i = head_no(half, n)
                        dve.wait_ge(exp_done, g * HEADS + i + 1 + EXP_CREDIT)
                        ins = nc.vector.reciprocal(recip[:, n, :], sums[:, n, :])
                        if A.bias:
                            step(ins)
                            ins = nc.vector.tensor_tensor(recip[:, n, :], recip[:, n, :],
                                                          row_kept[:, half * HB:(half + 1) * HB], ALU.mult)
                        ins.then_inc(recip_ready, 1)
                    elif kind == "T":
                        dve.wait_ge(turned_hi, g * HEADS + head_no(half, n) + 1)
                        nc.vector.tensor_tensor(probsT[1][:, :, n, :], G.ps[:, TURN:TURN + NS, :],
                                                probsT[0][:, :, n, :].bitcast(F32), ALU.subtract
                                                ).then_inc(turned_out, 1)
                    elif kind == "A":
                        m = batch_no(half, n)
                        dve.wait_ge(heads_hi, g * B + m + 1)
                        nc.vector.tensor_tensor(heads[1][:, m % HEAD_RING, :], G.ps[0:dh, HEAD + m % HEAD_BANKS, :],
                                                heads[0][:, m % HEAD_RING, :].bitcast(F32), ALU.subtract
                                                ).then_inc(heads_out, 1)
                    elif kind == "O":
                        m = batch_no(half, n)
                        dve.wait_ge(projected, g * B + m + 1 + HEAD_RING)
                        x = G.x[:, m, :]
                        nc.vector.tensor_tensor(x, x, G.ps[:, OUT, :], ALU.add).then_inc(added, 1)
                        if final:
                            dve.wait_ge(added, g * B + m + 1 + 1)
                            tile_stats(nc, G, m)
                assert done[0] == HEADS * PER_HEAD

            if A.rope:
                dve.sem_inc(rotated_out, 2)
            with dve.Fori(0, NG - 1) as g:
                group(g, False)
            group(NG - 1, True)


def swiglu_phase(nc, G, d):
    I2 = 2
    NG, NP, WIDE = d["glu_w"].shape[0], I2 + 1, 2 * D
    DOWN = I2
    PAIRS = I2 * 2
    OUTS = 4

    with ExitStack() as ctx:
        t = Tiles(nc, ctx, "glu")
        h = t.sb("h", [P, 4, D])
        stage, scales = t.sb("stage", [P, NP, WIDE]), t.sb("scales", [P, NP, WIDE])
        whole = t.sb("whole", [P, WIDE])
        w = t.pair("w", [P, NP, WIDE])
        gated = t.sb("gated", [P, 2, HALF])
        inner_f = t.sb("inner_f", [P, 2, HALF])
        inner = t.pair("inner", [P, I2, TOK])
        numbers_in = [t.sem(f"numbers_in{s}") for s in range(NP)]
        scales_in = [t.sem(f"scales_in{s}") for s in range(NP)]
        scaled, w_hi, w_ready = t.sem("scaled"), t.sem("w_hi"), t.sem("w_ready")
        gu_free = [t.sem(f"gu_free{i}") for i in range(I2)]
        gate_up, silu_done, pair_out = t.sem("gate_up"), t.sem("silu_done"), t.sem("pair_out")
        inner_hi, inner_out = t.sem("inner_hi"), t.sem("inner_out")
        projected, added = t.sem("projected"), t.sem("added")
        norm = Norm(t, G, h)
        block = ctx.enter_context(nc.Block())

        @block.sync
        def _(sp):
            with sp.Fori(0, NG) as g:
                for n in range(NP):
                    sp.wait_ge(scaled, g * NP + n + 1)
                    sp.dma_start(scales[:, n, :], d["glu_scale"][g, n].partition_broadcast(P)
                                 ).then_inc(scales_in[n], 16)

        @block.gpsimd
        def _(pool):
            def load(g, n):
                pool.dma_start(stage[:, n, :], d["glu_w"][g, n]).then_inc(numbers_in[n], 16)

            def turn(g, more):
                for n in range(NP):
                    m = g * NP + n
                    pool.wait_ge(numbers_in[n], g * 16 + 16)
                    pool.wait_ge(scales_in[n], g * 16 + 16)
                    if n == DOWN:
                        pool.wait_ge(added, g * B + OUTS)
                    else:
                        pool.wait_ge(gu_free[n], g + 1)
                    nc.gpsimd.tensor_tensor(w[0][:, n, :], stage[:, n, :], scales[:, n, :], ALU.mult).then_inc(w_hi, 1)
                    nc.gpsimd.tensor_tensor(whole[:], stage[:, n, :], scales[:, n, :], ALU.mult).then_inc(scaled, 1)
                    pool.wait_ge(scaled, m + NP + 1)
                    if more:
                        load(g + 1, n)
                    pool.wait_ge(w_hi, m + 1)
                    nc.gpsimd.tensor_tensor(w[1][:, n, :], whole[:], w[0][:, n, :].bitcast(F32), ALU.subtract
                                            ).then_inc(w_ready, 1)
                    pool.wait_ge(w_ready, m + 1)

            pool.sem_inc(scaled, NP)
            for n in range(NP):
                load(0, n)
            with pool.Fori(0, NG - 1) as g:
                turn(g, True)
            turn(NG - 1, False)

        @block.tensor
        def _(pe):
            for i in range(I2):
                pe.sem_inc(gu_free[i], 1)
            norm.tensor(pe)
            pe.wait_ge(norm.lo_done, HB)
            with pe.Fori(0, NG) as g:
                for i in range(I2):
                    pe.wait_ge(w_ready, g * NP + i + 1)
                    for hf in range(2):
                        n = i * 2 + hf
                        if n == 1:
                            pe.wait_ge(norm.lo_done, B)
                        pe.wait_ge(pair_out, g * PAIRS + n + 1)
                        for side in range(2):
                            for c in range(C):
                                last = product(nc, G.ps[:, 2 * (n % 2) + side, :],
                                               at(w, ALL, i, slice(side * D + c * P, side * D + (c + 1) * P)),
                                               at(G.xn, ALL, c, slice(hf * HALF, (hf + 1) * HALF)),
                                               c == 0, c == C - 1,
                                               gu_free[i - 1] if (n % 2, side, c) == (0, 0, 0) and i > 0 else None)
                        last.then_inc(gate_up, 1)
                pe.wait_ge(w_ready, g * NP + NP)
                for tile in range(B):
                    if tile % HB == 0:
                        pe.wait_ge(inner_out, g * PAIRS + PAIRS - 1 + tile // HB + 2)
                    pe.wait_ge(added, g * B + tile + 1)
                    for i in range(I2):
                        last = product(nc, G.ps[:, OUTS + tile % OUTS, :],
                                       at(inner, ALL, i, slice(tile * P, (tile + 1) * P)),
                                       at(w, ALL, DOWN, slice(i * D, (i + 1) * D)), i == 0, i == I2 - 1,
                                       gu_free[I2 - 1] if (tile, i) == (0, 0) else None)
                    last.then_inc(projected, 1)

        def inner_part(n):
            i, hf = n // 2, n % 2
            return at(inner, ALL, i, slice(hf * HALF, (hf + 1) * HALF))

        @block.scalar
        def _(a):
            norm.scalar(a)
            with a.Fori(0, NG) as g:
                for n in range(PAIRS):
                    a.wait_ge(gate_up, g * PAIRS + n + 1)
                    nc.scalar.activation(gated[:, n % 2, :], G.ps[:, 2 * (n % 2), :], ACT.Silu
                                         ).then_inc(silu_done, 1)
                    a.wait_ge(pair_out, g * PAIRS + n + 3)
                    nc.scalar.copy(inner_part(n)[0], inner_f[:, n % 2, :]).then_inc(inner_hi, 1)

        @block.vector
        def _(v):
            v.sem_inc(pair_out, 2)
            v.sem_inc(inner_out, 2)
            v.sem_inc(added, OUTS)
            norm.vector(v)

            def turn(g, final):
                for n in range(PAIRS):
                    hi, lo = inner_part(n)
                    v.wait_ge(inner_out, g * PAIRS + n + 1)
                    v.wait_ge(silu_done, g * PAIRS + n + 1)
                    nc.vector.tensor_tensor(inner_f[:, n % 2, :], gated[:, n % 2, :],
                                            G.ps[:, 2 * (n % 2) + 1, :], ALU.mult).then_inc(pair_out, 1)
                    v.wait_ge(inner_hi, g * PAIRS + n + 1)
                    nc.vector.tensor_tensor(lo, inner_f[:, n % 2, :], hi.bitcast(F32), ALU.subtract
                                            ).then_inc(inner_out, 1)
                for tile in range(B):
                    v.wait_ge(projected, g * B + tile + 1)
                    x = G.x[:, tile, :]
                    nc.vector.tensor_tensor(x, x, G.ps[:, OUTS + tile % OUTS, :], ALU.add).then_inc(added, 1)
                    if final:
                        v.wait_ge(added, g * B + tile + 1 + OUTS)
                        tile_stats(nc, G, tile)

            with v.Fori(0, NG - 1) as g:
                turn(g, False)
            turn(NG - 1, True)


def low_rank_phase(nc, G, d, name, rank, dense):
    RT = rank // P
    OUTS = 4
    with ExitStack() as ctx:
        t = Tiles(nc, ctx, name)
        h = t.sb("h", [P, 4, D])
        a, b = t.pair("a", [P, C, rank]), t.pair("b", [P, RT, D])
        parts = [("a", a, C * rank), ("b", b, RT * D)]
        if dense:
            w = t.pair("w", [P, C, D])
            parts.append(("w", w, C * D))
            bias = t.sb("bias", [P, D])
        raw = {k: t.sb(k + "_raw", [P, n]) for k, _, n in parts}
        factors = t.sb("factors", [P, 2, RT])
        weight = t.sb("weight", [P, RT])
        low_f, low = t.sb("low_f", [P, RT, TOK]), t.pair("low", [P, RT, TOK])
        part_in = {k: t.sem(k + "_in") for k, _, _ in parts}
        small_in, w_hi, w_ready = t.sem("small_in"), t.sem("w_hi"), t.sem("w_ready")
        weight_ready, low_done, low_scaled = t.sem("weight_ready"), t.sem("low_done"), t.sem("low_scaled")
        low_hi, low_out, projected, added = t.sem("low_hi"), t.sem("low_out"), t.sem("projected"), t.sem("added")
        biased = t.sem("biased")
        norm = Norm(t, G, h)
        block = ctx.enter_context(nc.Block())
        pieces = [(k, pr, n, c) for k, pr, n in parts for c in range(n // 512)]
        halves = [(r, hf) for r in range(RT) for hf in range(2)]
        smalls = 3 if dense else 1

        @block.sync
        def _(sp):
            for k, _, n in parts:
                sp.dma_start(raw[k][:], d[f"{name}_{k}"]).then_inc(part_in[k], 16)
                if k == "a":
                    sp.dma_start(factors[:, 0, :], d[f"{name}_factor0"]).then_inc(small_in, 16)
            if dense:
                sp.dma_start(factors[:, 1, :], d[f"{name}_factor1"]).then_inc(small_in, 16)
                sp.dma_start(bias[:], d[f"{name}_bias"].partition_broadcast(P)).then_inc(small_in, 16)

        @block.gpsimd
        def _(pool):
            for m, (k, pr, n, c) in enumerate(pieces):
                if c == 0:
                    pool.wait_ge(part_in[k], 16)
                cols = slice(c * 512, (c + 1) * 512)
                hi, lo = (x[:].rearrange("p a b -> p (a b)")[:, cols] for x in pr)
                rounded(nc, G, hi, raw[k][:, cols]).then_inc(w_hi, 1)
                pool.wait_ge(w_hi, m + 1)
                nc.gpsimd.tensor_tensor(lo, raw[k][:, cols], hi.bitcast(F32), ALU.subtract).then_inc(w_ready, 1)

        @block.tensor
        def _(pe):
            norm.tensor(pe)
            pe.wait_ge(norm.lo_done, HB)
            pe.wait_ge(w_ready, C * rank // 512)
            for n, (r, hf) in enumerate(halves):
                if n == 1:
                    pe.wait_ge(norm.lo_done, B)
                for c in range(C):
                    last = product(nc, G.ps[:, n, :], at(a, ALL, c, slice(r * P, (r + 1) * P)),
                                   at(G.xn, ALL, c, slice(hf * HALF, (hf + 1) * HALF)), c == 0, c == C - 1)
                last.then_inc(low_done, 1)
            pe.wait_ge(w_ready, len(pieces))
            if not dense:
                pe.wait_ge(low_out, len(halves))
            for tile in range(B):
                toks = slice(tile * P, (tile + 1) * P)
                if tile >= OUTS:
                    pe.wait_ge(added, tile - OUTS + 1)
                if dense:
                    for c in range(C):
                        product(nc, G.ps[:, OUTS + tile % OUTS, :], at(G.xn, ALL, c, toks), at(w, ALL, c),
                                c == 0, False)
                    if tile == 0:
                        pe.wait_ge(low_out, len(halves))
                for r in range(RT):
                    last = product(nc, G.ps[:, OUTS + tile % OUTS, :], at(low, ALL, r, toks), at(b, ALL, r),
                                   r == 0 and not dense, r == RT - 1)
                last.then_inc(projected, 1)

        @block.scalar
        def _(act):
            norm.scalar(act)
            act.wait_ge(weight_ready, 1)
            for n, (r, hf) in enumerate(halves):
                toks = slice(hf * HALF, (hf + 1) * HALF)
                act.wait_ge(low_done, n + 1)
                nc.scalar.mul(low_f[:, r, toks], G.ps[:, n, :], weight[:, r:r + 1]).then_inc(low_scaled, 1)
                act.wait_ge(low_scaled, n + 1)
                nc.scalar.copy(low[0][:, r, toks], low_f[:, r, toks]).then_inc(low_hi, 1)

        @block.vector
        def _(v):
            norm.vector(v)
            v.wait_ge(small_in, 16 * smalls)
            if dense:
                nc.vector.tensor_tensor(weight[:], factors[:, 0, :], factors[:, 1, :], ALU.mult
                                        ).then_inc(weight_ready, 1)
            else:
                nc.vector.tensor_copy(weight[:], factors[:, 0, :]).then_inc(weight_ready, 1)
            for n, (r, hf) in enumerate(halves):
                toks = slice(hf * HALF, (hf + 1) * HALF)
                v.wait_ge(low_hi, n + 1)
                nc.vector.tensor_tensor(low[1][:, r, toks], low_f[:, r, toks], low[0][:, r, toks].bitcast(F32),
                                        ALU.subtract).then_inc(low_out, 1)
            for tile in range(B):
                x = G.x[:, tile, :]
                v.wait_ge(projected, tile + 1)
                nc.vector.tensor_tensor(x, x, G.ps[:, OUTS + tile % OUTS, :], ALU.add).then_inc(added, 1)
                v.wait_ge(added, tile + 1)
                if dense:
                    nc.vector.tensor_tensor(x, x, bias[:], ALU.add).then_inc(biased, 1)
                    v.wait_ge(biased, tile + 1)
                tile_stats(nc, G, tile)


def linear_attention_phase(nc, G, d):
    H, DH = 8, P // 8
    R2 = 2
    TURNS = B // R2
    KTURN, QTURN, KV, QBACK, OUT = 0, 2, 4, 5, 6
    with ExitStack() as ctx:
        t = Tiles(nc, ctx, "lin")
        h = t.sb("h", [P, R2, D])
        k_raw, k_soft = t.sb("k_raw", [P, R2, D]), t.sb("k_soft", [P, R2, D])
        k_max, k_sum, k_rec = t.sb("k_max", [P, R2]), t.sb("k_sum", [P, R2]), t.sb("k_rec", [P, R2])
        kT = t.pair("kT", [P, R2, D])
        own_head = t.sb("own_head", [P, P])
        kv_f, kv = t.sb("kv_f", [P, R2, P]), t.pair("kv", [P, R2, P])
        q_max, q_sum = t.sb("q_max", [P, R2, C * H]), t.sb("q_sum", [P, R2, C * H])
        qT = t.sb("qT", [P, R2, D])
        q = t.pair("q", [P, R2, D])
        k_in = [t.sem(f"k_in{i}") for i in range(R2)]
        table_in = t.sem("table_in")
        names = ("k_maxed k_exped k_summed k_ready k_turned kT_hi kT_out kv_done kv_masked kv_hi kv_out "
                 "h_ready q_turned q_step q_shifted q_exped q_summed q_ready q_back q_hi q_out out_done added").split()
        S = {n: t.sem(n) for n in names}
        norm = Norm(t, G, h)
        block = ctx.enter_context(nc.Block())
        by_head = "p (g e) -> p g e"

        def wide(small):
            return small.unsqueeze(2).to_broadcast([P, C * H, DH])

        def batches(eng, turn):
            with eng.Fori(0, TURNS - 1) as t2:
                turn(t2, True)
            turn(TURNS - 1, False)

        @block.sync
        def _(sp):
            sp.dma_start(own_head[:], d["own_head"]).then_inc(table_in, 16)
            with sp.Fori(0, TURNS) as t2:
                for i in range(R2):
                    n = t2 * R2 + i
                    sp.wait_ge(S["k_exped"], n + 1)
                    sp.dma_start(k_raw[:, i, :], d["ctx"][n]).then_inc(k_in[i], 16)

        @block.vector
        def _(v):
            def maximum_of_keys(n, i, loads):
                v.wait_ge(k_in[i], loads * 16)
                nc.vector.tensor_reduce(k_max[:, i:i + 1], k_raw[:, i, :], AX.X, ALU.max, negate=True
                                        ).then_inc(S["k_maxed"], 1)

            def shifted_queries(n, i):
                v.wait_ge(S["q_turned"], n + 1)
                bank = G.ps[:, QTURN + i, :].rearrange(by_head, e=DH)
                nc.vector.tensor_reduce(q_max[:, i, :], bank, AX.X, ALU.max).then_inc(S["q_step"], 1)
                v.wait_ge(S["q_step"], n * 2 + 1)
                nc.vector.tensor_tensor(qT[:, i, :].rearrange(by_head, e=DH), bank, wide(q_max[:, i, :]),
                                        ALU.subtract).then_inc(S["q_shifted"], 1)

            def reciprocals(n, i):
                v.wait_ge(S["k_exped"], n + R2 + 1)
                nc.vector.reciprocal(k_rec[:, i:i + 1], k_sum[:, i:i + 1]).then_inc(S["k_summed"], 1)
                v.wait_ge(S["q_exped"], n + 1)
                nc.vector.tensor_reduce(q_sum[:, i, :], qT[:, i, :].rearrange(by_head, e=DH), AX.X, ALU.add
                                        ).then_inc(S["q_step"], 1)
                v.wait_ge(S["q_step"], n * 2 + 2)
                nc.vector.reciprocal(q_sum[:, i, :], q_sum[:, i, :]).then_inc(S["q_summed"], 1)

            def turn(t2, more):
                for i in range(R2):
                    n, prepare = t2 * R2 + i, more or i == 0
                    v.wait_ge(S["kT_hi"], n + 1)
                    nc.vector.tensor_tensor(kT[1][:, i, :], G.ps[:, KTURN + i, :], kT[0][:, i, :].bitcast(F32),
                                            ALU.subtract).then_inc(S["kT_out"], 1)
                    if prepare:
                        shifted_queries(n + 1, 1 - i)
                    v.wait_ge(S["q_hi"], n + 1)
                    nc.vector.tensor_tensor(q[1][:, i, :], G.ps[:, QBACK, :], q[0][:, i, :].bitcast(F32),
                                            ALU.subtract).then_inc(S["q_out"], 1)
                    v.wait_ge(S["kv_done"], n + 1)
                    nc.vector.tensor_tensor(kv_f[:, i, :], G.ps[:, KV, 0:P], own_head[:], ALU.mult
                                            ).then_inc(S["kv_masked"], 1)
                    if prepare:
                        reciprocals(n + 1, 1 - i)
                    v.wait_ge(S["kv_hi"], n + 1)
                    nc.vector.tensor_tensor(kv[1][:, i, :], kv_f[:, i, :], kv[0][:, i, :].bitcast(F32),
                                            ALU.subtract).then_inc(S["kv_out"], 1)
                    if more:
                        maximum_of_keys(n + R2, i, t2 + 2)
                    v.wait_ge(S["out_done"], n + 1)
                    x = G.x[:, n, :]
                    nc.vector.tensor_tensor(x, x, G.ps[:, OUT + i, :], ALU.add).then_inc(S["added"], 1)
                    v.wait_ge(S["added"], n + 1)
                    tile_stats(nc, G, n)

            norm.vector_moments(v)
            v.wait_ge(table_in, 16)
            for n in range(R2):
                maximum_of_keys(n, n, 1)
            shifted_queries(0, 0)
            reciprocals(0, 0)
            batches(v, turn)

        @block.gpsimd
        def _(pool):
            def soft_queries(n, i):
                pool.wait_ge(S["q_summed"], n + 1)
                qi = qT[:, i, :].rearrange(by_head, e=DH)
                nc.gpsimd.tensor_tensor(qi, qi, wide(q_sum[:, i, :]), ALU.mult).then_inc(S["q_ready"], 1)

            def turn(t2, more):
                for i in range(R2):
                    if more or i == 0:
                        soft_queries(t2 * R2 + i + 1, 1 - i)

            soft_queries(0, 0)
            batches(pool, turn)

        @block.scalar
        def _(a):
            def normed(n, i):
                nc.scalar.activation(h[:, i, :], G.x[:, n, :], ACT.Identity, bias=norm.shift[:, bass.ds(n, 1)],
                                     scale=norm.rstd[:, bass.ds(n, 1)]).then_inc(S["h_ready"], 1)

            def exp_of_keys(n, i):
                a.wait_ge(S["k_maxed"], n + 1)
                nc.scalar.activation(k_soft[:, i, :], k_raw[:, i, :], ACT.Exp, bias=k_max[:, i:i + 1],
                                     accum_out=k_sum[:, i:i + 1]).then_inc(S["k_exped"], 1)

            def exp_of_queries(n, i):
                a.wait_ge(S["q_shifted"], n + 1)
                nc.scalar.activation(qT[:, i, :], qT[:, i, :], ACT.Exp).then_inc(S["q_exped"], 1)

            def soft_keys(n, i):
                a.wait_ge(S["k_summed"], n + 1)
                nc.scalar.mul(k_soft[:, i, :], k_soft[:, i, :], k_rec[:, i:i + 1]).then_inc(S["k_ready"], 1)

            def turn(t2, more):
                for i in range(R2):
                    n, prepare = t2 * R2 + i, more or i == 0
                    if prepare:
                        exp_of_keys(n + 1, 1 - i)
                    a.wait_ge(S["k_turned"], n + 1)
                    nc.scalar.copy(kT[0][:, i, :], G.ps[:, KTURN + i, :]).then_inc(S["kT_hi"], 1)
                    a.wait_ge(S["q_back"], n + 1)
                    nc.scalar.copy(q[0][:, i, :], G.ps[:, QBACK, :]).then_inc(S["q_hi"], 1)
                    if more:
                        normed(n + R2, i)
                    if prepare:
                        exp_of_queries(n + 1, 1 - i)
                    a.wait_ge(S["kv_masked"], n + 1)
                    nc.scalar.copy(kv[0][:, i, :], kv_f[:, i, :]).then_inc(S["kv_hi"], 1)
                    if prepare:
                        soft_keys(n + 1, 1 - i)

            a.sem_inc(S["k_exped"], R2)
            norm.scalar_roots(a)
            a.wait_ge(norm.scaling, 1)
            for n in range(R2):
                normed(n, n)
            exp_of_keys(0, 0)
            exp_of_queries(0, 0)
            soft_keys(0, 0)
            batches(a, turn)

        @block.tensor
        def _(pe):
            def turned(bank, src):
                for c in range(C):
                    last = nc.tensor.transpose(G.ps[:, bank, c * P:(c + 1) * P], src[:, c * P:(c + 1) * P], G.ident[:])
                return last

            def queries(n, i):
                pe.wait_ge(S["h_ready"], n + 1)
                turned(QTURN + i, h[:, i, :]).then_inc(S["q_turned"], 1)

            def turn(t2, more):
                for i in range(R2):
                    n = t2 * R2 + i
                    pe.wait_ge(S["k_ready"], n + 1)
                    turned(KTURN + i, k_soft[:, i, :]).then_inc(S["k_turned"], 1)
                    pe.wait_ge(S["q_ready"], n + 1)
                    turned(QBACK, qT[:, i, :]).then_inc(S["q_back"], 1)
                    if more or i == 0:
                        queries(n + 1, 1 - i)
                    pe.wait_ge(S["kT_out"], n + 1)
                    for c in range(C):
                        chunk = slice(c * P, (c + 1) * P)
                        last = product(nc, G.ps[:, KV, 0:P], at(kT, ALL, i, chunk),
                                       (G.ctx[0][:, c, bass.ds(n * P, P)], G.ctx[1][:, c, bass.ds(n * P, P)]),
                                       c == 0, c == C - 1)
                    last.then_inc(S["kv_done"], 1)
                    pe.wait_ge(S["kv_out"], n + 1)
                    pe.wait_ge(S["q_out"], n + 1)
                    product(nc, G.ps[:, OUT + i, :], at(kv, ALL, i), at(q, ALL, i), True, True
                            ).then_inc(S["out_done"], 1)

            queries(0, 0)
            batches(pe, turn)


def experts_phase(nc, G, d, out):
    E = d["experts"].shape[0]
    E2 = 2
    NP = E2 * C
    STAGES = 4
    with ExitStack() as ctx:
        t = Tiles(nc, ctx, "moe")
        h = t.sb("h", [P, 4, D])
        stage = t.sb("stage", [P, STAGES, D])
        w = t.pair("w", [P, E2, C * D])
        gate_raw, gate = t.sb("gate_raw", [P, C, E]), t.pair("gate", [P, C, E])
        numbers = t.sb("numbers", [P, E])
        logits, logits_turned = t.sb("logits", [P, B, E]), t.sb("logits_turned", [E, TOK])
        logits_out = t.sem("logits_out")
        top, top_at = t.sb("top", [P, B, 8]), t.sb("top_at", [P, B, 8], U32)
        top_no = t.sb("top_no", [P, B, 8])
        chosen = t.sb("chosen", [P, 2, B, E])
        share = t.sb("share", [P, 3, B])
        per_expert = t.sb("per_expert", [P, E, B])
        staged = [t.sem(f"staged{s}") for s in range(STAGES)]
        stage_free, w_hi, w_ready, w_free = t.sem("stage_free"), t.sem("w_hi"), t.sem("w_ready"), t.sem("w_free")
        small_in, gate_split = t.sem("small_in"), t.sem("gate_split")
        logits_done, route, exp_in, exp_done = t.sem("logits_done"), t.sem("route"), t.sem("exp_in"), t.sem("exp_done")
        projected, added, stored = t.sem("projected"), t.sem("added"), t.sem("stored")
        norm = Norm(t, G, h)
        block = ctx.enter_context(nc.Block())

        @block.sync
        def _(sp):
            sp.dma_start(gate_raw[:], d["gate_w"]).then_inc(small_in, 16)
            sp.dma_start(numbers[:], d["numbers"].partition_broadcast(P)).then_inc(small_in, 16)
            with sp.Fori(0, E // E2) as g:
                for n in range(NP):
                    sp.wait_ge(stage_free, g * NP + n + 1)
                    sp.dma_start(stage[:, n % STAGES, :], d["experts"][g * E2 + n // C, n % C]
                                 ).then_inc(staged[n % STAGES], 16)
            for tile in range(B):
                sp.wait_ge(added, E * B + tile + 1)
                sp.dma_start(out[tile], G.x[:, tile, :]).then_inc(stored, 16)
            sp.wait_ge(stored, 16 * B)

        @block.gpsimd
        def _(pool):
            pool.sem_inc(stage_free, STAGES)
            pool.wait_ge(small_in, 32)
            nc.gpsimd.tensor_copy(gate[0][:], gate_raw[:]).then_inc(gate_split, 1)
            pool.wait_ge(gate_split, 1)
            nc.gpsimd.tensor_tensor(gate[1][:], gate_raw[:], gate[0][:].bitcast(F32), ALU.subtract
                                    ).then_inc(gate_split, 1)
            with pool.Fori(0, E // E2) as g:
                for n in range(NP):
                    turn = g * (NP // STAGES) + n // STAGES
                    e, c = n // C, n % C
                    cols = slice(c * D, (c + 1) * D)
                    if c == 0:
                        pool.wait_ge(w_free, g * E2 + e + 1)
                    pool.wait_ge(staged[n % STAGES], turn * 16 + 16)
                    src = stage[:, n % STAGES, :]
                    rounded(nc, G, w[0][:, e, cols], src).then_inc(w_hi, 1)
                    pool.wait_ge(w_hi, g * NP + n + 1)
                    nc.gpsimd.tensor_tensor(w[1][:, e, cols], src, w[0][:, e, cols].bitcast(F32), ALU.subtract
                                            ).then_inc(w_ready, 1)
                    pool.wait_ge(w_ready, g * NP + n + 1)
                    pool.sem_inc(stage_free, 1)

        @block.tensor
        def _(pe):
            pe.sem_inc(w_free, 1)
            norm.tensor(pe)
            pe.wait_ge(norm.lo_done, B)
            pe.wait_ge(gate_split, 2)
            for hf in range(2):
                for c in range(C):
                    last = product(nc, G.ps[0:E, hf, :], at(gate, ALL, c),
                                   at(G.xn, ALL, c, slice(hf * HALF, (hf + 1) * HALF)), c == 0, c == C - 1)
                last.then_inc(logits_done, 1)
            pe.wait_ge(logits_out, 2)
            for tile in range(B):
                last = nc.tensor.transpose(G.ps[:, B - 1, tile * E:(tile + 1) * E],
                                           logits_turned[:, tile * P:(tile + 1) * P], G.ident[0:E, 0:E])
            last.then_inc(logits_done, 1)
            with pe.Fori(0, E // E2) as g:
                for e in range(E2):
                    pe.wait_ge(w_ready, g * NP + (e + 1) * C)
                    for tile in range(B):
                        pe.wait_ge(added, g * (E2 * B) + e * B + tile + 1)
                        for c in range(C):
                            last = product(nc, G.ps[:, tile, :], at(G.xn, ALL, c, slice(tile * P, (tile + 1) * P)),
                                           at(w, ALL, e, slice(c * D, (c + 1) * D)), c == 0, c == C - 1,
                                           w_free if tile == 0 and c == 0 else None)
                        last.then_inc(projected, 1)

        @block.scalar
        def _(a):
            norm.scalar(a)
            a.wait_ge(exp_in, 1)
            nc.scalar.activation(share[:, 1, :], share[:, 0, :], ACT.Exp).then_inc(exp_done, 1)

        @block.vector
        def _(v):
            norm.vector(v)
            done = [0]

            def step(ins):
                done[0] += 1
                ins.then_inc(route, 1)
                v.wait_ge(route, done[0])

            for hf in range(2):
                v.wait_ge(logits_done, hf + 1)
                nc.vector.tensor_copy(logits_turned[:, hf * HALF:(hf + 1) * HALF], G.ps[0:E, hf, :]
                                      ).then_inc(logits_out, 1)
            v.wait_ge(logits_done, 3)
            v.wait_ge(small_in, 32)
            step(nc.vector.tensor_copy(logits[:], G.ps[:, B - 1, 0:B * E].rearrange("p (t e) -> p t e", t=B)))
            v.sem_inc(added, B)
            for tile in range(B):
                last = nc.vector.max(top[:, tile, :], logits[:, tile, :])
            step(last)
            for tile in range(B):
                last = nc.vector.max_index(top_at[:, tile, :], top[:, tile, :], logits[:, tile, :])
            step(last)
            step(nc.vector.tensor_copy(top_no[:], top_at[:]))
            nc.vector.tensor_tensor(share[:, 0, :], top[:, :, 1], top[:, :, 0], ALU.subtract).then_inc(exp_in, 1)
            v.wait_ge(exp_done, 1)
            step(nc.vector.tensor_scalar(share[:, 0, :], share[:, 1, :], 1.0, None, ALU.add))
            step(nc.vector.reciprocal(share[:, 2, :], share[:, 0, :]))
            step(nc.vector.tensor_tensor(share[:, 1, :], share[:, 1, :], share[:, 2, :], ALU.mult))
            for rank, s in ((0, 2), (1, 1)):
                step(nc.vector.tensor_tensor(chosen[:, rank], numbers[:].unsqueeze(1).to_broadcast([P, B, E]),
                                             top_no[:, :, rank].unsqueeze(2).to_broadcast([P, B, E]), ALU.is_equal))
                step(nc.vector.tensor_tensor(chosen[:, rank], chosen[:, rank],
                                             share[:, s, :].unsqueeze(2).to_broadcast([P, B, E]), ALU.mult))
            step(nc.vector.tensor_tensor(per_expert[:].rearrange("p e t -> p t e"), chosen[:, 0], chosen[:, 1], ALU.add))
            with v.Fori(0, E) as e:
                for tile in range(B):
                    x = G.x[:, tile, :]
                    v.wait_ge(projected, e * B + tile + 1)
                    nc.vector.scalar_tensor_tensor(out=x, in0=G.ps[:, tile, :],
                                                   scalar=per_expert[:, e, tile:tile + 1], in1=x,
                                                   op0=ALU.mult, op1=ALU.add).then_inc(added, 1)


L0 = Attention(
    "l0", groups=8, dh=128, shared_kv=False, on_latents=False, scale=1.0, bias=True, mask="bool", rope=False,
    order="aQ0 aK0 W0 aQ1 aK1 aS0 aQ2 aS1 aE0 aN0 aK2 aE1 W1 aQ3 aK3 aS2 aN1 aT0 aE2 aN2 W2 bQ0 bK0 aS3 aT1 "
          "aE3 bQ1 bS0 aT2 aN3 aV0 W3 bK1 aT3 aV1 aA0 aV2 aA1 aV3 aO0 bQ2 aA2 bE0 bS1 bE1 bN0 aA3 bQ3 bT0 aO1 "
          "bN1 bK2 W4 bK3 bT1 W5 bS2 bS3 bE2 bE3 bN2 bN3 aO2 W6 bV0 bT2 W7 bV1 bT3 W8 aO3 bA0 W9 bV2 bA1 W10 "
          "W11 bO0 bV3 bA2 bO1 bA3 W12 W13 W14 bO2 bO3 W15")
L1 = Attention(
    "l1", groups=4, dh=96, shared_kv=True, on_latents=True, scale=float(1 / np.sqrt(np.float32(96))),
    bias=False, mask=None, rope=False,
    order="aK0 aK1 aQ0 aV0 aS0 aE0 aN0 aQ1 W0 aQ2 aS1 aT0 aE1 aN1 aQ3 aS2 aE2 aU0 aN2 aV1 aT1 aS3 bK0 W1 bK1 "
          "aE3 aT2 aN3 W2 bQ0 bQ1 W3 bS0 aU1 aT3 bE0 bQ2 bN0 aA0 bS1 bE1 aA1 aO0 bS2 aA2 aO1 aA3 bN1 bE2 bT0 "
          "bQ3 bN2 W4 W5 bV0 bS3 bT1 bE3 bU0 bV1 bN3 bT2 aO2 W6 bU1 bT3 aO3 bA0 W7 bA1 bO0 bA2 bO1 W8 W9 bA3 "
          "bO2 bO3")
L3 = Attention(
    "l3", groups=8, dh=128, shared_kv=True, on_latents=False, scale=float(1 / np.sqrt(np.float32(128))),
    bias=False, mask="float", rope=True,
    order="aK0 aHK0 aQ0 W0 aHQ0 aQ1 aHQ1 aQ2 aV0 aHQ2 aS0 aE0 aQ3 aHQ3 aS1 aU0 aN0 aS2 aE1 W1 bV0 aN1 aS3 aT0 "
          "aE2 aN2 bK0 aE3 aN3 aT1 bHK0 bQ0 W2 aT2 bHQ0 bQ1 aT3 bHQ1 bQ2 aA0 W3 bHQ2 bQ3 bS0 aA1 bS1 bE0 aO0 "
          "bHQ3 bN0 aA2 bS2 W4 bE1 aO1 bN1 aA3 bT0 W5 bS3 bE2 bN2 bT1 bE3 bN3 aO2 bT2 W6 bU0 W7 bT3 aO3 bA0 "
          "bA1 W8 bO0 bA2 bO1 bA3 bO2 bO3 W9")


PHASES = [
    lambda nc, G, d, out: attention_phase(nc, G, d, L0),
    lambda nc, G, d, out: swiglu_phase(nc, G, d),
    lambda nc, G, d, out: attention_phase(nc, G, d, L1),
    lambda nc, G, d, out: low_rank_phase(nc, G, d, "lora", 256, True),
    lambda nc, G, d, out: linear_attention_phase(nc, G, d),
    lambda nc, G, d, out: low_rank_phase(nc, G, d, "svd", 128, False),
    lambda nc, G, d, out: attention_phase(nc, G, d, L3),
    lambda nc, G, d, out: experts_phase(nc, G, d, out),
]


def build_program(nc, d, out):
    with ExitStack() as ctx:
        t = Tiles(nc, ctx, "all")
        G = Globals()
        G.x = t.sb("x", [P, B, D])
        G.ctx = t.pair("ctx", [P, C, TOK])
        G.xn = t.pair("xn", [P, C, TOK])
        G.ident = t.sb("ident", [P, P])
        G.zero = t.sb("zero", [P, 1])
        G.stats = t.sb("stats", [P, B, 6])
        G.ps = ctx.enter_context(nc.psum_tensor("ps", [P, 8, 512], F32))
        load_phase(nc, G, d)
        for phase in PHASES:
            phase(nc, G, d, out)


def laid_out(i):
    def rows(w, groups, width, parts):
        return w.reshape(groups, width, parts, -1).transpose(0, 2, 3, 1)

    def fused(w, groups, width):
        return w.reshape(groups, width, C, P).transpose(0, 3, 2, 1)

    def glu_pieces(gate, up, down):
        gu = np.concatenate([gate, up], 2).reshape(7, 2, -1, 2 * D)
        return np.concatenate([gu, np.concatenate([down[0::2], down[1::2]], 2)[:, None]], 1)

    a = {
        "x": i["x"], "ctx": i["ctx_4096"],
        "ctxT": i["ctx_4096"].reshape(TOK, C, P).transpose(1, 2, 0),
        "ident": np.eye(P, dtype=np.float32),
        "l0_mask": i["mask_BxSxS2_bk0"].view(np.int32),
        "bias": i["L0_xattn_position_bias"].reshape(8, 4, P, P).transpose(0, 2, 1, 3),
        "ln_w": i["L0_xattn_ln_weight"],
        "l0_wq": rows(i["L0_xattn_w_q"], 8, 512, C), "l0_wk": rows(i["L0_xattn_w_k"], 8, 512, C),
        "l0_wv": rows(i["L0_xattn_w_v"], 8, 512, C),
        "l0_wo": i["L0_xattn_w_out"].T.reshape(8, 4, P, D),
        "glu_w": glu_pieces(fused(i["L0_ffn_gate_q"], 14, P).reshape(14, P, D),
                            fused(i["L0_ffn_up_q"], 14, P).reshape(14, P, D),
                            i["L0_ffn_down_q"].T.reshape(14, P, D)),
        "glu_scale": glu_pieces(i["L0_ffn_gate_s"].reshape(14, P, C).transpose(0, 2, 1).reshape(14, 1, D),
                                i["L0_ffn_up_s"].reshape(14, P, C).transpose(0, 2, 1).reshape(14, 1, D),
                                i["L0_ffn_down_s"].T.reshape(14, 1, D))[:, :, 0, :],
        "l1_wq": rows(i["L1_xattn_Wq"], 4, 384, C), "l1_wk": fused(i["L1_xattn_Wk"], 4, 96),
        "l1_wv": fused(i["L1_xattn_Wv"], 4, 96), "l1_wo": i["L1_xattn_Wo"].T.reshape(4, 4, 96, D),
        "lora_w": fused(i["L1_ffn_W"], 1, D).reshape(P, C * D), "lora_bias": i["L1_ffn_bias"],
        "lora_a": fused(i["L1_ffn_A"].reshape(256, D), 1, 256).reshape(P, C * 256),
        "lora_b": i["L1_ffn_Bf"].transpose(0, 2, 1).reshape(2, P, D).transpose(1, 0, 2).reshape(P, 2 * D),
        "lora_factor0": np.repeat(i["L1_ffn_coeffs"], 16).reshape(2, P).T,
        "lora_factor1": np.repeat(i["L1_ffn_scales"], 16).reshape(2, P).T,
        "own_head": np.kron(np.eye(8), np.ones((16, 16))).astype(np.float32),
        "svd_a": i["L2_ffn_V"].reshape(C, P, P).transpose(1, 0, 2).reshape(P, C * P),
        "svd_b": i["L2_ffn_U"].T, "svd_factor0": i["L2_ffn_S"].reshape(P, 1),
        "l3_mask": i["mask_BxSxS2_ff1"],
        "l3_wq": i["L3_xattn_wq"].reshape(C, P, 8, 512).transpose(2, 0, 1, 3),
        "l3_wk": i["L3_xattn_wk"].reshape(C, P, 8, P).transpose(2, 1, 0, 3),
        "l3_wv": i["L3_xattn_wv"].reshape(C, P, 8, P).transpose(2, 1, 0, 3),
        "l3_wo": i["L3_xattn_wo"].reshape(8, 4, P, D),
        "gate_w": i["L3_ffn_gate_w"].reshape(C, P, 8).transpose(1, 0, 2),
        "experts": i["L3_ffn_expert_w"].reshape(8, C, P, D),
        "numbers": np.arange(8, dtype=np.float32),
    }
    rate = (np.float32(1.0) / np.float32(10000.0) ** (np.arange(0, P, 2, dtype=np.float32) / np.float32(P)))
    angle = np.arange(P, dtype=np.float32)[:, None] * rate[None, :].astype(np.float32)
    a["cos"] = np.concatenate([np.cos(angle), np.cos(angle)], 1).T
    a["sin"] = np.concatenate([np.sin(angle), -np.sin(angle)], 1).T
    return {k: np.ascontiguousarray(v) for k, v in a.items()}


def kernel(**inputs):
    import concourse.bacc as bacc
    from concourse.bass_utils import run_bass_kernel_spmd

    nc = bacc.Bacc("TRN2", target_bir_lowering=False, num_devices=1)
    arrays = laid_out({k: np.asarray(v) for k, v in inputs.items()})
    d = {k: nc.dram_tensor("in_" + k, v.shape, mybir.dt.from_np(v.dtype), kind="ExternalInput").ap()
         for k, v in arrays.items()}
    out = nc.dram_tensor("out", (B, P, D), F32, kind="ExternalOutput").ap()
    build_program(nc, d, out)
    got = run_bass_kernel_spmd(nc, [{"in_" + k: v for k, v in arrays.items()}], core_ids=[0])
    return got.results[0]["out"]
```
